# Optimizing a Trainium2 kernel written in Bass

```python
import numpy as np
import jax
import jax.numpy as jnp

def _softmax(x, axis=-1):
    return jax.nn.softmax(x, axis=axis)

def _gelu(x):
    return jax.nn.gelu(x, approximate=True)

def _silu(x):
    return jax.nn.silu(x)

def _sigmoid(x):
    return jax.nn.sigmoid(x)

def _layernorm(x, axis=-1, eps=1e-05):
    m = jnp.mean(x, axis=axis, keepdims=True)
    v = jnp.var(x, axis=axis, keepdims=True)
    return (x - m) / jnp.sqrt(v + eps)

def _scatter_add(tgt, idx, src, axis=0):
    return tgt.at[idx].add(src)

def _segment_sum(src, seg, n):
    return jax.ops.segment_sum(src, seg, n)
kernel_name = 'mk_sandwich_d1_jaxref_r4_0c3b91'

def setup_inputs(seed: int=0):
    np.random.seed(seed)
    _w = jnp.asarray

    def _L0_attn_setup():
        import jax, jax.numpy as jnp
        import numpy as np
        D_MODEL = 256
        H = 16
        DH = D_MODEL // H
        WIN = 7
        PAD = WIN // 2
        B, L = (2, 1024)
        key = jax.random.key(seed)
        ks = jax.random.split(key, 12)
        s = lambda k, shape: jax.random.normal(k, shape, dtype=jnp.float32) * 0.02
        return {'x': jax.random.normal(ks[0], (B, L, D_MODEL), dtype=jnp.float32), 'wq': s(ks[1], (D_MODEL, D_MODEL)), 'wk': s(ks[2], (D_MODEL, D_MODEL)), 'wv': s(ks[3], (D_MODEL, D_MODEL)), 'wo': s(ks[4], (D_MODEL, D_MODEL)), 'bo': s(ks[5], (D_MODEL,)), 'cw1': s(ks[6], (H, 32, 1)), 'cb1': s(ks[7], (H, 32)), 'cw2': s(ks[8], (H, 32, 32)), 'cb2': s(ks[9], (H, 32)), 'cw3': s(ks[10], (H, 1, 32)), 'cb3': s(ks[11], (H, 1))}
    _L0_attn_in = _L0_attn_setup()

    def _L0_ffn_setup():
        import jax, jax.numpy as jnp
        import numpy as np
        B, T, D, H, E = (4, 512, 256, 512, 8)
        TOP_K = int(E * 0.25)
        key = jax.random.key(seed)
        ks = jax.random.split(key, 6)
        x = jax.random.normal(ks[0], (B, T, D), dtype=jnp.float32)
        gate = jax.random.normal(ks[1], (D, E), dtype=jnp.float32)
        W1 = jax.random.normal(ks[2], (E, D, H), dtype=jnp.float32) * D ** (-0.5)
        b1 = jnp.zeros((E, H), dtype=jnp.float32)
        W2 = jax.random.normal(ks[3], (E, H, D), dtype=jnp.float32) * H ** (-0.5)
        b2 = jnp.zeros((E, D), dtype=jnp.float32)
        return {'x': x, 'gate': gate, 'W1': W1, 'b1': b1, 'W2': W2, 'b2': b2}
    _L0_ffn_in = _L0_ffn_setup()
    _d = {'L0_attn_x': _L0_attn_in['x'], 'L0_attn_wq': _L0_attn_in['wq'], 'L0_attn_wk': _L0_attn_in['wk'], 'L0_attn_wv': _L0_attn_in['wv'], 'L0_attn_wo': _L0_attn_in['wo'], 'L0_attn_bo': _L0_attn_in['bo'], 'L0_attn_cw1': _L0_attn_in['cw1'], 'L0_attn_cb1': _L0_attn_in['cb1'], 'L0_attn_cw2': _L0_attn_in['cw2'], 'L0_attn_cb2': _L0_attn_in['cb2'], 'L0_attn_cw3': _L0_attn_in['cw3'], 'L0_attn_cb3': _L0_attn_in['cb3'], 'L0_ffn_gate': _L0_ffn_in['gate'], 'L0_ffn_W1': _L0_ffn_in['W1'], 'L0_ffn_b1': _L0_ffn_in['b1'], 'L0_ffn_W2': _L0_ffn_in['W2'], 'L0_ffn_b2': _L0_ffn_in['b2']}
    _x0 = _d['L0_attn_x']
    _d['L0_attn_x'] = jax.random.normal(jax.random.fold_in(jax.random.key(seed), 1), (4, 1024, 256), dtype=_x0.dtype)
    del _x0
    return _d

def reference(L0_attn_x, L0_attn_wq, L0_attn_wk, L0_attn_wv, L0_attn_wo, L0_attn_bo, L0_attn_cw1, L0_attn_cb1, L0_attn_cw2, L0_attn_cb2, L0_attn_cw3, L0_attn_cb3, L0_ffn_gate, L0_ffn_W1, L0_ffn_b1, L0_ffn_W2, L0_ffn_b2):

    def _L0_attn_ref(x, wq, wk, wv, wo, bo, cw1, cb1, cw2, cb2, cw3, cb3):
        import jax, jax.numpy as jnp
        import numpy as np
        D_MODEL = 256
        H = 16
        DH = D_MODEL // H
        WIN = 7
        PAD = WIN // 2
        B, L = (2, 1024)
        b, l, d = x.shape

        def heads(w):
            return (x @ w.T).reshape(b, l, H, DH).transpose(0, 2, 1, 3)
        Q, K, V = (heads(wq), heads(wk), heads(wv))
        Kp = jnp.pad(K, ((0, 0), (0, 0), (PAD, PAD), (0, 0)))
        Vp = jnp.pad(V, ((0, 0), (0, 0), (PAD, PAD), (0, 0)))
        idx = jnp.arange(l)[:, None] + jnp.arange(WIN)[None, :]
        Kw = Kp[:, :, idx]
        Vw = Vp[:, :, idx]
        scores = jnp.einsum('bhld,bhlwd->bhlw', Q, Kw) / np.float32(np.sqrt(DH))
        attn = jax.nn.softmax(scores, axis=-1)
        pos = jnp.linspace(0.0, 1.0, WIN, dtype=jnp.float32)[:, None]
        gelu = lambda z: jax.nn.gelu(z, approximate=False)
        h = gelu(jnp.einsum('wi,hji->hwj', pos, cw1) + cb1[:, None, :])
        h = gelu(jnp.einsum('hwi,hji->hwj', h, cw2) + cb2[:, None, :])
        cwt = (jnp.einsum('hwi,hji->hwj', h, cw3) + cb3[:, None, :])[..., 0]
        conn = jax.nn.softmax(cwt, axis=-1)[None, :, None, :]
        fw = attn * conn
        fw = fw / (fw.sum(axis=-1, keepdims=True) + 1e-09)
        out = jnp.einsum('bhlw,bhlwd->bhld', fw, Vw)
        out = out.transpose(0, 2, 1, 3).reshape(b, l, d)
        return out @ wo.T + bo

    def _L0_ffn_ref(x, gate, W1, b1, W2, b2):
        import jax, jax.numpy as jnp
        import numpy as np
        B, T, D, H, E = (4, 512, 256, 512, 8)
        TOP_K = int(E * 0.25)
        raw_gate = jax.nn.softmax(jnp.einsum('btd,de->bte', x, gate), axis=-1)
        topk_scores, topk_idx = jax.lax.top_k(raw_gate, TOP_K)
        mask = jax.nn.one_hot(topk_idx, E, dtype=raw_gate.dtype).sum(axis=-2)
        gate_topk = mask * raw_gate
        gate_topk = gate_topk / jnp.maximum(gate_topk.sum(axis=-1, keepdims=True), 1e-12)
        h = jax.nn.relu(jnp.einsum('btd,edh->beth', x, W1) + b1[None, :, None, :])
        expert_out = jnp.einsum('beth,ehd->betd', h, W2) + b2[None, :, None, :]
        out = jnp.einsum('bte,betd->btd', gate_topk, expert_out)
        return out
    x = L0_attn_x
    x = x + _layernorm(_L0_attn_ref(_layernorm(x, axis=-1), L0_attn_wq, L0_attn_wk, L0_attn_wv, L0_attn_wo, L0_attn_bo, L0_attn_cw1, L0_attn_cb1, L0_attn_cw2, L0_attn_cb2, L0_attn_cw3, L0_attn_cb3), axis=-1)
    x = x + _layernorm(_L0_ffn_ref(_layernorm(x, axis=-1), L0_ffn_gate, L0_ffn_W1, L0_ffn_b1, L0_ffn_W2, L0_ffn_b2), axis=-1)
    return x

_drawn_inputs = setup_inputs


def setup_inputs(seed=0):
    import zlib

    import numpy as np

    out = dict(_drawn_inputs(seed))
    spreads = {'L0_ffn_b1': (0.0, 0.1), 'L0_ffn_b2': (0.0, 0.1)}
    factors = {'L0_attn_cw1': 26.175,
     'L0_attn_cb1': 64.0,
     'L0_attn_cw2': 21.86,
     'L0_attn_cb2': 53.43,
     'L0_attn_cw3': 23.31,
     'L0_attn_cb3': 8.0}
    for name, (base, spread) in spreads.items():
        noise = np.random.default_rng([zlib.crc32(name.encode()), seed]).standard_normal(out[name].shape)
        drawn = base * np.exp(spread * noise) if base else spread * noise
        out[name] = jnp.asarray(drawn.astype(out[name].dtype))
    for name, factor in factors.items():
        out[name] = (out[name] * factor).astype(out[name].dtype)
    return out
```

```python
from contextlib import ExitStack

import concourse.bass as bass
from concourse import mybir

F32 = mybir.dt.float32
F32R = mybir.dt.float32r
BF16 = mybir.dt.bfloat16
I32 = mybir.dt.int32
ALU = mybir.AluOpType
ACT = mybir.ActivationFunctionType
AX = mybir.AxisListType

P = 128
ds = bass.ds


def even_up(n):
    return n + n % 2


def need(eng, sem, count):
    if isinstance(count, int) and count <= 0:
        return
    eng.wait_ge(sem, count)


def run_steps(eng, n, stages):
    most = max(lag for lag, _ in stages)

    def step(t, odd, edge):
        for lag, stage in stages:
            if not edge or 0 <= t - lag < n:
                stage(t - lag, (odd - lag) % 2)

    start = even_up(most + 2)
    turns = (n - start) // 2
    for t in range(start):
        step(t, t % 2, True)
    with eng.Fori(0, turns) as i:
        for odd in range(2):
            step(2 * i + (start + odd), odd, False)
    for t in range(start + 2 * turns, n + most):
        step(t, t % 2, True)


def build(nc, x, wqkvT, woT, bo, cw1, cb1, cw2, cb2, cw3, cb3, gate, w1, b1, w2, b2, consts, out):
    B, L, D = x.shape
    N = B * L
    NT = N // P
    H = cw1.shape[0]
    DH = D // H
    J = cw1.shape[1]
    WIN = 7
    PAD = WIN // 2
    WH = WIN * H
    KC = D // P
    E, _, F = w1.shape
    FC = F // P
    TOPK = E // 4
    ROOM = N + P
    TILES = N * TOPK // P + E - 1
    SPARE = (E - 1) * P
    EW = KC * F
    assert EW == FC * D and N == P * NT and L % NT == 0
    SEQP = L // NT
    LN_EPS = 1e-5
    scale = float(DH) ** -0.5

    rows_in = nc.dram_tensor("rows_in", [E * ROOM + SPARE, D], F32, kind="Internal").ap()
    rows_out = nc.dram_tensor("rows_out", [TILES * P, D], F32, kind="Internal").ap()

    with ExitStack() as top:
        def sem(name):
            return top.enter_context(nc.semaphore(name))

        def sb(ctx, name, shape, dt=F32):
            return ctx.enter_context(nc.sbuf_tensor(name, shape, dt))

        def psum(ctx, name, shape, dt=F32):
            return ctx.enter_context(nc.psum_tensor(name, shape, dt))

        xs = sb(top, "xs", [P, NT * D])
        con = sb(top, "con", [P, 3 * P + 8 + E])
        ident = con[:, 0:P]
        halves = con[:, 3 * P:3 * P + 1]
        rowsel = con[0:2, 3 * P + 1:3 * P + 2]
        posn = con[:, 3 * P + 2:3 * P + 3]
        gates = sb(top, "gates", [P, NT, 2])
        slots = sb(top, "slots", [P, 2, NT], I32)
        backs = sb(top, "backs", [P, 2, NT], I32)
        jobs = sb(top, "jobs", [1, 2, TILES + 1], I32)
        tails = sb(top, "tails", [1, E], I32)
        st1 = sb(top, "st1", [P, 2, 6])
        mv1 = sb(top, "mv1", [P, 2, 2])
        ve1 = sb(top, "ve1", [P, 2, 1])
        rs1 = sb(top, "rs1", [P, 2, 1])
        zeros = sb(top, "zeros", [P, D])

        s_const = sem("const_loaded")
        s_small = sem("small_loaded")

        def apart(eng, *waits):
            waits = [(s, n if isinstance(n, int) else eng.to_reg(n)) for s, n in waits]
            eng.wait_ge(s_const, 16)
            for s, n in waits:
                need(eng, s, n)
        s_x = sem("x_loaded")
        s_w = sem("attn_weights_loaded")


        ctx = ExitStack()
        K = sb(ctx, "K", [P, (NT + 2 * PAD) * D])
        V = sb(ctx, "V", [P, (NT + 2 * PAD) * D])
        Q = sb(ctx, "Q", [P, NT * D])
        prod = sb(ctx, "prod", [P, WIN * D])
        wval = sb(ctx, "wval", [P, WIN * D])
        wqkv = sb(ctx, "wqkv", [P, KC, 3 * D])
        wo = sb(ctx, "wo", [P, KC, D])
        bor = sb(ctx, "bor", [1, D])
        ones1 = sb(ctx, "ones1", [1, P])
        gatew = sb(ctx, "gatew", [P, KC, E])
        st0 = sb(ctx, "st0", [P, NT, 6])
        ln0 = sb(ctx, "ln0", [P, 6, NT])
        xn = sb(ctx, "xn", [P, 2, D])
        xnT = sb(ctx, "xnT", [P, 2, KC, P])
        conn = sb(ctx, "conn", [P, WH])
        sc = sb(ctx, "sc", [P, 2, 3, WH])
        sm = sb(ctx, "sm", [P, 2, 5, H])
        fw = sb(ctx, "fw", [P, 2, WH])
        att = sb(ctx, "att", [P, 2, D])
        attT = sb(ctx, "attT", [P, 2, KC, P])
        xm = sb(ctx, "xm", [P, 2, D])
        st2 = sb(ctx, "st2", [P, 2, 6])
        mv2 = sb(ctx, "mv2", [P, 2, 2])
        ve2 = sb(ctx, "ve2", [P, 2, 1])
        rs2 = sb(ctx, "rs2", [P, 2, 1])
        nm1 = sb(ctx, "nm1", [P, 2, 1])
        nm2 = sb(ctx, "nm2", [P, 2, 1])
        logit = sb(ctx, "logit", [P, NT, E])
        cn = sb(ctx, "cn", [WH, 6, J])
        cnw2 = sb(ctx, "cnw2", [WH, J, J])
        cnc = sb(ctx, "cnc", [WH, 4])
        crow = sb(ctx, "crow", [1, 3, WH])
        csum = sb(ctx, "csum", [1, 4, H])

        psa = ExitStack()
        psT = [psum(psa, f"psT{n}", [P, 512]) for n in range(2)]
        psA = [psum(psa, f"psA{n}", [P, 512]) for n in range(2)]
        psB = [psum(psa, f"psB{n}", [P, 512]) for n in range(2)]
        psC = [psum(psa, f"psC{n}", [P, 512]) for n in range(2)]

        s_zero = sem("zeros_set")
        s_stat0 = sem("ln1_stats")
        s_mom0 = sem("ln1_moments")
        s_rstd0 = sem("ln1_rstd")
        s_xn = sem("xn_ready")
        s_xTp = sem("xn_transposed")
        s_xT = sem("xnT_ready")
        s_qkv = sem("qkv_done")
        s_qkvs = sem("qkv_stored")
        s_halo0 = sem("halo_zeroed")
        s_halo = sem("halo_shifted")
        s_cn = sem("connectivity_step")
        s_cna = sem("connectivity_gelu")
        s_cnp = sem("connectivity_pe")
        s_prod = sem("products_ready")
        s_raw = sem("raw_scores_ready")
        s_max = sem("score_max_ready")
        s_sc = sem("scores_ready")
        s_exp = sem("exp_done")
        s_wt = sem("weighted_ready")
        s_z = sem("exp_sum_ready")
        s_s1 = sem("weighted_sum_ready")
        s_den = sem("denominator_ready")
        s_rden = sem("reciprocal_ready")
        s_fw = sem("weights_ready")
        s_wv = sem("weighted_values_ready")
        s_att = sem("attn_ready")
        s_aTp = sem("attn_transposed")
        s_aT = sem("attnT_ready")
        s_wo = sem("out_product_done")
        s_st1 = sem("ln2_stats")
        s_mv1 = sem("ln2_moments")
        s_ve1 = sem("ln2_var_eps")
        s_rs1 = sem("ln2_rstd")
        s_nm1 = sem("ln2_shift")
        s_xm = sem("x_shifted")
        s_x1 = sem("x1_ready")
        s_st2 = sem("ln3_stats")
        s_mv2 = sem("ln3_moments")
        s_ve2 = sem("ln3_var_eps")
        s_rs2 = sem("ln3_rstd")
        s_nm2 = sem("ln3_shift")
        s_xn2 = sem("xn2_ready")
        s_x2p = sem("xn2_transposed")
        s_x2T = sem("xn2T_ready")
        s_lg = sem("logits_done")
        s_lgs = sem("logits_stored")
        s_keep = sem("xn2_kept")

        g = {n: sb(ctx, f"g_{n}", [P, NT, E]) for n in ("p", "q", "oh1", "oh2")}
        gs = sb(ctx, "gs", [P, 6, NT])
        gm = sb(ctx, "gm", [P, NT + 1, E], BF16)
        tri = sb(ctx, "tri", [P, P], BF16)
        onesb = sb(ctx, "onesb", [P, P], BF16)
        gpos = sb(ctx, "gpos", [P, NT + 1, E])
        cnt = sb(ctx, "cnt", [P, 6, E])
        cnti = sb(ctx, "cnti", [P, E], I32)
        jcmp = sb(ctx, "jcmp", [1, TILES, E])
        jcm2 = sb(ctx, "jcm2", [1, TILES, E])
        jf = sb(ctx, "jf", [1, 3, TILES])
        prior = con[:, P * 2:P * 2 + E]
        ebase = con[:, P * 2 + E:P * 2 + 2 * E]
        s_g = sem("gate_step")
        s_gexp = sem("gate_exp")
        s_gcast = sem("gate_masks_cast")
        s_gpos = sem("positions_done")
        s_gposs = sem("positions_stored")
        s_slots = sem("slots_ready")
        s_jobs = sem("jobs_ready")
        s_spare = sem("spare_zeroed")
        s_tail = sem("tails_zeroed")
        s_scat = sem("rows_scattered")
        jota = sb(ctx, "jota", [1, TILES])
        s_jota = sem("tile_numbers")

        s_wraw = [sem(f"expert_weights_loaded{n}") for n in range(2)]
        s_whi = sem("weights_high")
        s_wlo = sem("weights_low")
        s_bias = sem("bias_step")
        s_braw = sem("biases_loaded")
        s_xg = [sem(f"tile_rows_loaded{n}") for n in range(2)]
        s_xgp = sem("tile_transposed")
        s_xgh = sem("tile_high")
        s_xgl = sem("tile_low")
        s_h = sem("hidden_done")
        s_hr = sem("hidden_relu")
        s_hTp = sem("hidden_transposed")
        s_hTh = sem("hiddenT_high")
        s_hTl = sem("hiddenT_low")
        s_y = sem("tile_out_done")
        s_ys = sem("tile_out_copied")
        s_yst = [sem(f"tile_out_stored{n}") for n in range(2)]
        s_gat = [sem(f"rows_gathered{n}") for n in range(2)]
        s_o1 = sem("first_weighted")
        s_o2 = sem("moe_ready")
        s_st3 = sem("ln4_stats")
        s_mv3 = sem("ln4_moments")
        s_ve3 = sem("ln4_var_eps")
        s_rs3 = sem("ln4_rstd")
        s_nrm = sem("ln4_normed")
        s_fin = sem("final_ready")
        s_out = [sem(f"out_stored{n}") for n in range(2)]

        ctx.close()
        w1h = sb(top, "w1h", [P, E * EW], F32R)
        w1l = sb(top, "w1l", [P, E * EW], F32R)
        w2h = sb(top, "w2h", [P, E * EW], F32R)
        w2l = sb(top, "w2l", [P, E * EW], F32R)
        bias = sb(top, "bias", [P, F + D], BF16)
        sel = sb(top, "sel", [P, E * P], BF16)
        late = ExitStack()
        wraw = sb(late, "wraw", [P, 2, EW])
        braw = sb(late, "braw", [3 * E, 3, F + D])
        late.close()
        xg = sb(top, "xg", [P, 2, D])
        xgh = sb(top, "xgh", [P, 2, KC, P], F32R)
        xgl = sb(top, "xgl", [P, 2, KC, P], F32R)
        hr = sb(top, "hr", [P, 2, F])
        hTh = sb(top, "hTh", [P, 2, FC, P], F32R)
        hTl = sb(top, "hTl", [P, 2, FC, P], F32R)
        ysb = sb(top, "ysb", [P, 2, D])
        gidx = sb(top, "gidx", [P, 2, 2], I32)
        yg = sb(top, "yg", [P, 2, 2, D])
        moe = sb(top, "moe", [P, 2, D])
        fin = sb(top, "fin", [P, 2, D])
        s_pick = sem("indices_picked")

        xv = x.rearrange("b (q t) d -> (b q) (t d)", t=NT)
        ov = out.rearrange("b (q t) d -> (b q) (t d)", t=NT)


        w1v = w1.rearrange("e (c p) f -> p e c f", p=P)
        w2v = w2.rearrange("e (c p) d -> p e c d", p=P)
        parts = ((w1v, w1h, w1l), (w2v, w2h, w2l))

        def experts(eng, body):
            for part in range(2):
                body(0, part)
            with eng.Fori(1, E) as e:
                for part in range(2):
                    body(e, part)

        def stage4_sp(sp):
            sp.wait_ge(s_scat, 16 * 2 * NT)
            for n in range(3):
                r = slice(n * E, (n + 1) * E)
                sp.dma_start(braw[r, 0, 0:F], b1).then_inc(s_braw, 16)
                sp.dma_start(braw[r, 0, F:F + D], b2).then_inc(s_braw, 16)

            def load_w(e, part):
                need(sp, s_wlo, 2 * e + part - 1)
                src = parts[part][0]
                sp.dma_start(wraw[:, part, :].rearrange("p (e c f) -> p e c f", e=1, c=src.shape[2]),
                             src[:, ds(e, 1)]).then_inc(s_wraw[part], 16)

            experts(sp, load_w)
            sp.wait_ge(s_spare, 16 * (E - 1))
            sp.wait_ge(s_tail, 16 * E)
            sp.wait_ge(s_wlo, 2 * E)
            sp.wait_ge(s_bias, 7)

            def load_rows(j, k):
                need(sp, s_xgp, j - 1)
                first = sp.value_load(jobs[0:1, 1, ds(j, 1)], min_val=0,
                                      max_val=E * ROOM + SPARE - P)
                sp.dma_start(xg[:, k, :], rows_in[ds(first, P), :]).then_inc(s_xg[k], 16)

            def store_rows(j, k):
                sp.wait_ge(s_ys, j + 1)
                sp.dma_start(rows_out[ds(j * P, P), :], ysb[:, k, :]).then_inc(s_yst[k], 16)

            run_steps(sp, TILES, [(0, load_rows), (3, store_rows)])

            def store_out(t, k):
                sp.wait_ge(s_fin, t + 1)
                sp.dma_start(ov[:, ds(t * D, D)], fin[:, k, :]).then_inc(s_out[k], 16)

            run_steps(sp, NT, [(0, store_out)])
            for k in range(2):
                sp.wait_ge(s_out[k], 16 * NT // 2)

        def stage4_act(act):
            def high(e, part):
                act.wait_ge(s_wraw[part], 16 * e + 16)
                nc.scalar.copy(parts[part][1][:, ds(e * EW, EW)], wraw[:, part, :]).then_inc(s_whi, 1)

            experts(act, high)

            def rows_high(j, k):
                act.wait_ge(s_xgp, j + 1)
                need(act, s_h, j - 1)
                nc.scalar.copy(xgh[:, k, :, :], psT[k][:, 0:D].rearrange("p (c m) -> p c m", c=KC)) \
                  .then_inc(s_xgh, 1)

            def hidden_high(j, k):
                act.wait_ge(s_hTp, j + 1)
                need(act, s_y, j - 1)
                nc.scalar.copy(hTh[:, k, :, :], psB[k][:, :].rearrange("p (c m) -> p c m", c=FC)) \
                  .then_inc(s_hTh, 1)

            def relu(j, k):
                act.wait_ge(s_h, j + 1)
                need(act, s_hTp, j - 1)
                nc.scalar.activation(hr[:, k, :], psA[k][:, 0:F], ACT.Relu).then_inc(s_hr, 1)

            run_steps(act, TILES, [(0, rows_high), (2, hidden_high), (1, relu)])

        def stage4_dve(v):
            v.wait_ge(s_scat, 16 * 2 * NT)
            nc.vector.memset(bias[:, :], 0.0).then_inc(s_bias, 1)
            nc.vector.tensor_copy(sel[:, :], con[:, 3 * P + 8:3 * P + 8 + E].rearrange(
                "p (e o) -> p e o", o=1).to_broadcast([P, E, P])).then_inc(s_bias, 1)
            v.wait_ge(s_braw, 16 * 6)
            G = 3 * E
            raw, hi, mid = (braw[:, n, :] for n in range(3))
            less = lambda n: con[0:G, 3 * P + 3 + n:3 * P + 4 + n]
            v.wait_ge(s_bias, 2)
            nc.vector.tensor_copy(bias[0:G, :], raw).then_inc(s_bias, 1)
            v.wait_ge(s_bias, 3)
            nc.vector.scalar_tensor_tensor(hi, bias[0:G, :], less(0), raw, ALU.mult,
                                           ALU.add).then_inc(s_bias, 1)
            v.wait_ge(s_bias, 4)
            nc.vector.tensor_copy(bias[0:G, :], hi).then_inc(s_bias, 1)
            v.wait_ge(s_bias, 5)
            nc.vector.scalar_tensor_tensor(mid, bias[0:G, :], less(1), hi, ALU.mult,
                                           ALU.add).then_inc(s_bias, 1)
            v.wait_ge(s_bias, 6)
            nc.vector.tensor_copy(bias[0:G, :], mid).then_inc(s_bias, 1)

            def low(e, part):
                v.wait_ge(s_whi, 2 * e + part + 1)
                _, whi, wlo = parts[part]
                nc.vector.tensor_tensor(wlo[:, ds(e * EW, EW)], wraw[:, part, :],
                                        whi[:, ds(e * EW, EW)].bitcast(F32),
                                        ALU.subtract).then_inc(s_wlo, 1)

            experts(v, low)

            def rows_low(j, k):
                v.wait_ge(s_xgh, j + 1)
                nc.vector.tensor_tensor(xgl[:, k, :, :].rearrange("p c m -> p (c m)"), psT[k][:, 0:D],
                                        xgh[:, k, :, :].bitcast(F32).rearrange("p c m -> p (c m)"),
                                        ALU.subtract).then_inc(s_xgl, 1)

            def hidden_low(j, k):
                v.wait_ge(s_hTh, j + 1)
                nc.vector.tensor_tensor(hTl[:, k, :, :].rearrange("p c m -> p (c m)"), psB[k][:, :],
                                        hTh[:, k, :, :].bitcast(F32).rearrange("p c m -> p (c m)"),
                                        ALU.subtract).then_inc(s_hTl, 1)

            def copy_out(j, k):
                v.wait_ge(s_y, j + 1)
                need(v, s_yst[k], 8 * (j - k))
                nc.vector.tensor_copy(ysb[:, k, :], psC[k][:, 0:D]).then_inc(s_ys, 1)

            run_steps(v, TILES, [(0, rows_low), (2, hidden_low), (3, copy_out)])

            def pick(t, k):
                need(v, s_gat[k], 16 * (t - k))
                nc.vector.tensor_copy(gidx[:, k, :].rearrange("p (n o) -> p n o", o=1),
                                      backs[:, :, ds(t, 1)]).then_inc(s_pick, 1)

            def combine(t, k):
                v.wait_ge(s_gat[k], 16 * (t - k) + 32)
                need(v, s_fin, t - 1)
                nc.vector.tensor_scalar(moe[:, k, :], yg[:, k, 0, :], gates[:, ds(t, 1), 0], None,
                                        ALU.mult).then_inc(s_o1, 1)
                v.wait_ge(s_o1, t + 1)
                nc.vector.scalar_tensor_tensor(moe[:, k, :], yg[:, k, 1, :], gates[:, ds(t, 1), 1],
                                               moe[:, k, :], ALU.mult, ALU.add).then_inc(s_o2, 1)
                v.wait_ge(s_o2, t + 1)
                nc.vector.bn_stats(st1[:, k, :], moe[:, k, :]).then_inc(s_st3, 1)
                apart(v, (s_st3, t + 1))
                nc.vector.bn_aggr(mv1[:, k, :], st1[:, k, :]).then_inc(s_mv3, 1)

            def finish(t, k):
                v.wait_ge(s_rs3, t + 1)
                nc.vector.tensor_scalar(moe[:, k, :], moe[:, k, :], mv1[:, k, 0:1], rs1[:, k, :],
                                        ALU.subtract, ALU.mult).then_inc(s_nrm, 1)
                v.wait_ge(s_nrm, t + 1)
                need(v, s_out[k], 8 * (t - k))
                nc.vector.tensor_tensor(fin[:, k, :], moe[:, k, :], xs[:, ds(t * D, D)],
                                        ALU.add).then_inc(s_fin, 1)

            run_steps(v, NT, [(0, pick), (1, combine), (2, finish)])

        def stage5_pool(pool):
            for k in range(2):
                pool.wait_ge(s_yst[k], 16 * ((TILES + 1 - k) // 2))

            def gather(t, k):
                apart(pool, (s_o2, t - 1),
                      (s_pick, t + 1))
                for n in range(2):
                    nc.gpsimd.indirect_dma_start(
                        yg[:, k, n, :], None, rows_out,
                        bass.IndirectOffsetOnAxis(ap=gidx[:, k, n:n + 1], axis=0)).then_inc(s_gat[k], 16)

            def rstd4(t, k):
                apart(pool, (s_nrm, t - 1),
                      (s_mv3, t + 1))
                nc.gpsimd.tensor_scalar(ve1[:, k, :], mv1[:, k, 1:2], LN_EPS, None,
                                        ALU.add).then_inc(s_ve3, 1)
                pool.wait_ge(s_ve3, t + 1)
                nc.gpsimd.tensor_tensor(rs1[:, k, :], ve1[:, k, :], halves, ALU.pow).then_inc(s_rs3, 1)

            run_steps(pool, NT, [(0, gather), (1, rstd4)])

        def stage4_pe(pe):
            pe.wait_ge(s_gpos, 1)
            pe.wait_ge(s_gposs, 1)
            pe.wait_ge(s_wlo, 2 * E)
            pe.wait_ge(s_bias, 7)

            def turn_rows(j, k):
                pe.wait_ge(s_xg[k], 8 * (j - k) + 16)
                need(pe, s_xgl, j - 1)
                transposes(pe, xg[:, k, :], psT[k], KC).then_inc(s_xgp, 1)

            def product(pe, bank, j, xh, xl, wh, wl, chunks, n, bias_at):
                e = pe.value_load(jobs[0:1, 0, ds(j, 1)], min_val=0, max_val=E - 1)
                nc.tensor.matmul(bank, sel[:, ds(e * P, P)], bias[:, bias_at:bias_at + n],
                                 start=True, stop=False)
                for c in range(chunks):
                    w = ds(e * EW + c * n, n)
                    nc.tensor.matmul(bank, xl[:, c, :], wh[:, w], start=False, stop=False)
                    nc.tensor.matmul(bank, xh[:, c, :], wl[:, w], start=False, stop=False)
                    mm = nc.tensor.matmul(bank, xh[:, c, :], wh[:, w], start=False,
                                          stop=(c == chunks - 1))
                return mm

            def hidden(j, k):
                apart(pe, (s_hr, j - 1),
                      (s_xgl, j + 1))
                product(pe, psA[k][:, 0:F], j, xgh[:, k], xgl[:, k], w1h, w1l, KC, F, 0) \
                    .then_inc(s_h, 1)

            def turn_hidden(j, k):
                pe.wait_ge(s_hr, j + 1)
                need(pe, s_hTl, j - 1)
                transposes(pe, hr[:, k, :], psB[k], FC).then_inc(s_hTp, 1)

            def outp(j, k):
                apart(pe, (s_ys, j - 1),
                      (s_hTl, j + 1))
                product(pe, psC[k][:, 0:D], j, hTh[:, k], hTl[:, k], w2h, w2l, FC, D, F) \
                    .then_inc(s_y, 1)

            run_steps(pe, TILES, [(0, turn_rows), (2, turn_hidden), (1, hidden), (2, outp)])

        def transposes(pe, src, dst, chunks):
            for c in range(chunks):
                mm = nc.tensor.transpose(dst[:, c * P:(c + 1) * P], src[:, c * P:(c + 1) * P], ident)
            return mm

        block = top.enter_context(nc.Block())

        @block.sync
        def _(sp):
            sp.dma_start(con[:, :], consts).then_inc(s_const, 16)
            for n in range(4):
                m = NT * D // 4
                sp.dma_start(xs[:, n * m:(n + 1) * m], xv[:, n * m:(n + 1) * m]).then_inc(s_x, 16)
            sp.dma_start(wqkv[:, :, :], wqkvT.rearrange("(c p) n -> p c n", p=P)).then_inc(s_w, 16)
            sp.dma_start(wo[:, :, :], woT.rearrange("(c p) n -> p c n", p=P)).then_inc(s_w, 16)
            sp.dma_start(gatew[:, :, :], gate.rearrange("(c p) n -> p c n", p=P)).then_inc(s_w, 16)
            sp.dma_start(bor[:, :], bo.rearrange("(a d) -> a d", a=1)).then_inc(s_w, 16)
            for w in range(WIN):
                r = slice(w * H, (w + 1) * H)
                sp.dma_start(cn[r, 0, :], cw1.rearrange("h j a -> h (j a)")).then_inc(s_small, 16)
                sp.dma_start(cn[r, 1, :], cb1).then_inc(s_small, 16)
                sp.dma_start(cnw2[r, :, :], cw2).then_inc(s_small, 16)
                sp.dma_start(cn[r, 2, :], cb2).then_inc(s_small, 16)
                sp.dma_start(cn[r, 3, :], cw3.rearrange("h a j -> h (a j)")).then_inc(s_small, 16)
                sp.dma_start(cnc[r, 0:1], cb3).then_inc(s_small, 16)
            sp.wait_ge(s_qkvs, NT)
            sp.wait_ge(s_halo0, 4)
            for T in (K, V):
                for b in range(B):
                    lo, hi = b * SEQP, (b + 1) * SEQP
                    sp.dma_start(T[lo + 1:hi, 0:PAD * D],
                                 T[lo:hi - 1, NT * D:(NT + PAD) * D]).then_inc(s_halo, 16)
                    sp.dma_start(T[lo:hi - 1, (NT + PAD) * D:(NT + 2 * PAD) * D],
                                 T[lo + 1:hi, PAD * D:2 * PAD * D]).then_inc(s_halo, 16)
            sp.wait_ge(s_zero, 1)
            for n in range(E - 1):
                sp.dma_start(rows_in[E * ROOM + n * P:E * ROOM + (n + 1) * P, :],
                             zeros[:, :]).then_inc(s_spare, 16)
            sp.wait_ge(s_jobs, 1)
            for e in range(E):
                first = sp.value_load(tails[0:1, e:e + 1], min_val=0, max_val=E * ROOM - P)
                sp.dma_start(rows_in[ds(first, P), :], zeros[:, :]).then_inc(s_tail, 16)
            stage4_sp(sp)

        @block.gpsimd
        def _(pool):
            nc.gpsimd.iota(jota[0:1, :], [[1, TILES]], base=0, channel_multiplier=0,
                           allow_small_or_imprecise_dtypes=True).then_inc(s_jota, 1)
            pool.wait_ge(s_const, 16)
            pool.wait_ge(s_mom0, 6)
            nc.gpsimd.tensor_tensor(ln0[:, 5, :], ln0[:, 4, :], halves.to_broadcast([P, NT]),
                                    ALU.pow).then_inc(s_rstd0, 1)

            def rstd2(t, k):
                apart(pool, (s_xm, t - 1),
                      (s_x1, t - 1),
                      (s_mv1, t + 1))
                nc.gpsimd.tensor_scalar(ve1[:, k, :], mv1[:, k, 1:2], LN_EPS, None,
                                        ALU.add).then_inc(s_ve1, 1)
                pool.wait_ge(s_ve1, t + 1)
                nc.gpsimd.tensor_tensor(rs1[:, k, :], ve1[:, k, :], halves, ALU.pow).then_inc(s_rs1, 1)
                apart(pool, (s_rs1, t + 1))
                nc.gpsimd.tensor_scalar(nm1[:, k, :], mv1[:, k, 0:1], rs1[:, k, :], -1.0,
                                        ALU.mult, ALU.mult).then_inc(s_nm1, 1)

            def rstd3(t, k):
                apart(pool, (s_keep, t - 1),
                      (s_mv2, t + 1))
                nc.gpsimd.tensor_scalar(ve2[:, k, :], mv2[:, k, 1:2], LN_EPS, None,
                                        ALU.add).then_inc(s_ve2, 1)
                pool.wait_ge(s_ve2, t + 1)
                nc.gpsimd.tensor_tensor(rs2[:, k, :], ve2[:, k, :], halves, ALU.pow).then_inc(s_rs2, 1)
                apart(pool, (s_rs2, t + 1))
                nc.gpsimd.tensor_scalar(nm2[:, k, :], mv2[:, k, 0:1], rs2[:, k, :], -1.0,
                                        ALU.mult, ALU.mult).then_inc(s_nm2, 1)

            run_steps(pool, NT, [(0, rstd2), (1, rstd3)])

            pool.wait_ge(s_slots, 2)
            pool.wait_ge(s_keep, NT)
            for t in range(NT):
                for k in range(2):
                    nc.gpsimd.indirect_dma_start(
                        rows_in, bass.IndirectOffsetOnAxis(ap=slots[:, k, t:t + 1], axis=0),
                        Q[:, t * D:(t + 1) * D], None).then_inc(s_scat, 16)
            stage5_pool(pool)

        @block.vector
        def _(v):
            nc.vector.memset(zeros[:, :], 0.0).then_inc(s_zero, 1)
            nc.vector.memset(ones1[:, :], 1.0).then_inc(s_zero, 1)
            nc.vector.memset(onesb[:, :], 1.0).then_inc(s_zero, 1)
            nc.vector.memset(gm[:, NT:NT + 1, :], 0.0).then_inc(s_zero, 1)
            for T in (K, V):
                nc.vector.memset(T[:, 0:PAD * D], 0.0).then_inc(s_halo0, 1)
                nc.vector.memset(T[:, (NT + PAD) * D:(NT + 2 * PAD) * D], 0.0).then_inc(s_halo0, 1)
            v.wait_ge(s_const, 16)
            nc.vector.tensor_copy(tri[:, :], con[:, P:2 * P]).then_inc(s_zero, 1)
            v.wait_ge(s_x, 64)
            with v.Fori(0, NT // 4) as i:
                for m in range(4):
                    t = 4 * i + m
                    nc.vector.bn_stats(st0[:, ds(t, 1), :], xs[:, ds(t * D, D)]).then_inc(s_stat0, 1)
            v.wait_ge(s_stat0, NT)
            mean, dif, dsq, m2, var = (ln0[:, n, :] for n in range(5))
            col = [st0[:, :, n] for n in range(6)]
            nc.vector.tensor_tensor(mean, col[1], col[4], ALU.add).then_inc(s_mom0, 1)
            nc.vector.tensor_tensor(dif, col[1], col[4], ALU.subtract).then_inc(s_mom0, 1)
            nc.vector.tensor_tensor(m2, col[2], col[5], ALU.add).then_inc(s_mom0, 1)
            v.wait_ge(s_mom0, 3)
            nc.vector.tensor_tensor(dsq, dif, dif, ALU.mult).then_inc(s_mom0, 1)
            nc.vector.tensor_scalar(m2, m2, 1.0 / D, LN_EPS, ALU.mult, ALU.add).then_inc(s_mom0, 1)
            v.wait_ge(s_mom0, 5)
            nc.vector.scalar_tensor_tensor(var, dsq, 0.25, m2, ALU.mult, ALU.add).then_inc(s_mom0, 1)
            nc.vector.tensor_scalar(mean, mean, 0.5, None, ALU.mult).then_inc(s_mom0, 1)
            v.wait_ge(s_mom0, 7)
            v.wait_ge(s_rstd0, 1)

            def norm1(t, k):
                need(v, s_xTp, t - 1)
                nc.vector.tensor_scalar(xn[:, k, :], xs[:, ds(t * D, D)], ln0[:, 0, ds(t, 1)],
                                        ln0[:, 5, ds(t, 1)], ALU.subtract, ALU.mult).then_inc(s_xn, 1)

            run_steps(v, NT, [(0, norm1)])

            v.wait_ge(s_small, 16 * 6 * WIN)
            nc.vector.tensor_scalar(cn[:, 4, :], cn[:, 0, :], posn[0:WH, :], None,
                                    ALU.mult).then_inc(s_cn, 1)
            v.wait_ge(s_cn, 1)
            nc.vector.tensor_tensor(cn[:, 4, :], cn[:, 4, :], cn[:, 1, :], ALU.add).then_inc(s_cn, 1)
            v.wait_ge(s_cna, 1)
            nc.vector.tensor_tensor(cnw2[:, :, :], cnw2[:, :, :],
                                    cn[:, 5:6, :].to_broadcast([WH, J, J]), ALU.mult).then_inc(s_cn, 1)
            v.wait_ge(s_cn, 3)
            nc.vector.tensor_reduce(cn[:, 4, :], cnw2[:, :, :], AX.X, ALU.add).then_inc(s_cn, 1)
            v.wait_ge(s_cn, 4)
            nc.vector.tensor_tensor(cn[:, 4, :], cn[:, 4, :], cn[:, 2, :], ALU.add).then_inc(s_cn, 1)
            v.wait_ge(s_cna, 2)
            nc.vector.tensor_tensor(cn[:, 4, :], cn[:, 5, :], cn[:, 3, :], ALU.mult).then_inc(s_cn, 1)
            v.wait_ge(s_cn, 6)
            nc.vector.tensor_reduce(cnc[:, 1:2], cn[:, 4, :], AX.X, ALU.add).then_inc(s_cn, 1)
            v.wait_ge(s_cn, 7)
            nc.vector.tensor_tensor(cnc[:, 2:3], cnc[:, 1:2], cnc[:, 0:1], ALU.add).then_inc(s_cn, 1)
            v.wait_ge(s_cnp, 1)
            row = crow[:, 0, :]
            byh = lambda a: a.rearrange("p (w h) -> p h w", h=H)
            nc.vector.tensor_copy(row, psC[0][0:1, 0:WH]).then_inc(s_cn, 1)
            v.wait_ge(s_cn, 9)
            nc.vector.tensor_reduce(csum[:, 0, :], byh(row), AX.X, ALU.max).then_inc(s_cn, 1)
            v.wait_ge(s_cn, 10)
            nc.vector.tensor_tensor(crow[:, 1, :].rearrange("p (w h) -> p w h", h=H),
                                    row.rearrange("p (w h) -> p w h", h=H),
                                    csum[:, 0:1, :].to_broadcast([1, WIN, H]),
                                    ALU.subtract).then_inc(s_cn, 1)
            v.wait_ge(s_cna, 3)
            nc.vector.tensor_reduce(csum[:, 1, :], byh(crow[:, 2, :]), AX.X, ALU.add).then_inc(s_cn, 1)
            v.wait_ge(s_cn, 12)
            nc.vector.reciprocal(csum[:, 2, :], csum[:, 1, :]).then_inc(s_cn, 1)
            v.wait_ge(s_cn, 13)
            nc.vector.tensor_tensor(crow[:, 1, :].rearrange("p (w h) -> p w h", h=H),
                                    crow[:, 2, :].rearrange("p (w h) -> p w h", h=H),
                                    csum[:, 2:3, :].to_broadcast([1, WIN, H]),
                                    ALU.mult).then_inc(s_cn, 1)
            v.wait_ge(s_cnp, 2)
            nc.vector.tensor_copy(conn[:, :], psC[1][:, 0:WH]).then_inc(s_cn, 1)
            v.wait_ge(s_cn, 15)

            v.wait_ge(s_qkvs, NT)
            v.wait_ge(s_halo, 16 * 4 * B)
            w_h = lambda a: a.rearrange("p (w h) -> p w h", h=H)
            over_w = lambda a: a.rearrange("p (o h) -> p o h", o=1).to_broadcast([P, WIN, H])

            def scores(t, k):
                need(v, s_raw, t)
                nc.vector.tensor_tensor(
                    prod[:, :].rearrange("p (w d) -> p w d", w=WIN),
                    Q[:, ds(t * D, D)].rearrange("p (o d) -> p o d", o=1).to_broadcast([P, WIN, D]),
                    K[:, ds(t * D, WIN * D)].rearrange("p (w d) -> p w d", w=WIN),
                    ALU.mult).then_inc(s_prod, 1)
                v.wait_ge(s_prod, t + 1)
                nc.vector.tensor_reduce(sc[:, k, 0, :], prod[:, :].rearrange("p (a d) -> p a d", d=DH),
                                        AX.X, ALU.add).then_inc(s_raw, 1)
                v.wait_ge(s_raw, t + 1)
                nc.vector.tensor_reduce(sm[:, k, 0, :], byh(sc[:, k, 0, :]), AX.X,
                                        ALU.max).then_inc(s_max, 1)
                v.wait_ge(s_max, t + 1)
                nc.vector.tensor_tensor(w_h(sc[:, k, 1, :]), w_h(sc[:, k, 0, :]),
                                        over_w(sm[:, k, 0, :]), ALU.subtract).then_inc(s_sc, 1)

            def weigh(t, k):
                v.wait_ge(s_exp, t + 1)
                e = sc[:, k, 2, :]
                nc.vector.tensor_tensor(sc[:, k, 0, :], e, conn[:, :], ALU.mult).then_inc(s_wt, 1)
                nc.vector.tensor_reduce(sm[:, k, 1, :], byh(e), AX.X, ALU.add).then_inc(s_z, 1)
                v.wait_ge(s_wt, t + 1)
                nc.vector.tensor_reduce(sm[:, k, 2, :], byh(sc[:, k, 0, :]), AX.X,
                                        ALU.add).then_inc(s_s1, 1)
                v.wait_ge(s_s1, t + 1)
                nc.vector.scalar_tensor_tensor(sm[:, k, 3, :], sm[:, k, 1, :], 1e-9, sm[:, k, 2, :],
                                               ALU.mult, ALU.add).then_inc(s_den, 1)
                v.wait_ge(s_den, t + 1)
                nc.vector.reciprocal(sm[:, k, 4, :], sm[:, k, 3, :]).then_inc(s_rden, 1)
                v.wait_ge(s_rden, t + 1)
                nc.vector.tensor_tensor(w_h(fw[:, k, :]), w_h(sc[:, k, 0, :]),
                                        over_w(sm[:, k, 4, :]), ALU.mult).then_inc(s_fw, 1)
                v.wait_ge(s_fw, t + 1)
                need(v, s_att, t)
                nc.vector.tensor_tensor(
                    wval[:, :].rearrange("p (a d) -> p a d", d=DH),
                    fw[:, k, :].rearrange("p (a o) -> p a o", o=1).to_broadcast([P, WH, DH]),
                    V[:, ds(t * D, WIN * D)].rearrange("p (a d) -> p a d", d=DH),
                    ALU.mult).then_inc(s_wv, 1)
                v.wait_ge(s_wv, t + 1)
                need(v, s_aTp, t - 1)
                nc.vector.tensor_reduce(att[:, k, :], wval[:, :].rearrange("p (w d) -> p d w", w=WIN),
                                        AX.X, ALU.add).then_inc(s_att, 1)

            def stats2(t, k):
                v.wait_ge(s_wo, t + 1)
                nc.vector.bn_stats(st1[:, k, :], psB[k][:, 0:D]).then_inc(s_st1, 1)
                apart(v, (s_nm1, t - 1),
                      (s_st1, t + 1))
                nc.vector.bn_aggr(mv1[:, k, :], st1[:, k, :]).then_inc(s_mv1, 1)

            def residual(t, k):
                v.wait_ge(s_xm, t + 1)
                v.wait_ge(s_rs1, t + 1)
                nc.vector.scalar_tensor_tensor(xs[:, ds(t * D, D)], psB[k][:, 0:D], rs1[:, k, :],
                                               xm[:, k, :], ALU.mult, ALU.add).then_inc(s_x1, 1)
                apart(v, (s_x1, t + 1))
                nc.vector.bn_stats(st2[:, k, :], xs[:, ds(t * D, D)]).then_inc(s_st2, 1)
                apart(v, (s_nm2, t - 1),
                      (s_st2, t + 1))
                nc.vector.bn_aggr(mv2[:, k, :], st2[:, k, :]).then_inc(s_mv2, 1)

            run_steps(v, NT, [(0, scores), (1, weigh), (2, stats2), (3, residual)])

            step = [0]

            def gop(ins):
                step[0] += 1
                ins.then_inc(s_g, 1)
                v.wait_ge(s_g, step[0])

            v.wait_ge(s_lgs, NT)
            lg = logit[:, :, :]
            p_, q_, oh1, oh2 = (g[n][:, :, :] for n in ("p", "q", "oh1", "oh2"))
            col = lambda n: gs[:, n, :]
            bc = lambda n: gs[:, n, :].rearrange("p (t o) -> p t o", o=1).to_broadcast([P, NT, E])
            per_t = lambda a: a.rearrange("p (o e) -> p o e", o=1).to_broadcast([P, NT, E])
            V_ = nc.vector
            gop(V_.tensor_reduce(col(0), lg, AX.X, ALU.max))
            gop(V_.tensor_tensor(q_, lg, bc(0), ALU.subtract))
            v.wait_ge(s_gexp, 1)
            gop(V_.tensor_reduce(col(1), p_, AX.X, ALU.add))
            gop(V_.reciprocal(col(2), col(1)))
            gop(V_.tensor_tensor(p_, p_, bc(2), ALU.mult))
            for n, oh in ((3, oh1), (4, oh2)):
                gop(V_.tensor_reduce(col(n), p_, AX.X, ALU.max))
                gop(V_.tensor_tensor(q_, p_, bc(n), ALU.is_ge))
                gop(V_.tensor_tensor(q_, q_, per_t(prior), ALU.mult))
                gop(V_.tensor_reduce(col(5), q_, AX.X, ALU.max))
                gop(V_.tensor_tensor(oh, q_, bc(5), ALU.is_equal))
                if n == 3:
                    gop(V_.scalar_tensor_tensor(p_, oh, -2.0, p_, ALU.mult, ALU.add))
            V_.tensor_tensor(gm[:, 0:NT, :], oh1, oh2, ALU.add).then_inc(s_gcast, 1)
            gop(V_.tensor_tensor(col(0), col(3), col(4), ALU.add))
            gop(V_.tensor_scalar(col(0), col(0), 1e-12, None, ALU.max))
            gop(V_.reciprocal(col(1), col(0)))
            gop(V_.tensor_tensor(gates[:, :, 0], col(3), col(1), ALU.mult))
            gop(V_.tensor_tensor(gates[:, :, 1], col(4), col(1), ALU.mult))
            v.wait_ge(s_gpos, 1)
            V_.tensor_copy(gpos[:, :, :].rearrange("p t e -> p (t e)"),
                           psA[0][:, 0:(NT + 1) * E]).then_inc(s_gposs, 1)
            v.wait_ge(s_gposs, 1)
            n_, tl, tf, c_, o_, base = (cnt[:, n, :] for n in range(6))
            gop(V_.tensor_scalar(n_, gpos[:, NT, :], float(P - 1), None, ALU.add))
            gop(V_.tensor_copy(cnti[:, :], n_))
            gop(V_.tensor_single_scalar(cnti[:, :], cnti[:, :], P.bit_length() - 1,
                                        ALU.logical_shift_right))
            gop(V_.tensor_copy(tl, cnti[:, :]))
            gop(V_.memset(o_, 1.0))
            gop(V_.tensor_tensor_scan(c_, o_, tl, 0.0, ALU.mult, ALU.add))
            gop(V_.tensor_scalar(tf, tl, float(-P), float(ROOM), ALU.mult, ALU.add))
            gop(V_.tensor_tensor(n_, gpos[:, NT, :], ebase, ALU.add))
            gop(V_.tensor_copy(tails[:, :], n_[0:1, :]))
            gop(V_.tensor_tensor(base, c_, tl, ALU.subtract))
            gop(V_.scalar_tensor_tensor(base, base, float(P), ebase, ALU.mult, ALU.subtract))
            v.wait_ge(s_jota, 1)
            over_j = lambda a: a.rearrange("p (o e) -> p o e", o=1).to_broadcast([1, TILES, E])
            gop(V_.tensor_tensor(jcmp[:, :, :], over_j(c_[0:1, :]),
                                 jota[:, :].rearrange("p (j o) -> p j o", o=1).to_broadcast([1, TILES, E]),
                                 ALU.is_le))
            gop(V_.tensor_reduce(jf[:, 0, :], jcmp[:, :, :], AX.X, ALU.add))
            gop(V_.tensor_tensor(jcm2[:, :, :], jcmp[:, :, :], over_j(tf[0:1, :]), ALU.mult))
            gop(V_.tensor_reduce(jf[:, 1, :], jcm2[:, :, :], AX.X, ALU.add))
            gop(V_.scalar_tensor_tensor(jf[:, 2, :], jota[:, :], float(P), jf[:, 1, :],
                                        ALU.mult, ALU.add))
            gop(V_.tensor_scalar(jf[:, 0, :], jf[:, 0, :], float(E - 1), None, ALU.min))
            gop(V_.tensor_copy(jobs[:, 0, 0:TILES], jf[:, 0, :]))
            V_.tensor_copy(jobs[:, 1, 0:TILES], jf[:, 2, :]).then_inc(s_jobs, 1)
            gop(V_.tensor_tensor(gpos[:, 0:NT, :], gpos[:, 0:NT, :], per_t(ebase), ALU.add))
            for k, oh in enumerate((oh1, oh2)):
                gop(V_.tensor_tensor(q_, oh, gpos[:, 0:NT, :], ALU.mult))
                gop(V_.tensor_reduce(col(0), q_, AX.X, ALU.add))
                V_.tensor_copy(slots[:, k, :], col(0)).then_inc(s_slots, 1)
                v.wait_ge(s_slots, k + 1)
            gop(V_.tensor_tensor(gpos[:, 0:NT, :], gpos[:, 0:NT, :], per_t(base), ALU.add))
            for k, oh in enumerate((oh1, oh2)):
                gop(V_.tensor_tensor(q_, oh, gpos[:, 0:NT, :], ALU.mult))
                gop(V_.tensor_reduce(col(0), q_, AX.X, ALU.add))
                gop(V_.tensor_copy(backs[:, k, :], col(0)))
            stage4_dve(v)

        @block.scalar
        def _(act):
            def stage(n, k):
                return psT[k][:, 0:D].rearrange("p (c m) -> p c m", c=KC)

            def evac_xT(t, k):
                act.wait_ge(s_xTp, t + 1)
                need(act, s_qkv, t - 1)
                nc.scalar.copy(xnT[:, k, :, :], stage(t, k)).then_inc(s_xT, 1)

            def evac_qkv(t, k):
                act.wait_ge(s_qkv, t + 1)
                nc.scalar.copy(Q[:, ds(t * D, D)], psA[k][:, 0:D])
                nc.scalar.copy(K[:, ds((t + PAD) * D, D)], psA[k][:, D:2 * D])
                nc.scalar.copy(V[:, ds((t + PAD) * D, D)], psB[k][:, 0:D]).then_inc(s_qkvs, 1)

            run_steps(act, NT, [(0, evac_xT), (1, evac_qkv)])

            act.wait_ge(s_cn, 2)
            nc.scalar.activation(cn[:, 5, :], cn[:, 4, :], ACT.Gelu).then_inc(s_cna, 1)
            act.wait_ge(s_cn, 5)
            nc.scalar.activation(cn[:, 5, :], cn[:, 4, :], ACT.Gelu).then_inc(s_cna, 1)
            act.wait_ge(s_cn, 11)
            nc.scalar.activation(crow[:, 2, :], crow[:, 1, :], ACT.Exp).then_inc(s_cna, 1)

            def expo(t, k):
                act.wait_ge(s_sc, t + 1)
                nc.scalar.activation(sc[:, k, 2, :], sc[:, k, 1, :], ACT.Exp,
                                     scale=scale).then_inc(s_exp, 1)

            def evac_attT(t, k):
                act.wait_ge(s_aTp, t + 1)
                need(act, s_wo, t - 1)
                nc.scalar.copy(attT[:, k, :, :], psA[k][:, 0:D].rearrange("p (c m) -> p c m", c=KC)) \
                  .then_inc(s_aT, 1)

            def shift_x(t, k):
                act.wait_ge(s_nm1, t + 1)
                need(act, s_x1, t - 1)
                nc.scalar.activation(xm[:, k, :], xs[:, ds(t * D, D)], ACT.Identity,
                                     bias=nm1[:, k, :]).then_inc(s_xm, 1)

            def norm3(t, k):
                act.wait_ge(s_mv2, t + 1)
                act.wait_ge(s_nm2, t + 1)
                need(act, s_x2p, t - 1)
                nc.scalar.activation(xn[:, k, :], xs[:, ds(t * D, D)], ACT.Identity,
                                     bias=nm2[:, k, :], scale=rs2[:, k, :]).then_inc(s_xn2, 1)
                nc.scalar.activation(Q[:, ds(t * D, D)], xs[:, ds(t * D, D)], ACT.Identity,
                                     bias=nm2[:, k, :], scale=rs2[:, k, :]).then_inc(s_keep, 1)

            def evac_x2T(t, k):
                act.wait_ge(s_x2p, t + 1)
                need(act, s_lg, t - 1)
                nc.scalar.copy(xnT[:, k, :, :], stage(t, k)).then_inc(s_x2T, 1)

            def evac_logits(t, k):
                act.wait_ge(s_lg, t + 1)
                nc.scalar.copy(logit[:, ds(t, 1), :], psC[k][:, 0:E].rearrange("p (o e) -> p o e", o=1)) \
                  .then_inc(s_lgs, 1)

            run_steps(act, NT, [(0, expo), (1, evac_attT), (2, shift_x), (4, norm3), (5, evac_x2T),
                                (6, evac_logits)])
            act.wait_ge(s_g, 2)
            nc.scalar.activation(g["p"][:, :, :], g["q"][:, :, :], ACT.Exp).then_inc(s_gexp, 1)
            stage4_act(act)

        @block.tensor
        def _(pe):
            pe.wait_ge(s_const, 16)
            pe.wait_ge(s_w, 64)
            pe.wait_ge(s_zero, 5)

            def turn_x(t, k):
                pe.wait_ge(s_xn, t + 1)
                need(pe, s_xT, t - 1)
                transposes(pe, xn[:, k, :], psT[k], KC).then_inc(s_xTp, 1)

            def qkv(t, k):
                pe.wait_ge(s_xT, t + 1)
                need(pe, s_qkvs, t - 1)
                for out_, lo, n in ((psA[k], 0, 2 * D), (psB[k], 2 * D, D)):
                    for c in range(KC):
                        mm = nc.tensor.matmul(out_[:, 0:n], xnT[:, k, c, :], wqkv[:, c, lo:lo + n],
                                              start=(c == 0), stop=(c == KC - 1))
                mm.then_inc(s_qkv, 1)

            run_steps(pe, NT, [(0, turn_x), (1, qkv)])

            pe.wait_ge(s_cn, 8)
            nc.tensor.matmul(psC[0][0:1, 0:WH], cnc[:, 2:3], ident[0:WH, 0:WH], start=True,
                             stop=True).then_inc(s_cnp, 1)
            pe.wait_ge(s_cn, 14)
            nc.tensor.matmul(psC[1][:, 0:WH], ones1[:, :], crow[:, 1, :], start=True,
                             stop=True).then_inc(s_cnp, 1)

            def turn_att(t, k):
                pe.wait_ge(s_att, t + 1)
                need(pe, s_aT, t - 1)
                transposes(pe, att[:, k, :], psA[k], KC).then_inc(s_aTp, 1)

            def out_product(t, k):
                pe.wait_ge(s_aT, t + 1)
                need(pe, s_x1, t - 1)
                nc.tensor.matmul(psB[k][:, 0:D], ones1[:, :], bor[:, :], start=True, stop=False)
                for c in range(KC):
                    mm = nc.tensor.matmul(psB[k][:, 0:D], attT[:, k, c, :], wo[:, c, :],
                                          start=False, stop=(c == KC - 1))
                mm.then_inc(s_wo, 1)

            def turn_x2(t, k):
                pe.wait_ge(s_xn2, t + 1)
                need(pe, s_x2T, t - 1)
                transposes(pe, xn[:, k, :], psT[k], KC).then_inc(s_x2p, 1)

            def logits(t, k):
                pe.wait_ge(s_x2T, t + 1)
                need(pe, s_lgs, t - 1)
                for c in range(KC):
                    mm = nc.tensor.matmul(psC[k][:, 0:E], xnT[:, k, c, :], gatew[:, c, :],
                                          start=(c == 0), stop=(c == KC - 1))
                mm.then_inc(s_lg, 1)

            pe.wait_ge(s_cn, 15)
            run_steps(pe, NT, [(0, turn_att), (1, out_product), (4, turn_x2), (5, logits)])

            pe.wait_ge(s_gcast, 1)
            flat = gm[:, :, :].rearrange("p t e -> p (t e)")
            nc.tensor.matmul(psA[0][:, 0:(NT + 1) * E], tri[:, :], flat, start=True, stop=False)
            for t in range(NT):
                n = NT - t
                mm = nc.tensor.matmul(
                    psA[0][:, (t + 1) * E:(NT + 1) * E].rearrange("p (t e) -> p t e", e=E),
                    onesb[:, :], gm[:, t:t + 1, :].to_broadcast([P, n, E]),
                    start=False, stop=(t == NT - 1))
            mm.then_inc(s_gpos, 1)
            stage4_pe(pe)


def kernel(L0_attn_x, L0_attn_wq, L0_attn_wk, L0_attn_wv, L0_attn_wo, L0_attn_bo, L0_attn_cw1, L0_attn_cb1,
           L0_attn_cw2, L0_attn_cb2, L0_attn_cw3, L0_attn_cb3, L0_ffn_gate, L0_ffn_W1, L0_ffn_b1,
           L0_ffn_W2, L0_ffn_b2):
    import numpy as np
    import concourse.bacc as bacc
    from concourse.bass_utils import run_bass_kernel_spmd

    wqkvT = np.concatenate([np.asarray(w).T for w in (L0_attn_wq, L0_attn_wk, L0_attn_wv)], axis=1)
    H, E, N = L0_attn_cw1.shape[0], L0_ffn_W1.shape[0], L0_attn_x.shape[0] * L0_attn_x.shape[1]
    p = np.arange(P)
    consts = np.zeros((P, 3 * P + 8 + E), np.float32)
    consts[:, 0:P] = np.eye(P)
    consts[:, P:2 * P] = p[:, None] < p[None, :]
    consts[:, 2 * P:2 * P + E] = E - np.arange(E)
    consts[:, 2 * P + E:2 * P + 2 * E] = np.arange(E) * (N + P)
    consts[:, 3 * P] = -0.5
    consts[:, 3 * P + 2] = np.linspace(0.0, 1.0, 7, dtype=np.float32)[np.minimum(p // H, 6)]
    consts[:, 3 * P + 3] = -1.0 * (p >= E)
    consts[:, 3 * P + 4] = -1.0 * (p >= 2 * E)
    consts[:, 3 * P + 8:] = (p[:, None] % E == np.arange(E)) & (p[:, None] < 3 * E)
    arrays = {
        "x": L0_attn_x, "wqkvT": wqkvT, "woT": np.asarray(L0_attn_wo).T, "bo": L0_attn_bo,
        "cw1": L0_attn_cw1, "cb1": L0_attn_cb1, "cw2": L0_attn_cw2, "cb2": L0_attn_cb2,
        "cw3": L0_attn_cw3, "cb3": L0_attn_cb3, "gate": L0_ffn_gate, "w1": L0_ffn_W1,
        "b1": L0_ffn_b1, "w2": L0_ffn_W2, "b2": L0_ffn_b2, "consts": consts,
    }
    arrays = {f"in_{n}": np.ascontiguousarray(a) for n, a in arrays.items()}
    nc = bacc.Bacc("TRN2", target_bir_lowering=False, num_devices=1)
    args = [nc.dram_tensor(n, a.shape, mybir.dt.from_np(a.dtype), kind="ExternalInput").ap()
            for n, a in arrays.items()]
    out = nc.dram_tensor("out_x", L0_attn_x.shape, F32, kind="ExternalOutput").ap()
    build(nc, *args, out)
    r = run_bass_kernel_spmd(nc, [arrays], core_ids=[0])
    return r.results[0]["out_x"]
```

```python
from contextlib import ExitStack

import concourse.bass as bass
from concourse import mybir

F32 = mybir.dt.float32
F32R = mybir.dt.float32r
BF16 = mybir.dt.bfloat16
I32 = mybir.dt.int32
ALU = mybir.AluOpType
ACT = mybir.ActivationFunctionType
AX = mybir.AxisListType

P = 128
ds = bass.ds


def even_up(n):
    return n + n % 2


def need(eng, sem, count):
    if isinstance(count, int) and count <= 0:
        return
    eng.wait_ge(sem, count)


def run_steps(eng, n, stages, unroll=2, reuse=2):
    first = min(lag for lag, _ in stages)
    stages = [(lag - first, stage) for lag, stage in stages]
    most = max(lag for lag, _ in stages)

    def step(t, at, edge):
        for lag, stage in stages:
            if not edge or 0 <= t - lag < n:
                stage(t - lag, (at - lag) % unroll)

    start = -(-(most + reuse) // unroll) * unroll
    turns = max(0, (n - start) // unroll)
    if turns < 2:
        start, turns = n + most, 0
    for t in range(start):
        step(t, t % unroll, True)
    if turns:
        with eng.Fori(0, turns) as i:
            for at in range(unroll):
                step(unroll * i + (start + at), at, False)
        for t in range(start + unroll * turns, n + most):
            step(t, t % unroll, True)


def build(nc, x, wqkvT, woT, bo, cw1, cb1, cw2, cb2, cw3, cb3, gate, w1, b1, w2, b2, consts, out):
    B, L, D = x.shape
    N = B * L
    NT = N // P
    H = cw1.shape[0]
    DH = D // H
    J = cw1.shape[1]
    WIN = 7
    PAD = WIN // 2
    WH = WIN * H
    KC = D // P
    E, _, F = w1.shape
    FC = F // P
    TOPK = E // 4
    ROOM = N + P
    TILES = N * TOPK // P + E - 1
    SPARE = (E - 1) * P
    EW = KC * F
    assert EW == FC * D and N == P * NT and L % NT == 0
    SEQP = L // NT
    LN_EPS = 1e-5
    scale = float(DH) ** -0.5
    C = 2
    NU = NT // C
    GROUP = NT // 4
    PW = 5
    G = 2 * C
    RW = D + 2
    LATE = NT - PAD

    rows_in = nc.dram_tensor("rows_in", [E * ROOM + SPARE, RW], F32, kind="Internal").ap()
    rows_back = nc.dram_tensor("rows_back", [TOPK * N + (TILES + 1) * P, D], F32, kind="Internal").ap()

    with ExitStack() as top:
        def sem(name):
            return top.enter_context(nc.semaphore(name))

        def sb(ctx, name, shape, dt=F32):
            return ctx.enter_context(nc.sbuf_tensor(name, shape, dt))

        def psum(ctx, name, shape, dt=F32):
            return ctx.enter_context(nc.psum_tensor(name, shape, dt))

        xs = sb(top, "xs", [P, NT * D])
        con = sb(top, "con", [P, 3 * P + 8 + E])
        ident = con[:, 0:P]
        halves = con[:, 3 * P:3 * P + 1]
        later = lambda n: con[0:3, 3 * P + 5 + n:3 * P + 6 + n]
        epss = con[:, 3 * P + 7:3 * P + 8]
        minus = con[:, 3 * P + 1:3 * P + 2]
        posn = con[:, 3 * P + 2:3 * P + 3]
        gates = sb(top, "gates", [P, TOPK, NT])
        jobs = sb(top, "jobs", [1, 2, TILES], I32)
        mark = sb(top, "mark", [P, TILES])
        past = sb(top, "past", [P, TILES])
        tails = sb(top, "tails", [1, E], I32)
        fill = sb(top, "fill", [P, RW])

        s_const = sem("const_loaded")
        s_small = sem("small_loaded")

        def apart(eng, *waits):
            waits = [(s, n if isinstance(n, int) else eng.to_reg(n)) for s, n in waits]
            eng.wait_ge(s_const, 16)
            for s, n in waits:
                need(eng, s, n)
        s_x = [sem(f"x_loaded{n}") for n in range(4)]
        s_w = sem("attn_weights_loaded")


        ctx = ExitStack()
        Q = sb(ctx, "Q", [P, NT, RW])
        K = sb(ctx, "K", [P, (NT + 2 * PAD) * D])
        V = sb(ctx, "V", [P, (NT + 2 * PAD) * D])
        prod = sb(ctx, "prod", [P, C, WIN * D])
        wval = sb(ctx, "wval", [P, C, WIN * D])
        wqkv = sb(ctx, "wqkv", [P, KC, 3 * D])
        wo = sb(ctx, "wo", [P, KC, D])
        bo3 = sb(ctx, "bo3", [3, C, D], BF16)
        ones3 = sb(ctx, "ones3", [3, P], BF16)
        ones1 = sb(ctx, "ones1", [1, P])
        gatew = sb(ctx, "gatew", [P, KC, E])
        st0 = sb(ctx, "st0", [P, NT, 6])
        ln0 = sb(ctx, "ln0", [P, 6, NT])
        xn = sb(ctx, "xn", [P, C, D])
        xnT = sb(ctx, "xnT", [P, C, KC, P])
        conn = sb(ctx, "conn", [P, WH])
        raw = sb(ctx, "raw", [P, C, WH])
        low_s = sb(ctx, "low_s", [P, C, WH])
        ew = sb(ctx, "ew", [P, 2, C, WH])
        fw = sb(ctx, "fw", [P, C, WH])
        top_s = sb(ctx, "top_s", [P, C, H])
        zs = sb(ctx, "zs", [P, 2, C, H])
        den = sb(ctx, "den", [P, C, H])
        rden = sb(ctx, "rden", [P, C, H])
        attT = sb(ctx, "attT", [P, KC, C, P])
        xm = sb(ctx, "xm", [P, C, D])
        xn2 = sb(ctx, "xn2", [P, C, D])
        x2T = sb(ctx, "x2T", [P, C, KC, P])
        lst, lmv, lve, lneg, lrs, lnm = ([sb(ctx, f"ln{m + 2}_{n}", [P, C] + w) for m in range(2)]
                                         for n, w in (("stats", [6]), ("moments", [2]), ("var", []),
                                                      ("neg_mean", []), ("rstd", []), ("shift", [])))
        xr = sb(ctx, "xr", [P, G, RW])
        lend = [prod[:, :, :].rearrange("p c d -> p (c d)"), 0]

        def carve(rows, *shape):
            n = 1
            for m in shape:
                n *= m
            flat, at = lend
            lend[1] += n
            v = flat[0:rows, at:at + n]
            return v if len(shape) == 1 else v.rearrange("p (a b) -> p a b", b=shape[1])

        cn = carve(WH, 6, J)
        cnw2 = carve(WH, J, J)
        cnc = carve(WH, 4)
        crow = carve(1, 3, WH)
        csum = carve(1, 4, H)
        bo_raw, bo_mid, bo_low = (carve(3, D) for _ in range(3))

        psa = ExitStack()
        psT = [psum(psa, f"psT{n}", [P, 512]) for n in range(2)]
        psA = [psum(psa, f"psA{n}", [P, 512]) for n in range(2)]
        psB = [psum(psa, f"psB{n}", [P, 512]) for n in range(2)]
        psC = [psum(psa, f"psC{n}", [P, 512]) for n in range(2)]

        psQ, psK, psV, psW = psA[0], psA[1], psC[0], psC[1]
        psY, psL, psX, psX2 = psB[0], psB[1], psT[0], psT[1]
        psG = psX2[:, 0:(G + 1) * E].rearrange("p (t e) -> p t e", e=E)
        s_zero = sem("zeros_set")
        s_stat0 = sem("ln1_stats")
        s_mom0 = sem("ln1_moments")
        s_rstd0 = sem("ln1_rstd")
        s_xn = sem("xn_ready")
        s_xTp = sem("xn_transposed")
        s_xT = sem("xnT_ready")
        s_qkv = sem("qkv_done")
        s_qkvs = sem("qkv_stored")
        s_halo0 = sem("halo_zeroed")
        s_halo = sem("halo_shifted")
        s_cn = sem("connectivity_step")
        s_cna = sem("connectivity_gelu")
        s_cnp = sem("connectivity_pe")
        (s_prod, s_raw, s_max, s_low, s_exp, s_wt, s_zs, s_den, s_rden, s_fw, s_wvp, s_wvd, s_ws, s_aT,
         s_wo) = (sem(n) for n in (
             "products_ready", "raw_scores_ready", "score_max_ready", "lowered_scores_ready",
             "exp_ready", "weighted_exp_ready", "sums_ready", "denominator_ready",
             "reciprocal_ready", "weights_ready", "weighted_values_gpsimd",
             "weighted_values_vector", "window_summed", "attnT_ready", "out_product_done"))
        s_lst, s_lmv, s_lve, s_lrs, s_lnm, s_lneg = (
            [sem(f"ln{m + 2}_{n}") for m in range(2)]
            for n in ("stats", "moments", "var_eps", "rstd", "shift", "neg_mean"))
        (s_xm, s_x1, s_xn2, s_x2p, s_x2T, s_lg, s_lgs, s_keep, s_nm0, s_bo) = (sem(n) for n in (
            "x_shifted", "x1_ready", "xn2_ready", "xn2_transposed", "x2T_ready", "logits_done",
            "logits_stored", "xn2_kept", "ln1_shift", "out_bias_split"))

        lgt = sb(ctx, "lgt", [P, G, E])
        gl = sb(ctx, "gl", [P, G, E])
        gp = sb(ctx, "gp", [P, G, E])
        gq = sb(ctx, "gq", [P, G, E])
        gu = sb(ctx, "gu", [P, G, E])
        gsc = sb(ctx, "gsc", [P, 7, G])
        gtop = sb(ctx, "gtop", [P, TOPK, G])
        oh = sb(ctx, "oh", [P, TOPK, G, E])
        ohp = sb(ctx, "ohp", [P, TOPK, G, E])
        gm = sb(ctx, "gm", [P, G + 1, E], BF16)
        tri = sb(ctx, "tri", [P, P], BF16)
        onesb = sb(ctx, "onesb", [P, P], BF16)
        gpos = sb(ctx, "gpos", [P, G, E])
        base = sb(ctx, "base", [P, E])
        slotf = sb(ctx, "slotf", [P, TOPK, G])
        slots = sb(ctx, "slots", [P, TOPK, G], I32)
        lend[1] = 0
        cnt = carve(P, 6, E)
        jcmp = carve(P, TILES, E)
        jcm2 = carve(P, TILES, E)
        jf = carve(P, 3, TILES)
        jota = carve(P, TILES)
        cnti = sb(ctx, "cnti", [P, E], I32)
        prior = con[:, P * 2:P * 2 + E]
        ebase = con[:, P * 2 + E:P * 2 + 2 * E]
        (s_glow, s_gexp, s_g, s_gmask, s_gcnt, s_slots, s_first, s_rows) = (sem(n) for n in (
            "gate_lowered", "gate_exp", "gate_step", "gate_masks", "pairs_counted", "slots_ready",
            "first_experts_kept", "rows_staged"))
        (s_jobs, s_job, s_spare, s_tail, s_scat, s_iota) = (sem(n) for n in (
            "jobs_ready", "job_step", "spare_filled", "tails_filled", "rows_scattered",
            "numbers_set"))

        s_wlast = [sem(f"last_expert_weights_loaded{n}") for n in range(2)]
        s_wraw = [sem(f"expert_weights_loaded{n}") for n in range(2)]
        s_whi = sem("weights_high")
        s_wlo = sem("weights_low")
        s_bias = sem("bias_step")
        s_braw = sem("biases_loaded")
        s_xg = [sem(f"tile_rows_loaded{n}") for n in range(4)]
        s_xoff, s_xid = sem("tile_id_step"), sem("tile_ids")
        s_xgp = sem("tile_transposed")
        s_xgh = sem("tile_high")
        s_xgl = sem("tile_low")
        s_h = sem("hidden_done")
        s_hr = sem("hidden_relu")
        s_hTp = sem("hidden_transposed")
        s_hTh = sem("hiddenT_high")
        s_hTl = sem("hiddenT_low")
        s_y = sem("tile_out_done")
        s_ys = sem("tile_out_copied")
        s_yst = [sem(f"tile_out_scattered{n}") for n in range(4)]
        s_yp = [sem(f"results_loaded{n}") for n in range(2)]
        (s_o1, s_o2, s_st4, s_mv4, s_ve4, s_rs4, s_neg4, s_nm4, s_nrm, s_fin) = (sem(n) for n in (
            "first_weighed", "results_added", "ln4_stats", "ln4_moments", "ln4_var_eps",
            "ln4_rstd", "ln4_neg_mean", "ln4_shift", "ln4_normed", "final_ready"))
        s_out = [sem(f"out_stored{n}") for n in range(2)]

        ctx.close()
        ctx = ExitStack()
        w1h = sb(ctx, "w1h", [P, E * EW], F32R)
        sb(ctx, "gap_q", [P, NT * RW - E * EW])
        alias = ExitStack()
        halo = 2 * PAD * D
        w1r = sb(alias, "w1r", [P, E * EW])
        sb(alias, "gap_kr", [P, halo])
        w2r = sb(alias, "w2r", [P, E * EW])
        alias.close()
        w1l = sb(ctx, "w1l", [P, E * EW], F32R)
        sb(ctx, "gap_k", [P, halo])
        w2l = sb(ctx, "w2l", [P, E * EW], F32R)
        sb(ctx, "gap_v", [P, halo])
        w2h = sb(ctx, "w2h", [P, E * EW], F32R)
        bias = sb(ctx, "bias", [P, F + D], BF16)
        sel = sb(ctx, "sel", [P, E * P], BF16)
        xg = sb(ctx, "xg", [P, 4, RW])
        xoff = sb(ctx, "xoff", [P, 3])
        xid = sb(ctx, "xid", [P, 4], I32)
        xgh = sb(ctx, "xgh", [P, 2, KC, P], F32R)
        xgl = sb(ctx, "xgl", [P, 2, KC, P], F32R)
        ysb = sb(ctx, "ysb", [P, 4, D])
        alias = ExitStack()
        braw = sb(alias, "braw", [3 * E, 3, F + D])
        alias.close()
        hr = sb(ctx, "hr", [P, 2, F])
        hTh = sb(ctx, "hTh", [P, 2, FC, P], F32R)
        hTl = sb(ctx, "hTl", [P, 2, FC, P], F32R)
        ctx.close()
        M = 4
        yp = sb(top, "yp", [P, 2, TOPK, M * D])
        moe = sb(top, "moe", [P, 2, M * D])
        nrm = sb(top, "nrm", [P, 2, M * D])
        fin = sb(top, "fin", [P, 2, M * D])
        st4 = sb(top, "st4", [P, M, 6])
        mv4 = sb(top, "mv4", [P, M, 2])
        ve4, neg4, rs4, nm4 = (sb(top, n, [P, M]) for n in ("ve4", "neg4", "rs4", "nm4"))

        xv = x.rearrange("b (q t) d -> (b q) (t d)", t=NT)
        ov = out.rearrange("b (q t) d -> (b q) (t d)", t=NT)


        w1v = w1.rearrange("e (c p) f -> p e c f", p=P)
        w2v = w2.rearrange("e (c p) d -> p e c d", p=P)
        parts = ((w1v, w1r, w1h, w1l), (w2v, w2r, w2h, w2l))

        def experts(eng, body):
            with eng.Fori(0, E - 1) as e:
                for part in range(2):
                    body(e, part)
            for part in range(2):
                body(E - 1, part)

        def stage4_sp(sp):
            def load_w(e, part):
                if part == 0:
                    apart(sp, (s_prod, G * e + G))
                else:
                    apart(sp, (s_wvp, G * e + G), (s_wvd, G * e + G))
                src, raw_w = parts[part][0:2]
                sp.dma_start(raw_w[:, ds(e * EW, EW)].rearrange("p (e c f) -> p e c f", e=1,
                                                                c=src.shape[2]),
                             src[:, ds(e, 1)]).then_inc((s_wlast if isinstance(e, int) else
                                                         s_wraw)[part], 16)

            experts(sp, load_w)
            sp.wait_ge(s_jobs, 1)
            for e in range(E):
                first = sp.value_load(tails[0:1, e:e + 1], min_val=0, max_val=E * ROOM - P)
                sp.dma_start(rows_in[ds(first, P), :], fill[:, :]).then_inc(s_tail, 16)
            sp.wait_ge(s_scat, 16 * TOPK * NT)
            for n in range(3):
                r = slice(n * E, (n + 1) * E)
                sp.dma_start(braw[r, 0, 0:F], b1).then_inc(s_braw, 16)
                sp.dma_start(braw[r, 0, F:F + D], b2).then_inc(s_braw, 16)
            sp.wait_ge(s_spare, 16 * (E - 1))
            sp.wait_ge(s_tail, 16 * E)

            def load_rows(j, k):
                need(sp, s_xgp, j - 3)
                need(sp, s_xid, j - 3)
                first = sp.value_load(jobs[0:1, 1, ds(j, 1)], min_val=0,
                                      max_val=E * ROOM + SPARE - P)
                sp.dma_start(xg[:, k, :], rows_in[ds(first, P), :]).then_inc(s_xg[k], 16)

            run_steps(sp, TILES, [(0, load_rows)], 4, 4)

            for k in range(4):
                sp.wait_ge(s_yst[k], 16 * ((TILES + 3 - k) // 4))
            back = rows_back[0:TOPK * N, :].rearrange("(k p t) d -> k p (t d)", k=TOPK, t=NT)

            def load_back(q, k):
                need(sp, s_o2, M * (q - 1))
                for n in range(TOPK):
                    sp.dma_start(yp[:, k, n, :], back[n, :, ds(q * M * D, M * D)]) \
                      .then_inc(s_yp[k], 16)

            def store_out(q, k):
                sp.wait_ge(s_fin, q + 1)
                sp.dma_start(ov[:, ds(q * M * D, M * D)], fin[:, k, :]).then_inc(s_out[k], 16)

            run_steps(sp, NT // M, [(0, load_back), (2, store_out)])
            for k in range(2):
                sp.wait_ge(s_out[k], 16 * NT // M // 2)

        def stage4_act(act):
            def high(e, part):
                if isinstance(e, int):
                    act.wait_ge(s_wlast[part], 16)
                nc.scalar.copy(parts[part][2][:, ds(e * EW, EW)],
                               parts[part][1][:, ds(e * EW, EW)]).then_inc(s_whi, 1)

            act.wait_ge(s_jobs, 1)
            act.wait_ge(s_rows, NU)
            for part in range(2):
                act.wait_ge(s_wraw[part], 16 * (E - 1))
            experts(act, high)

            def rows_high(j, k):
                act.wait_ge(s_xgp, j + 1)
                need(act, s_h, j - 1)
                k = k % 2
                nc.scalar.copy(xgh[:, k, :, :], psT[k][:, 0:D].rearrange("p (c m) -> p c m", c=KC)) \
                  .then_inc(s_xgh, 1)

            def hidden_high(j, k):
                act.wait_ge(s_hTp, j + 1)
                need(act, s_y, j - 1)
                k = k % 2
                nc.scalar.copy(hTh[:, k, :, :], psB[k][:, :].rearrange("p (c m) -> p c m", c=FC)) \
                  .then_inc(s_hTh, 1)

            def relu(j, k):
                act.wait_ge(s_h, j + 1)
                need(act, s_hTp, j - 1)
                k = k % 2
                nc.scalar.activation(hr[:, k, :], psA[k][:, 0:F], ACT.Relu).then_inc(s_hr, 1)

            run_steps(act, TILES, [(0, rows_high), (2, hidden_high), (1, relu)], 4)

            def norm4(q, k):
                act.wait_ge(s_nm4, q + 1)
                need(act, s_fin, q - 1)
                for m in range(M):
                    mv = nc.scalar.activation(nrm[:, k, m * D:(m + 1) * D],
                                              moe[:, k, m * D:(m + 1) * D], ACT.Identity,
                                              bias=nm4[:, m:m + 1], scale=rs4[:, m:m + 1])
                mv.then_inc(s_nrm, 1)

            run_steps(act, NT // M, [(0, norm4)])

        def stage4_dve(v):
            def low(e, part):
                v.wait_ge(s_whi, 2 * e + part + 1)
                _, raw_w, whi, wlo = parts[part]
                nc.vector.tensor_tensor(wlo[:, ds(e * EW, EW)], raw_w[:, ds(e * EW, EW)],
                                        whi[:, ds(e * EW, EW)].bitcast(F32),
                                        ALU.subtract).then_inc(s_wlo, 1)

            experts(v, low)

            v.wait_ge(s_scat, 16 * TOPK * NT)
            nc.vector.memset(bias[:, :], 0.0).then_inc(s_bias, 1)
            nc.vector.tensor_copy(sel[:, :], con[:, 3 * P + 8:3 * P + 8 + E].rearrange(
                "p (e o) -> p e o", o=1).to_broadcast([P, E, P])).then_inc(s_bias, 1)
            v.wait_ge(s_braw, 16 * 6)
            G = 3 * E
            raw, hi, mid = (braw[:, n, :] for n in range(3))
            less = lambda n: con[0:G, 3 * P + 3 + n:3 * P + 4 + n]
            v.wait_ge(s_bias, 2)
            nc.vector.tensor_copy(bias[0:G, :], raw).then_inc(s_bias, 1)
            v.wait_ge(s_bias, 3)
            nc.vector.scalar_tensor_tensor(hi, bias[0:G, :], less(0), raw, ALU.mult,
                                           ALU.add).then_inc(s_bias, 1)
            v.wait_ge(s_bias, 4)
            nc.vector.tensor_copy(bias[0:G, :], hi).then_inc(s_bias, 1)
            v.wait_ge(s_bias, 5)
            nc.vector.scalar_tensor_tensor(mid, bias[0:G, :], less(1), hi, ALU.mult,
                                           ALU.add).then_inc(s_bias, 1)
            v.wait_ge(s_bias, 6)
            nc.vector.tensor_copy(bias[0:G, :], mid).then_inc(s_bias, 1)

            def rows_low(j, k):
                v.wait_ge(s_xgh, j + 1)
                k2 = k % 2
                nc.vector.tensor_tensor(xgl[:, k2, :, :].rearrange("p c m -> p (c m)"), psT[k2][:, 0:D],
                                        xgh[:, k2, :, :].bitcast(F32).rearrange("p c m -> p (c m)"),
                                        ALU.subtract).then_inc(s_xgl, 1)
                need(v, s_xid, j)
                w = xg[:, k, D + 1:D + 2]
                nc.vector.tensor_tensor(xoff[:, 0:1], w, mark[:, ds(j, 1)],
                                        ALU.not_equal).then_inc(s_xoff, 1)
                nc.vector.scalar_tensor_tensor(xoff[:, 1:2], w, 0.0, past[:, ds(j, 1)], ALU.is_equal,
                                               ALU.mult).then_inc(s_xoff, 1)
                apart(v, (s_xoff, 3 * j + 2))
                nc.vector.scalar_tensor_tensor(xoff[:, 2:3], xoff[:, 0:1], float(N), xoff[:, 1:2],
                                               ALU.mult, ALU.add).then_inc(s_xoff, 1)
                apart(v, (s_xoff, 3 * j + 3),
                      (s_yst[k], 4 * (j - k)))
                nc.vector.tensor_tensor(xid[:, k:k + 1], xoff[:, 2:3], xg[:, k, D:D + 1],
                                        ALU.add).then_inc(s_xid, 1)

            def hidden_low(j, k):
                v.wait_ge(s_hTh, j + 1)
                k = k % 2
                nc.vector.tensor_tensor(hTl[:, k, :, :].rearrange("p c m -> p (c m)"), psB[k][:, :],
                                        hTh[:, k, :, :].bitcast(F32).rearrange("p c m -> p (c m)"),
                                        ALU.subtract).then_inc(s_hTl, 1)

            def copy_out(j, k):
                v.wait_ge(s_y, j + 1)
                need(v, s_yst[k], 4 * (j - k))
                nc.vector.tensor_copy(ysb[:, k, :], psC[k % 2][:, 0:D]).then_inc(s_ys, 1)

            run_steps(v, TILES, [(0, rows_low), (2, hidden_low), (3, copy_out)], 4, 4)

            def combine(q, k):
                v.wait_ge(s_yp[k], 16 * (q - k) + 32)
                need(v, s_nrm, q - 1)
                for m in range(M):
                    r = slice(m * D, (m + 1) * D)
                    nc.vector.tensor_scalar(moe[:, k, r], yp[:, k, 0, r], gates[:, 0, ds(q * M + m, 1)],
                                            None, ALU.mult).then_inc(s_o1, 1)
                for m in range(M):
                    r = slice(m * D, (m + 1) * D)
                    apart(v, (s_o1, q * M + m + 1))
                    nc.vector.scalar_tensor_tensor(moe[:, k, r], yp[:, k, 1, r],
                                                   gates[:, 1, ds(q * M + m, 1)], moe[:, k, r],
                                                   ALU.mult, ALU.add).then_inc(s_o2, 1)
                for m in range(M):
                    apart(v, (s_mv4, q * M), (s_o2, q * M + m + 1))
                    nc.vector.bn_stats(st4[:, m, :], moe[:, k, m * D:(m + 1) * D]).then_inc(s_st4, 1)
                for m in range(M):
                    apart(v, (s_nm4, q),
                          (s_st4, q * M + m + 1))
                    nc.vector.bn_aggr(mv4[:, m, :], st4[:, m, :]).then_inc(s_mv4, 1)

            run_steps(v, NT // M, [(0, combine)])

        def stage5_pool(pool):
            def scatter_back(j, k):
                apart(pool, (s_xid, j + 1), (s_ys, j + 1))
                nc.gpsimd.indirect_dma_start(
                    rows_back, bass.IndirectOffsetOnAxis(ap=xid[:, k:k + 1], axis=0),
                    ysb[:, k, :], None).then_inc(s_yst[k], 16)

            run_steps(pool, TILES, [(0, scatter_back)], 4)

            def rstd4(q, k):
                pair = lambda a: a.to_broadcast([P, M])
                pool.wait_ge(s_mv4, M * q + M)
                nc.gpsimd.tensor_tensor(ve4[:, :], mv4[:, :, 1], pair(epss), ALU.add) \
                  .then_inc(s_ve4, 1)
                need(pool, s_nm4, q)
                nc.gpsimd.tensor_tensor(neg4[:, :], mv4[:, :, 0], pair(minus), ALU.mult) \
                  .then_inc(s_neg4, 1)
                pool.wait_ge(s_ve4, q + 1)
                need(pool, s_nrm, q)
                nc.gpsimd.tensor_tensor(rs4[:, :], ve4[:, :], pair(halves), ALU.pow) \
                  .then_inc(s_rs4, 1)
                pool.wait_ge(s_neg4, q + 1)
                pool.wait_ge(s_rs4, q + 1)
                nc.gpsimd.tensor_tensor(nm4[:, :], neg4[:, :], rs4[:, :], ALU.mult) \
                  .then_inc(s_nm4, 1)

            def finish(q, k):
                pool.wait_ge(s_nrm, q + 1)
                need(pool, s_out[k], 8 * (q - k))
                nc.gpsimd.tensor_tensor(fin[:, k, :], nrm[:, k, :], xs[:, ds(q * M * D, M * D)],
                                        ALU.add).then_inc(s_fin, 1)

            run_steps(pool, NT // M, [(0, rstd4), (1, finish)])

        def stage4_pe(pe):
            pe.wait_ge(s_jobs, 1)
            pe.wait_ge(s_wlo, 2 * E)
            pe.wait_ge(s_bias, 7)

            def turn_rows(j, k):
                pe.wait_ge(s_xg[k], 4 * (j - k) + 16)
                need(pe, s_xgl, j - 1)
                transposes(pe, xg[:, k, :], psT[k % 2], KC).then_inc(s_xgp, 1)

            def product(pe, bank, j, xh, xl, wh, wl, chunks, n, bias_at):
                e = pe.value_load(jobs[0:1, 0, ds(j, 1)], min_val=0, max_val=E - 1)
                nc.tensor.matmul(bank, sel[:, ds(e * P, P)], bias[:, bias_at:bias_at + n],
                                 start=True, stop=False)
                for c in range(chunks):
                    w = ds(e * EW + c * n, n)
                    nc.tensor.matmul(bank, xl[:, c, :], wh[:, w], start=False, stop=False)
                    nc.tensor.matmul(bank, xh[:, c, :], wl[:, w], start=False, stop=False)
                    mm = nc.tensor.matmul(bank, xh[:, c, :], wh[:, w], start=False,
                                          stop=(c == chunks - 1))
                return mm

            def hidden(j, k):
                apart(pe, (s_hr, j - 1),
                      (s_xgl, j + 1))
                k = k % 2
                product(pe, psA[k][:, 0:F], j, xgh[:, k], xgl[:, k], w1h, w1l, KC, F, 0) \
                    .then_inc(s_h, 1)

            def turn_hidden(j, k):
                pe.wait_ge(s_hr, j + 1)
                need(pe, s_hTl, j - 1)
                k = k % 2
                transposes(pe, hr[:, k, :], psB[k], FC).then_inc(s_hTp, 1)

            def outp(j, k):
                apart(pe, (s_ys, j - 1),
                      (s_hTl, j + 1))
                k = k % 2
                product(pe, psC[k][:, 0:D], j, hTh[:, k], hTl[:, k], w2h, w2l, FC, D, F) \
                    .then_inc(s_y, 1)

            run_steps(pe, TILES, [(0, turn_rows), (2, turn_hidden), (1, hidden), (2, outp)], 4, 4)

        def proj_step(w, c):
            r = w * C + c
            return (r + LATE) % NT if isinstance(w, int) else r - PAD

        def weighted(eng, on, u, c, lo, hi):
            eng.wait_ge(s_fw, u + 1)
            need(eng, s_ws, C * u + c - 1)
            n = (hi - lo) * H
            return on.tensor_tensor(
                wval[:, c, lo * D:hi * D].rearrange("p (a d) -> p a d", d=DH),
                fw[:, c, lo * H:hi * H].rearrange("p (a o) -> p a o", o=1).to_broadcast([P, n, DH]),
                V[:, ds((u * C + c + lo) * D, (hi - lo) * D)].rearrange("p (a d) -> p a d", d=DH),
                ALU.mult)

        w_h = lambda a: a.rearrange("p c (w h) -> p c w h", h=H)
        SMALL = 6 * WIN + 3

        def transposes(pe, src, dst, chunks):
            for c in range(chunks):
                mm = nc.tensor.transpose(dst[:, c * P:(c + 1) * P], src[:, c * P:(c + 1) * P], ident)
            return mm

        block = top.enter_context(nc.Block())

        @block.sync
        def _(sp):
            sp.dma_start(con[:, :], consts).then_inc(s_const, 16)
            for n in (3, 0, 1, 2):
                m = GROUP * D
                sp.dma_start(xs[:, n * m:(n + 1) * m], xv[:, n * m:(n + 1) * m]).then_inc(s_x[n], 16)
                if n == 3:
                    sp.dma_start(wqkv[:, :, :], wqkvT.rearrange("(c p) n -> p c n", p=P)) \
                      .then_inc(s_w, 16)
            sp.dma_start(wo[:, :, :], woT.rearrange("(c p) n -> p c n", p=P)).then_inc(s_w, 16)
            sp.dma_start(gatew[:, :, :], gate.rearrange("(c p) n -> p c n", p=P)).then_inc(s_w, 16)
            sp.wait_ge(s_halo0, 4)
            sp.wait_ge(s_qkvs, 2)
            for T in (K, V):
                for b in range(B):
                    lo, hi = b * SEQP, (b + 1) * SEQP
                    sp.dma_start(T[lo + 1:hi, 0:PAD * D],
                                 T[lo:hi - 1, NT * D:(NT + PAD) * D]).then_inc(s_halo, 16)
            sp.wait_ge(s_qkvs, 3)
            for T in (K, V):
                for b in range(B):
                    lo, hi = b * SEQP, (b + 1) * SEQP
                    sp.dma_start(T[lo:hi - 1, (NT + PAD) * D:(NT + 2 * PAD) * D],
                                 T[lo + 1:hi, PAD * D:2 * PAD * D]).then_inc(s_halo, 16)
            sp.wait_ge(s_iota, 3)
            sp.wait_ge(s_zero, 1)
            for n in range(E - 1):
                sp.dma_start(rows_in[E * ROOM + n * P:E * ROOM + (n + 1) * P, :],
                             fill[:, :]).then_inc(s_spare, 16)
            stage4_sp(sp)

        @block.gpsimd
        def _(pool):
            number = dict(allow_small_or_imprecise_dtypes=True)
            nc.gpsimd.iota(past[:, :], [[P, TILES]], base=0, channel_multiplier=0,
                           **number).then_inc(s_iota, 1)
            nc.gpsimd.iota(Q[:, :, D], [[1, NT]], base=0, channel_multiplier=NT,
                           **number).then_inc(s_iota, 1)
            nc.gpsimd.iota(fill[:, D:D + 1], [[1, 1]], base=N, channel_multiplier=1,
                           **number).then_inc(s_iota, 1)
            pool.wait_ge(s_const, 16)
            for i, n in enumerate((3, 0, 1, 2)):
                r = slice(n * GROUP, (n + 1) * GROUP)
                pool.wait_ge(s_mom0, 7 * i + 7)
                nc.gpsimd.tensor_tensor(ln0[:, 5, r], ln0[:, 4, r], halves.to_broadcast([P, GROUP]),
                                        ALU.pow).then_inc(s_rstd0, 1)
                pool.wait_ge(s_rstd0, i + 1)
                nc.gpsimd.tensor_tensor(ln0[:, 3, r], ln0[:, 0, r], ln0[:, 5, r],
                                        ALU.mult).then_inc(s_nm0, 1)

            def rstd(m, u, used):
                var = lmv[m][:, :, 1]
                mean = lmv[m][:, :, 0]
                pair = lambda a: a.to_broadcast([P, C])
                pool.wait_ge(s_lmv[m], C * u + C)
                nc.gpsimd.tensor_tensor(lve[m][:, :], var, pair(epss), ALU.add).then_inc(s_lve[m], 1)
                need(pool, s_lnm[m], u)
                nc.gpsimd.tensor_tensor(lneg[m][:, :], mean, pair(minus),
                                        ALU.mult).then_inc(s_lneg[m], 1)
                pool.wait_ge(s_lve[m], u + 1)
                for sem_, n in used:
                    need(pool, sem_, n)
                nc.gpsimd.tensor_tensor(lrs[m][:, :], lve[m][:, :], pair(halves),
                                        ALU.pow).then_inc(s_lrs[m], 1)
                pool.wait_ge(s_lneg[m], u + 1)
                pool.wait_ge(s_lrs[m], u + 1)
                nc.gpsimd.tensor_tensor(lnm[m][:, :], lneg[m][:, :], lrs[m][:, :],
                                        ALU.mult).then_inc(s_lnm[m], 1)

            def rstd2(u, k):
                rstd(0, u, ((s_x1, C * u),))

            def rstd3(u, k):
                rstd(1, u, ((s_xn2, u),))

            def weigh_exp(u, k):
                pool.wait_ge(s_exp, u + 1)
                need(pool, s_zs, u)
                need(pool, s_fw, u)
                nc.gpsimd.tensor_tensor(ew[:, 1], ew[:, 0],
                                        conn[:, :].rearrange("p (o a) -> p o a", o=1)
                                        .to_broadcast([P, C, WH]), ALU.mult).then_inc(s_wt, 1)

            def weights(u, k):
                pool.wait_ge(s_rden, u + 1)
                need(pool, s_wvd, C * u)
                need(pool, s_wvp, C * u)
                nc.gpsimd.tensor_tensor(
                    w_h(fw[:, :, :]), w_h(ew[:, 1]),
                    rden[:, :, :].rearrange("p c (o h) -> p c o h", o=1).to_broadcast([P, C, WIN, H]),
                    ALU.mult).then_inc(s_fw, 1)
                for c in range(C):
                    weighted(pool, nc.gpsimd, u, c, 0, PW).then_inc(s_wvp, 1)

            def send(n):
                for i in range(G):
                    nc.gpsimd.indirect_dma_start(
                        rows_in, bass.IndirectOffsetOnAxis(ap=slots[:, n, i:i + 1], axis=0),
                        xr[:, i, :], None).then_inc(s_scat, 16)

            def scatter(u, k):
                if k == 1:
                    apart(pool, (s_slots, u + 1), (s_rows, u + 1))
                    send(0)
                elif not (isinstance(u, int) and u == 0):
                    send(1)

            pool.wait_ge(s_cn, 15)
            pool.wait_ge(s_halo, 16 * 4 * B)
            run_steps(pool, NU, [(12, scatter), (8, rstd2), (6, weigh_exp), (8, rstd3), (6, weights)])
            send(1)
            stage5_pool(pool)

        @block.vector
        def _(v):
            nc.vector.memset(fill[:, 0:D], 0.0)
            nc.vector.memset(fill[:, D + 1:RW], 0.0).then_inc(s_zero, 1)
            nc.vector.memset(ones1[:, :], 1.0).then_inc(s_zero, 1)
            nc.vector.memset(onesb[:, :], 1.0).then_inc(s_zero, 1)
            nc.vector.memset(gm[:, G:G + 1, :], 0.0).then_inc(s_zero, 1)
            for T in (K, V):
                nc.vector.memset(T[:, 0:PAD * D], 0.0).then_inc(s_halo0, 1)
                nc.vector.memset(T[:, (NT + PAD) * D:(NT + 2 * PAD) * D], 0.0).then_inc(s_halo0, 1)
            v.wait_ge(s_const, 16)
            nc.vector.tensor_copy(tri[:, :], con[:, P:2 * P]).then_inc(s_zero, 1)
            nc.vector.tensor_copy(base[:, :], ebase).then_inc(s_zero, 1)
            def put(a):
                return nc.vector.tensor_copy(bo3[:, :, :], a.rearrange("p (o d) -> p o d", o=1)
                                             .to_broadcast([3, C, D]))

            nc.vector.memset(ones3[:, :], 1.0).then_inc(s_zero, 1)
            v.wait_ge(s_small, 16 * SMALL)
            put(bo_raw).then_inc(s_bo, 1)
            v.wait_ge(s_bo, 1)
            nc.vector.scalar_tensor_tensor(bo_mid, bo3[:, 0, :], later(0), bo_raw, ALU.mult,
                                           ALU.add).then_inc(s_bo, 1)
            v.wait_ge(s_bo, 2)
            put(bo_mid).then_inc(s_bo, 1)
            v.wait_ge(s_bo, 3)
            nc.vector.scalar_tensor_tensor(bo_low, bo3[:, 0, :], later(1), bo_mid, ALU.mult,
                                           ALU.add).then_inc(s_bo, 1)
            v.wait_ge(s_bo, 4)
            put(bo_low).then_inc(s_bo, 1)

            def ln1(i, n):
                r = slice(n * GROUP, (n + 1) * GROUP)
                v.wait_ge(s_x[n], 16)
                for t in range(n * GROUP, (n + 1) * GROUP):
                    nc.vector.bn_stats(st0[:, t:t + 1, :], xs[:, t * D:(t + 1) * D]) \
                      .then_inc(s_stat0, 1)
                v.wait_ge(s_stat0, GROUP * (i + 1))
                mean, dif, dsq, m2, var = (ln0[:, a, r] for a in range(5))
                col = [st0[:, r, a] for a in range(6)]
                nc.vector.tensor_tensor(mean, col[1], col[4], ALU.add).then_inc(s_mom0, 1)
                nc.vector.tensor_tensor(dif, col[1], col[4], ALU.subtract).then_inc(s_mom0, 1)
                nc.vector.tensor_tensor(m2, col[2], col[5], ALU.add).then_inc(s_mom0, 1)
                v.wait_ge(s_mom0, 7 * i + 3)
                nc.vector.tensor_tensor(dsq, dif, dif, ALU.mult).then_inc(s_mom0, 1)
                nc.vector.tensor_scalar(m2, m2, 1.0 / D, LN_EPS, ALU.mult, ALU.add) \
                  .then_inc(s_mom0, 1)
                v.wait_ge(s_mom0, 7 * i + 5)
                nc.vector.scalar_tensor_tensor(var, dsq, 0.25, m2, ALU.mult, ALU.add) \
                  .then_inc(s_mom0, 1)
                nc.vector.tensor_scalar(mean, mean, -0.5, None, ALU.mult).then_inc(s_mom0, 1)

            ln1(0, 3)
            ln1(1, 0)

            nc.vector.tensor_scalar(cn[:, 4, :], cn[:, 0, :], posn[0:WH, :], None,
                                    ALU.mult).then_inc(s_cn, 1)
            v.wait_ge(s_cn, 1)
            nc.vector.tensor_tensor(cn[:, 4, :], cn[:, 4, :], cn[:, 1, :], ALU.add).then_inc(s_cn, 1)
            v.wait_ge(s_cna, 1)
            nc.vector.tensor_tensor(cnw2[:, :, :], cnw2[:, :, :],
                                    cn[:, 5:6, :].to_broadcast([WH, J, J]), ALU.mult).then_inc(s_cn, 1)
            v.wait_ge(s_cn, 3)
            nc.vector.tensor_reduce(cn[:, 4, :], cnw2[:, :, :], AX.X, ALU.add).then_inc(s_cn, 1)
            v.wait_ge(s_cn, 4)
            nc.vector.tensor_tensor(cn[:, 4, :], cn[:, 4, :], cn[:, 2, :], ALU.add).then_inc(s_cn, 1)
            v.wait_ge(s_cna, 2)
            nc.vector.tensor_tensor(cn[:, 4, :], cn[:, 5, :], cn[:, 3, :], ALU.mult).then_inc(s_cn, 1)
            v.wait_ge(s_cn, 6)
            nc.vector.tensor_reduce(cnc[:, 1:2], cn[:, 4, :], AX.X, ALU.add).then_inc(s_cn, 1)
            v.wait_ge(s_cn, 7)
            nc.vector.tensor_tensor(cnc[:, 2:3], cnc[:, 1:2], cnc[:, 0:1], ALU.add).then_inc(s_cn, 1)
            v.wait_ge(s_cnp, 1)
            row = crow[:, 0, :]
            byh = lambda a: a.rearrange("p (w h) -> p h w", h=H)
            nc.vector.tensor_copy(row, psX2[0:1, 0:WH]).then_inc(s_cn, 1)
            v.wait_ge(s_cn, 9)
            nc.vector.tensor_reduce(csum[:, 0, :], byh(row), AX.X, ALU.max).then_inc(s_cn, 1)
            v.wait_ge(s_cn, 10)
            nc.vector.tensor_tensor(crow[:, 1, :].rearrange("p (w h) -> p w h", h=H),
                                    row.rearrange("p (w h) -> p w h", h=H),
                                    csum[:, 0:1, :].to_broadcast([1, WIN, H]),
                                    ALU.subtract).then_inc(s_cn, 1)
            v.wait_ge(s_cna, 3)
            nc.vector.tensor_reduce(csum[:, 1, :], byh(crow[:, 2, :]), AX.X, ALU.add).then_inc(s_cn, 1)
            v.wait_ge(s_cn, 12)
            nc.vector.reciprocal(csum[:, 2, :], csum[:, 1, :]).then_inc(s_cn, 1)
            v.wait_ge(s_cn, 13)
            nc.vector.tensor_tensor(crow[:, 1, :].rearrange("p (w h) -> p w h", h=H),
                                    crow[:, 2, :].rearrange("p (w h) -> p w h", h=H),
                                    csum[:, 2:3, :].to_broadcast([1, WIN, H]),
                                    ALU.mult).then_inc(s_cn, 1)
            v.wait_ge(s_cnp, 2)
            nc.vector.tensor_copy(conn[:, :], psL[:, 0:WH]).then_inc(s_cn, 1)
            v.wait_ge(s_cn, 15)
            ln1(2, 1)
            ln1(3, 2)

            v.wait_ge(s_halo, 16 * 4 * B)
            flat_c = lambda a: a.rearrange("p c d -> p (c d)")

            def scores(u, k):
                v.wait_ge(s_qkvs, u + 4)
                for c in range(C):
                    need(v, s_raw, C * u + c - 1)
                    nc.vector.tensor_tensor(
                        prod[:, c, :].rearrange("p (w d) -> p w d", w=WIN),
                        Q[:, ds(u * C + c, 1), 0:D]
                        .to_broadcast([P, WIN, D]),
                        K[:, ds((u * C + c) * D, WIN * D)].rearrange("p (w d) -> p w d", w=WIN),
                        ALU.mult).then_inc(s_prod, 1)
                for c in range(C):
                    v.wait_ge(s_prod, C * u + c + 1)
                    need(v, s_low, u)
                    nc.vector.tensor_reduce(raw[:, c, :], prod[:, c, :].rearrange(
                        "p (a d) -> p a d", d=DH), AX.X, ALU.add).then_inc(s_raw, 1)
                v.wait_ge(s_raw, C * u + C)
                nc.vector.tensor_reduce(top_s[:, :, :], raw[:, :, :].rearrange(
                    "p c (w h) -> p c h w", h=H), AX.X, ALU.max).then_inc(s_max, 1)
                v.wait_ge(s_max, u + 1)
                need(v, s_exp, u)
                nc.vector.tensor_tensor(
                    w_h(low_s[:, :, :]), w_h(raw[:, :, :]),
                    top_s[:, :, :].rearrange("p c (o h) -> p c o h", o=1)
                    .to_broadcast([P, C, WIN, H]), ALU.subtract).then_inc(s_low, 1)

            def sums(u, k):
                v.wait_ge(s_wt, u + 1)
                need(v, s_den, u)
                nc.vector.tensor_reduce(
                    zs[:, :, :, :].rearrange("p n c h -> p (n c) h"),
                    ew[:, :, :, :].rearrange("p n c (w h) -> p (n c) h w", h=H),
                    AX.X, ALU.add).then_inc(s_zs, 1)
                v.wait_ge(s_zs, u + 1)
                need(v, s_rden, u)
                nc.vector.scalar_tensor_tensor(flat_c(den[:, :, :]), flat_c(zs[:, 0]), 1e-9,
                                               flat_c(zs[:, 1]), ALU.mult,
                                               ALU.add).then_inc(s_den, 1)
                v.wait_ge(s_den, u + 1)
                need(v, s_fw, u)
                nc.vector.reciprocal(flat_c(rden[:, :, :]), flat_c(den[:, :, :])).then_inc(s_rden, 1)

            def values(u, k):
                for c in range(C):
                    weighted(v, nc.vector, u, c, PW, WIN).then_inc(s_wvd, 1)

            def moments(m, u, src, ready):
                for c in range(C):
                    ready(c)
                    nc.vector.bn_stats(lst[m][:, c, :], src(c)).then_inc(s_lst[m], 1)
                for c in range(C):
                    apart(v, (s_lnm[m], u),
                          (s_lst[m], C * u + c + 1))
                    nc.vector.bn_aggr(lmv[m][:, c, :], lst[m][:, c, :]).then_inc(s_lmv[m], 1)

            def stats2(u, k):
                def ready(c):
                    if c == 0:
                        need(v, s_lmv[0], C * u)
                        v.wait_ge(s_wo, u + 1)

                moments(0, u, lambda c: psY[:, c * D:(c + 1) * D], ready)

            def residual(u, k):
                v.wait_ge(s_xm, u + 1)
                v.wait_ge(s_lrs[0], u + 1)
                for c in range(C):
                    nc.vector.scalar_tensor_tensor(
                        xs[:, ds((u * C + c) * D, D)], psY[:, c * D:(c + 1) * D], lrs[0][:, c:c + 1],
                        xm[:, c, :], ALU.mult, ALU.add).then_inc(s_x1, 1)
                moments(1, u, lambda c: xs[:, ds((u * C + c) * D, D)],
                        lambda c: apart(v, (s_lmv[1], C * u), (s_x1, C * u + c + 1)))

            V_ = nc.vector
            each = lambda a: a.rearrange("p (t o) -> p t o", o=1).to_broadcast([P, G, E])
            per_t = lambda a: a.rearrange("p (o e) -> p o e", o=1).to_broadcast([P, G, E])
            col = lambda n: gsc[:, n, :]
            q_, e_, u_ = (a[:, :, :] for a in (gq, gp, gu))
            GS = 24

            class Chain:

                def __init__(self, u, at):
                    self.u, self.at = u, at

                def __call__(self, ins):
                    self.at += 1
                    ins.then_inc(s_g, 1)
                    v.wait_ge(s_g, (self.u - 1) * (GS // 2) + self.at)

            def gate_low(u, k):
                if k == 1:
                    gop = Chain(u, 0)
                    v.wait_ge(s_lgs, u + 1)
                    gop(V_.tensor_reduce(col(0), lgt[:, :, :], AX.X, ALU.max))
                    need(v, s_gexp, u - 1)
                    V_.tensor_tensor(gl[:, :, :], lgt[:, :, :], each(col(0)),
                                     ALU.subtract).then_inc(s_glow, 2)

            def gate_pick(u, k):
                if k != 1:
                    return
                gop = Chain(u, 1)
                v.wait_ge(s_gexp, u + 1)
                gop(V_.tensor_reduce(col(1), e_, AX.X, ALU.add))
                gop(V_.reciprocal(col(2), col(1)))
                src = e_
                for n in range(TOPK):
                    gop(V_.tensor_reduce(gtop[:, n, :], src, AX.X, ALU.max))
                    gop(V_.tensor_tensor(q_, src, each(gtop[:, n, :]), ALU.is_ge))
                    gop(V_.tensor_tensor(q_, q_, per_t(prior), ALU.mult))
                    gop(V_.tensor_reduce(col(3), q_, AX.X, ALU.max))
                    gop(V_.tensor_tensor(oh[:, n], q_, each(col(3)), ALU.is_equal))
                    if n == 0:
                        V_.tensor_copy(Q[:, ds(u * C - C, G), D + 1], col(3)).then_inc(s_first, 2)
                        gop(V_.scalar_tensor_tensor(u_, oh[:, 0], -2.0, e_, ALU.mult, ALU.add))
                        v.wait_ge(s_first, u + 1)
                        src = u_
                need(v, s_gcnt, u - 1)
                V_.tensor_tensor(gm[:, 0:G, :], oh[:, 0], oh[:, 1], ALU.add).then_inc(s_gmask, 2)

            def gate_place(u, k):
                if k != 1:
                    return
                gop = Chain(u, 14)
                gop(V_.tensor_tensor(gtop[:, :, :], gtop[:, :, :],
                                     gsc[:, 2:3, :].to_broadcast([P, TOPK, G]), ALU.mult))
                gop(V_.tensor_tensor(col(4), gtop[:, 0, :], gtop[:, 1, :], ALU.add))
                gop(V_.tensor_scalar(col(5), col(4), 1e-12, None, ALU.max))
                gop(V_.reciprocal(col(6), col(5)))
                gop(V_.tensor_tensor(gates[:, :, ds(u * C - C, G)], gtop[:, :, :],
                                     gsc[:, 6:7, :].to_broadcast([P, TOPK, G]), ALU.mult))
                v.wait_ge(s_gcnt, u + 1)
                gop(V_.tensor_tensor(gpos[:, :, :], psG[:, 0:G, :], per_t(base[:, :]), ALU.add))
                gop(V_.tensor_tensor(base[:, :], base[:, :], psG[:, G, :], ALU.add))
                gop(V_.tensor_tensor(ohp[:, 0], oh[:, 0], gpos[:, :, :], ALU.mult))
                gop(V_.tensor_tensor(ohp[:, 1], oh[:, 1], gpos[:, :, :], ALU.mult))
                gop(V_.tensor_reduce(slotf[:, :, :], ohp[:, :, :, :], AX.X, ALU.add))
                need(v, s_scat, 16 * G * (u - 1))
                assert gop.at == GS
                V_.tensor_copy(slots[:, :, :], slotf[:, :, :]).then_inc(s_slots, 2)

            run_steps(v, NU, [(8, stats2), (6, scores), (8, residual), (6, sums), (6, values),
                              (10, gate_low), (11, gate_place), (10, gate_pick)])

            step = [0]

            def jop(ins):
                step[0] += 1
                ins.then_inc(s_job, 1)
                v.wait_ge(s_job, step[0])

            n_, tl, tf, c_, o_ = (cnt[:, n, :] for n in range(5))
            jop(V_.tensor_copy(tails[:, :], base[0:1, :]))
            jop(V_.tensor_tensor(n_, base[:, :], ebase, ALU.subtract))
            jop(V_.tensor_scalar(n_, n_, float(P - 1), None, ALU.add))
            jop(V_.tensor_copy(cnti[:, :], n_))
            jop(V_.tensor_single_scalar(cnti[:, :], cnti[:, :], P.bit_length() - 1,
                                        ALU.logical_shift_right))
            jop(V_.tensor_copy(tl, cnti[:, :]))
            jop(V_.memset(o_, 1.0))
            jop(V_.tensor_tensor_scan(c_, o_, tl, 0.0, ALU.mult, ALU.add))
            jop(V_.tensor_scalar(tf, tl, float(-P), float(ROOM), ALU.mult, ALU.add))
            over_j = lambda a: a.rearrange("p (o e) -> p o e", o=1).to_broadcast([P, TILES, E])
            v.wait_ge(s_iota, 1)
            jop(V_.tensor_scalar(jota, past[:, :], 1.0 / P, None, ALU.mult))
            jop(V_.tensor_tensor(jcmp[:, :, :], over_j(c_),
                                 jota.rearrange("p (j o) -> p j o", o=1).to_broadcast([P, TILES, E]),
                                 ALU.is_le))
            jop(V_.tensor_reduce(jf[:, 0, :], jcmp[:, :, :], AX.X, ALU.add))
            jop(V_.tensor_tensor(jcm2[:, :, :], jcmp[:, :, :], over_j(tf), ALU.mult))
            jop(V_.tensor_reduce(jf[:, 1, :], jcm2[:, :, :], AX.X, ALU.add))
            jop(V_.scalar_tensor_tensor(jf[:, 2, :], jota, float(P), jf[:, 1, :],
                                        ALU.mult, ALU.add))
            jop(V_.tensor_scalar(jf[:, 0, :], jf[:, 0, :], float(E - 1), None, ALU.min))
            jop(V_.tensor_scalar(mark[:, :], jf[:, 0, :], -1.0, float(E), ALU.mult, ALU.add))
            jop(V_.tensor_copy(jobs[:, 0, :], jf[0:1, 0, :]))
            V_.tensor_copy(jobs[:, 1, :], jf[0:1, 2, :]).then_inc(s_jobs, 1)
            stage4_dve(v)

        @block.scalar
        def _(act):
            for dst, src in ((cn[:, 0, :], cw1.rearrange("h j a -> h (j a)")), (cn[:, 1, :], cb1),
                             (cnw2, cw2.rearrange("h j i -> h (j i)")), (cn[:, 2, :], cb2),
                             (cn[:, 3, :], cw3.rearrange("h a j -> h (a j)")), (cnc[:, 0:1], cb3)):
                if dst is cnw2:
                    dst = dst.rearrange("p j i -> p (j i)")
                for w in range(WIN):
                    nc.scalar.dma_start(dst[w * H:(w + 1) * H, :], src).then_inc(s_small, 16)
            for n in range(3):
                nc.scalar.dma_start(bo_raw[n:n + 1, :], bo.rearrange("(a d) -> a d", a=1)) \
                  .then_inc(s_small, 16)
            act.wait_ge(s_cn, 2)
            nc.scalar.activation(cn[:, 5, :], cn[:, 4, :], ACT.Gelu).then_inc(s_cna, 1)
            act.wait_ge(s_cn, 5)
            nc.scalar.activation(cn[:, 5, :], cn[:, 4, :], ACT.Gelu).then_inc(s_cna, 1)
            act.wait_ge(s_cn, 11)
            nc.scalar.activation(crow[:, 2, :], crow[:, 1, :], ACT.Exp).then_inc(s_cna, 1)

            def norm1(w, k):
                if isinstance(w, int):
                    t = w * C + C - 1 - PAD
                    act.wait_ge(s_nm0, 1 if t < 0 else min(t // GROUP + 2, 4))
                apart(act, (s_xTp, w))
                for c in range(C):
                    t = proj_step(w, c)
                    nc.scalar.activation(xn[:, c, :], xs[:, ds(t * D, D)], ACT.Identity,
                                         bias=ln0[:, 3, ds(t, 1)],
                                         scale=ln0[:, 5, ds(t, 1)]).then_inc(s_xn, 1)

            def evac_xT(w, k):
                act.wait_ge(s_xTp, w + 1)
                need(act, s_qkv, w)
                nc.scalar.copy(xnT[:, :, :, :].rearrange("p c k m -> p (c k m)"),
                               psX[:, :]).then_inc(s_xT, 1)

            def evac_qkv(w, k):
                act.wait_ge(s_qkv, w + 1)
                t = proj_step(w, 0)
                jumps = isinstance(w, int) and proj_step(w, C - 1) < t
                spans = [(0, 1), (1, C)] if jumps else [(0, C)]
                for a, b in spans:
                    t = proj_step(w, a)
                    nc.scalar.copy(Q[:, ds(t, b - a), 0:D],
                                   psQ[:, a * D:b * D].rearrange("p (c d) -> p c d", d=D))
                    for T, bank in ((K, psK), (V, psV)):
                        mv = nc.scalar.copy(T[:, ds((t + PAD) * D, (b - a) * D)], bank[:, a * D:b * D])
                mv.then_inc(s_qkvs, 4 if isinstance(w, int) and w == NU - 1 else 1)

            def expo(u, k):
                act.wait_ge(s_low, u + 1)
                need(act, s_zs, u)
                need(act, s_wt, u)
                nc.scalar.activation(ew[:, 0], low_s[:, :, :], ACT.Exp, scale=scale) \
                  .then_inc(s_exp, 1)

            def evac_attT(u, k):
                act.wait_ge(s_ws, C * u + C)
                need(act, s_wo, u)
                nc.scalar.copy(attT[:, :, :, :].rearrange("p k c m -> p (k c m)"),
                               psW[:, :]).then_inc(s_aT, 1)

            def shift_x(u, k):
                act.wait_ge(s_lnm[0], u + 1)
                need(act, s_x1, C * u)
                for c in range(C):
                    mv = nc.scalar.activation(xm[:, c, :], xs[:, ds((u * C + c) * D, D)],
                                              ACT.Identity, bias=lnm[0][:, c:c + 1])
                mv.then_inc(s_xm, 1)

            def norm3(u, k):
                apart(act, (s_x2p, u),
                      (s_keep, u), (s_lnm[1], u + 1))
                for c in range(C):
                    mv = nc.scalar.activation(xn2[:, c, :], xs[:, ds((u * C + c) * D, D)],
                                              ACT.Identity, bias=lnm[1][:, c:c + 1],
                                              scale=lrs[1][:, c:c + 1])
                mv.then_inc(s_xn2, 1)

            def keep(u, k):
                act.wait_ge(s_xn2, u + 1)
                nc.scalar.copy(Q[:, ds(u * C, C), 0:D], xn2[:, :, :]).then_inc(s_keep, 1)

            def gate_exp(u, k):
                if k == 1:
                    act.wait_ge(s_glow, u + 1)
                    need(act, s_first, u - 1)
                    nc.scalar.activation(gp[:, :, :], gl[:, :, :], ACT.Exp).then_inc(s_gexp, 2)

            def stage_rows(u, k):
                if k == 1:
                    act.wait_ge(s_first, u + 1)
                    act.wait_ge(s_keep, u + 1)
                    need(act, s_scat, 16 * G * (u - 1))
                    nc.scalar.copy(xr[:, :, :], Q[:, ds(u * C - C, G), :]).then_inc(s_rows, 2)

            def evac_x2T(u, k):
                act.wait_ge(s_x2p, u + 1)
                need(act, s_lg, u)
                nc.scalar.copy(x2T[:, :, :, :].rearrange("p c k m -> p (c k m)"),
                               psX[:, :]).then_inc(s_x2T, 1)

            def evac_logits(u, k):
                act.wait_ge(s_lg, u + 1)
                need(act, s_glow, u - k)
                nc.scalar.copy(lgt[:, k * C:(k + 1) * C, :].rearrange("p c e -> p (c e)"),
                               psL[:, 0:C * E]).then_inc(s_lgs, 1)

            act.wait_ge(s_cn, 15)
            run_steps(act, NU, [(2, evac_qkv), (9, norm3), (1, evac_xT), (8, shift_x), (7, evac_attT),
                                (9, evac_x2T), (6, expo), (9, evac_logits), (9, keep),
                                (10, gate_exp), (11, stage_rows), (0, norm1)])
            stage4_act(act)

        @block.tensor
        def _(pe):
            pe.wait_ge(s_const, 16)
            pe.wait_ge(s_zero, 7)

            def turn_x(w, k):
                pe.wait_ge(s_xn, C * w + C)
                need(pe, s_xT, w)
                need(pe, s_x2T, w - APART)
                for c in range(C):
                    mm = transposes(pe, xn[:, c, :], psX[:, c * D:(c + 1) * D], KC)
                mm.then_inc(s_xTp, 1)

            def qkv(w, k):
                pe.wait_ge(s_xT, w + 1)
                need(pe, s_qkvs, w)
                for n, bank in enumerate((psQ, psK, psV)):
                    for c in range(C):
                        for i in range(KC):
                            mm = nc.tensor.matmul(bank[:, c * D:(c + 1) * D], xnT[:, c, i, :],
                                                  wqkv[:, i, n * D:(n + 1) * D],
                                                  start=(i == 0), stop=(i == KC - 1))
                mm.then_inc(s_qkv, 1)

            def window_sum(u, k):
                need(pe, s_aT, u)
                for c in range(C):
                    pe.wait_ge(s_wvp, C * u + c + 1)
                    pe.wait_ge(s_wvd, C * u + c + 1)
                    for i in range(KC):
                        for w in range(WIN):
                            mm = nc.tensor.matmul(
                                psW[:, (i * C + c) * P:(i * C + c + 1) * P],
                                wval[:, c, w * D + i * P:w * D + (i + 1) * P], ident,
                                start=(w == 0), stop=(w == WIN - 1))
                    mm.then_inc(s_ws, 1)

            def out_product(u, k):
                pe.wait_ge(s_aT, u + 1)
                need(pe, s_x1, C * u)
                nc.tensor.matmul(psY[:, :], ones3[:, :], bo3[:, :, :].rearrange("p c d -> p (c d)"),
                                 start=True, stop=False)
                for c in range(C):
                    for i in range(KC):
                        mm = nc.tensor.matmul(psY[:, c * D:(c + 1) * D], attT[:, i, c, :], wo[:, i, :],
                                              start=False, stop=(c == C - 1 and i == KC - 1))
                mm.then_inc(s_wo, 1)

            def turn_x2(u, k):
                pe.wait_ge(s_xn2, u + 1)
                need(pe, s_x2T, u)
                pe.wait_ge(s_xT, min(u + APART + 1, NU) if isinstance(u, int) else u + APART + 1)
                for c in range(C):
                    mm = transposes(pe, xn2[:, c, :], psX[:, c * D:(c + 1) * D], KC)
                mm.then_inc(s_x2p, 1)

            def logits(u, k):
                pe.wait_ge(s_x2T, u + 1)
                need(pe, s_lgs, u)
                for c in range(C):
                    for i in range(KC):
                        mm = nc.tensor.matmul(psL[:, c * E:(c + 1) * E], x2T[:, c, i, :],
                                              gatew[:, i, :], start=(i == 0), stop=(i == KC - 1))
                mm.then_inc(s_lg, 1)

            pe.wait_ge(s_cn, 8)
            nc.tensor.matmul(psX2[0:1, 0:WH], cnc[:, 2:3], ident[0:WH, 0:WH], start=True,
                             stop=True).then_inc(s_cnp, 1)
            pe.wait_ge(s_cn, 14)
            nc.tensor.matmul(psL[:, 0:WH], ones1[:, :], crow[:, 1, :], start=True,
                             stop=True).then_inc(s_cnp, 1)
            pe.wait_ge(s_w, 48)
            pe.wait_ge(s_bo, 5)
            def count_pairs(u, k):
                if k == 1:
                    pe.wait_ge(s_gmask, u + 1)
                    need(pe, s_slots, u - 1)
                    nc.tensor.matmul(psG[:, :, :], tri[:, :], gm[:, :, :], start=True, stop=False)
                    for t in range(G):
                        mm = nc.tensor.matmul(psG[:, t + 1:G + 1, :], onesb[:, :],
                                              gm[:, t:t + 1, :].to_broadcast([P, G - t, E]),
                                              start=False, stop=(t == G - 1))
                    mm.then_inc(s_gcnt, 2)

            APART = 8
            run_steps(pe, NU, [(1, turn_x), (7, window_sum), (9, turn_x2), (7, out_product),
                               (9, logits), (1, qkv), (10, count_pairs)])

            stage4_pe(pe)


def kernel(L0_attn_x, L0_attn_wq, L0_attn_wk, L0_attn_wv, L0_attn_wo, L0_attn_bo, L0_attn_cw1, L0_attn_cb1,
           L0_attn_cw2, L0_attn_cb2, L0_attn_cw3, L0_attn_cb3, L0_ffn_gate, L0_ffn_W1, L0_ffn_b1,
           L0_ffn_W2, L0_ffn_b2):
    import numpy as np
    import concourse.bacc as bacc
    from concourse.bass_utils import run_bass_kernel_spmd

    wqkvT = np.concatenate([np.asarray(w).T for w in (L0_attn_wq, L0_attn_wk, L0_attn_wv)], axis=1)
    H, E, N = L0_attn_cw1.shape[0], L0_ffn_W1.shape[0], L0_attn_x.shape[0] * L0_attn_x.shape[1]
    p = np.arange(P)
    consts = np.zeros((P, 3 * P + 8 + E), np.float32)
    consts[:, 0:P] = np.eye(P)
    consts[:, P:2 * P] = p[:, None] < p[None, :]
    consts[:, 2 * P:2 * P + E] = E - np.arange(E)
    consts[:, 2 * P + E:2 * P + 2 * E] = np.arange(E) * (N + P)
    consts[:, 3 * P] = -0.5
    consts[:, 3 * P + 1] = -1.0
    consts[:, 3 * P + 5] = -1.0 * (p >= 1)
    consts[:, 3 * P + 6] = -1.0 * (p >= 2)
    consts[:, 3 * P + 7] = 1e-5
    consts[:, 3 * P + 2] = np.linspace(0.0, 1.0, 7, dtype=np.float32)[np.minimum(p // H, 6)]
    consts[:, 3 * P + 3] = -1.0 * (p >= E)
    consts[:, 3 * P + 4] = -1.0 * (p >= 2 * E)
    consts[:, 3 * P + 8:] = (p[:, None] % E == np.arange(E)) & (p[:, None] < 3 * E)
    arrays = {
        "x": L0_attn_x, "wqkvT": wqkvT, "woT": np.asarray(L0_attn_wo).T, "bo": L0_attn_bo,
        "cw1": L0_attn_cw1, "cb1": L0_attn_cb1, "cw2": L0_attn_cw2, "cb2": L0_attn_cb2,
        "cw3": L0_attn_cw3, "cb3": L0_attn_cb3, "gate": L0_ffn_gate, "w1": L0_ffn_W1,
        "b1": L0_ffn_b1, "w2": L0_ffn_W2, "b2": L0_ffn_b2, "consts": consts,
    }
    arrays = {f"in_{n}": np.ascontiguousarray(a) for n, a in arrays.items()}
    nc = bacc.Bacc("TRN2", target_bir_lowering=False, num_devices=1)
    args = [nc.dram_tensor(n, a.shape, mybir.dt.from_np(a.dtype), kind="ExternalInput").ap()
            for n, a in arrays.items()]
    out = nc.dram_tensor("out_x", L0_attn_x.shape, F32, kind="ExternalOutput").ap()
    build(nc, *args, out)
    r = run_bass_kernel_spmd(nc, [arrays], core_ids=[0])
    return r.results[0]["out_x"]
```

```python
from contextlib import ExitStack

import concourse.bass as bass
from concourse import mybir

F32 = mybir.dt.float32
F32R = mybir.dt.float32r
BF16 = mybir.dt.bfloat16
I32 = mybir.dt.int32
ALU = mybir.AluOpType
ACT = mybir.ActivationFunctionType
AX = mybir.AxisListType

P = 128
ds = bass.ds


def even_up(n):
    return n + n % 2


def need(eng, sem, count):
    if isinstance(count, int) and count <= 0:
        return
    eng.wait_ge(sem, count)


def run_steps(eng, n, stages, unroll=2, reuse=2):
    first = min(lag for lag, _ in stages)
    stages = [(lag - first, stage) for lag, stage in stages]
    most = max(lag for lag, _ in stages)

    def step(t, at, edge):
        for lag, stage in stages:
            if not edge or 0 <= t - lag < n:
                stage(t - lag, (at - lag) % unroll)

    start = -(-(most + reuse) // unroll) * unroll
    turns = max(0, (n - start) // unroll)
    if turns < 2:
        start, turns = n + most, 0
    for t in range(start):
        step(t, t % unroll, True)
    if turns:
        with eng.Fori(0, turns) as i:
            for at in range(unroll):
                step(unroll * i + (start + at), at, False)
        for t in range(start + unroll * turns, n + most):
            step(t, t % unroll, True)


def build(nc, x, wqkvT, woT, bo, cw1, cb1, cw2, cb2, cw3, cb3, gate, w1, b1, w2, b2, consts, out):
    B, L, D = x.shape
    N = B * L
    NT = N // P
    H = cw1.shape[0]
    DH = D // H
    J = cw1.shape[1]
    WIN = 7
    PAD = WIN // 2
    WH = WIN * H
    KC = D // P
    E, _, F = w1.shape
    FC = F // P
    TOPK = E // 4
    ROOM = N + P
    TILES = N * TOPK // P + E - 1
    SPARE = (E - 1) * P
    EW = KC * F
    assert EW == FC * D and N == P * NT and L % NT == 0
    SEQP = L // NT
    LN_EPS = 1e-5
    scale = float(DH) ** -0.5
    C = 2
    NU = NT // C
    GROUP = NT // 4
    PW = 6
    G = 2 * C
    CODED = 5
    RW = D + 2
    LATE = NT - PAD

    rows_in = nc.dram_tensor("rows_in", [E * ROOM + SPARE, RW], F32, kind="Internal").ap()
    rows_back = nc.dram_tensor("rows_back", [TOPK * N + (TILES + 1) * P, D], F32, kind="Internal").ap()

    with ExitStack() as top:
        def sem(name):
            return top.enter_context(nc.semaphore(name))

        def sb(ctx, name, shape, dt=F32):
            return ctx.enter_context(nc.sbuf_tensor(name, shape, dt))

        def psum(ctx, name, shape, dt=F32):
            return ctx.enter_context(nc.psum_tensor(name, shape, dt))

        xs = sb(top, "xs", [P, NT * D])
        con = sb(top, "con", [P, 3 * P + 8 + E])
        ident = con[:, 0:P]
        halves = con[:, 3 * P:3 * P + 1]
        later = lambda n: con[0:3, 3 * P + 5 + n:3 * P + 6 + n]
        epss = con[:, 3 * P + 7:3 * P + 8]
        minus = con[:, 3 * P + 1:3 * P + 2]
        posn = con[:, 3 * P + 2:3 * P + 3]
        gates = sb(top, "gates", [P, TOPK, NT])
        jobs = sb(top, "jobs", [1, 3, TILES], I32)
        mark = sb(top, "mark", [P, TILES])
        past = sb(top, "past", [P, TILES])
        tails = sb(top, "tails", [1, E], I32)
        fill = sb(top, "fill", [P, RW])

        s_const = sem("const_loaded")
        s_small = sem("small_loaded")

        def apart(eng, *waits):
            waits = [(s, n if isinstance(n, int) else eng.to_reg(n)) for s, n in waits]
            eng.wait_ge(s_const, 16)
            for s, n in waits:
                need(eng, s, n)
        s_x = [sem(f"x_loaded{n}") for n in range(4)]
        s_wq = sem("projection_weights_loaded")
        s_w = sem("attn_weights_loaded")

        ctx = ExitStack()
        Q = sb(ctx, "Q", [P, NT, RW])
        K = sb(ctx, "K", [P, (NT + 2 * PAD) * D])
        V = sb(ctx, "V", [P, (NT + 2 * PAD) * D])
        prod = sb(ctx, "prod", [P, C, WIN * D])
        wval = sb(ctx, "wval", [P, C, WIN * D])
        wqkv = sb(ctx, "wqkv", [P, KC, 3 * D])
        wo = sb(ctx, "wo", [P, KC, D])
        bo3 = sb(ctx, "bo3", [3, C, D], BF16)
        ones3 = sb(ctx, "ones3", [3, P], BF16)
        ones1 = sb(ctx, "ones1", [1, P])
        gatew = sb(ctx, "gatew", [P, KC, E])
        ln0 = sb(ctx, "ln0", [P, 2, NT])
        early = sb(ctx, "early", [P, 2 * C * D + WH])
        xn = early[:, 0:C * D].rearrange("p (c d) -> p c d", d=D)
        xnT = early[:, C * D:2 * C * D].rearrange("p (c k m) -> p c k m", c=C, m=P)
        conn = early[:, 2 * C * D:]
        raw = sb(ctx, "raw", [P, C, WH])
        low_s = sb(ctx, "low_s", [P, C, WH])
        ew = sb(ctx, "ew", [P, 2, C, WH])
        fw = sb(ctx, "fw", [P, C, WH])
        top_s = sb(ctx, "top_s", [P, C, H])
        zs = sb(ctx, "zs", [P, 2, C, H])
        den = sb(ctx, "den", [P, C, H])
        rden = sb(ctx, "rden", [P, C, H])
        attT = sb(ctx, "attT", [P, KC, C, P])
        xm = sb(ctx, "xm", [P, C, D])
        xn2 = sb(ctx, "xn2", [P, C, D])
        x2T = sb(ctx, "x2T", [P, C, KC, P])
        lst, lmv, lve, lneg, lrs, lnm = ([sb(ctx, f"ln{m + 2}_{n}", [P, C] + w) for m in range(2)]
                                         for n, w in (("stats", [6]), ("moments", [2]), ("var", []),
                                                      ("neg_mean", []), ("rstd", []), ("shift", [])))
        xr = sb(ctx, "xr", [P, G, RW])
        xr_last = early[:, 0:G * RW].rearrange("p (t r) -> p t r", r=RW)
        lend = [prod[:, :, :].rearrange("p c d -> p (c d)"), 0]

        def carve(rows, *shape):
            n = 1
            for m in shape:
                n *= m
            flat, at = lend
            lend[1] += n
            assert lend[1] <= flat.shape[1]
            v = flat[0:rows, at:at + n]
            return v if len(shape) == 1 else v.rearrange("p (a b) -> p a b", b=shape[1])

        st0 = wval[:, 0, 0:6 * NT].rearrange("p (t n) -> p t n", n=6)
        ln1s = wval[:, 1, 0:5 * NT].rearrange("p (n t) -> p n t", t=NT)
        cn = carve(WH, 6, J)
        cnw2 = carve(WH, J, J)
        cnc = carve(WH, 4)
        crow = carve(1, 3, WH)
        csum = carve(1, 4, H)
        bo_raw, bo_mid, bo_low = (carve(3, D) for _ in range(3))

        psT = [psum(top, f"psT{n}", [P, 512]) for n in range(2)]
        psA = [psum(top, f"psA{n}", [P, 512]) for n in range(2)]
        psB = [psum(top, f"psB{n}", [P, 512]) for n in range(2)]
        psC = [psum(top, f"psC{n}", [P, 512]) for n in range(2)]

        psQ, psK, psV, psW = psA[0], psA[1], psC[0], psC[1]
        psY, psL, psX, psX2 = psB[0], psB[1], psT[0], psT[1]
        psG = psX2[:, 0:(G + 1) * E].rearrange("p (t e) -> p t e", e=E)
        s_zero = sem("zeros_set")
        s_stat0 = sem("ln1_stats")
        s_mom0 = sem("ln1_moments")
        s_rstd0 = sem("ln1_rstd")
        s_xn = sem("xn_ready")
        s_xTp = sem("xn_transposed")
        s_xT = sem("xnT_ready")
        s_qkv = sem("qkv_done")
        s_qkvs = sem("qkv_stored")
        s_halo0 = sem("halo_zeroed")
        s_halo = [sem(f"halo_shifted{n}") for n in range(2)]
        s_cn = sem("connectivity_step")
        s_cna = sem("connectivity_gelu")
        s_cnp = sem("connectivity_pe")
        (s_prod, s_raw, s_max, s_low, s_exp, s_wt, s_zs, s_den, s_rden, s_fw, s_wvp, s_wvd, s_ws, s_aT,
         s_wo) = (sem(n) for n in (
             "products_ready", "raw_scores_ready", "score_max_ready", "lowered_scores_ready",
             "exp_ready", "weighted_exp_ready", "sums_ready", "denominator_ready",
             "reciprocal_ready", "weights_ready", "weighted_values_gpsimd",
             "weighted_values_vector", "window_summed", "attnT_ready", "out_product_done"))
        s_lst, s_lmv, s_lve, s_lrs, s_lnm, s_lneg = (
            [sem(f"ln{m + 2}_{n}") for m in range(2)]
            for n in ("stats", "moments", "var_eps", "rstd", "shift", "neg_mean"))
        (s_xm, s_x1, s_xn2, s_x2p, s_x2T, s_lg, s_lgs, s_keep, s_nm0, s_bo) = (sem(n) for n in (
            "x_shifted", "x1_ready", "xn2_ready", "xn2_transposed", "x2T_ready", "logits_done",
            "logits_stored", "xn2_kept", "ln1_shift", "out_bias_split"))

        lgt = sb(ctx, "lgt", [P, NT, E])
        gmax = sb(ctx, "gmax", [P, 2, NT])
        gl = sb(ctx, "gl", [P, G, E])
        gq = sb(ctx, "gq", [P, G, E])
        gu = sb(ctx, "gu", [P, G, E])
        gsc = sb(ctx, "gsc", [P, 2, G])
        oh = sb(ctx, "oh", [P, TOPK, G, E])
        ohp = sb(ctx, "ohp", [P, TOPK, G, E])
        gm = sb(ctx, "gm", [P, G + 1, E], BF16)
        tri = sb(ctx, "tri", [P, P], BF16)
        onesb = sb(ctx, "onesb", [P, P], BF16)
        gpos = sb(ctx, "gpos", [P, G, E])
        base = sb(ctx, "base", [P, E])
        slotf = sb(ctx, "slotf", [P, TOPK, G])
        slots = sb(ctx, "slots", [P, 2, TOPK, G], I32)
        lend = [V[:, :], NT * D + F + D]
        gw = carve(P, 5, NT)
        cnt = carve(P, 6, E)
        at = NT * D + (F + D + E * P) // 2
        jcmp = K[:, at:at + TILES * E].rearrange("p (j e) -> p j e", e=E)
        jf = carve(P, 3, TILES)
        ones_e = cnt[:, 4, :]
        cnti = sb(ctx, "cnti", [P, E], I32)
        prior = con[:, P * 2:P * 2 + E]
        ebase = con[:, P * 2 + E:P * 2 + 2 * E]
        (s_glow, s_gexp, s_g, s_gmask, s_gcnt, s_slots, s_first, s_rows) = (sem(n) for n in (
            "gate_lowered", "gate_exp", "gate_step", "gate_masks", "pairs_counted", "slots_ready",
            "first_experts_kept", "rows_staged"))
        (s_jobs, s_job, s_spare, s_scat, s_iota) = (sem(n) for n in (
            "jobs_ready", "job_step", "spare_filled", "rows_scattered",
            "numbers_set"))

        s_tail = [sem(f"tails_filled{n}") for n in range(2)]
        s_wlast = sem("last_expert_weights_loaded1")
        s_wraw = [sem(f"expert_weights_loaded{n}") for n in range(2)]
        s_whi = [sem(f"weights_high{n}") for n in range(2)]
        s_wlo = [sem(f"weights_low{n}") for n in range(2)]
        s_bias = sem("bias_step")
        s_braw = sem("biases_loaded")
        s_xg = [sem(f"tile_rows_loaded{n}") for n in range(4)]
        s_xoff, s_xid = sem("tile_id_step"), sem("tile_ids")
        s_xgp = sem("tile_transposed")
        s_xgh = sem("tile_high")
        s_xgl = sem("tile_low")
        s_h = sem("hidden_done")
        s_hr = sem("hidden_relu")
        s_hTp = sem("hidden_transposed")
        s_hTh = sem("hiddenT_high")
        s_hTl = sem("hiddenT_low")
        s_y = sem("tile_out_done")
        s_ys = sem("tile_out_copied")
        s_yst = [sem(f"tile_out_scattered{n}") for n in range(4)]
        s_yp = [sem(f"results_loaded{n}") for n in range(8)]
        (s_o1, s_o2, s_st4, s_mv4, s_ve4, s_rs4, s_neg4, s_nm4, s_nrm, s_fin) = (sem(n) for n in (
            "first_weighed", "results_added", "ln4_stats", "ln4_moments", "ln4_var_eps",
            "ln4_rstd", "ln4_neg_mean", "ln4_shift", "ln4_normed", "final_ready"))
        s_out = [sem(f"out_stored{n}") for n in range(4)]

        ctx.close()
        ctx = ExitStack()
        w1h = sb(ctx, "w1h", [P, E * EW], F32R)
        sb(ctx, "gap_q", [P, NT * RW - E * EW])
        alias = ExitStack()
        halo = 2 * PAD * D
        w1r = sb(alias, "w1r", [P, E * EW])
        sb(alias, "gap_kr", [P, halo])
        w2r = sb(alias, "w2r", [P, E * EW])
        alias.close()
        w1l = sb(ctx, "w1l", [P, E * EW], F32R)
        bias = sb(ctx, "bias", [P, F + D], BF16)
        sel = sb(ctx, "sel", [P, E * P], BF16)
        used = (F + D + E * P) // 2
        sb(ctx, "gap_k", [P, halo - used])
        alias = ExitStack()
        sb(alias, "skip_v", [P, E * EW])
        braw = sb(alias, "braw", [3 * E, F + D])
        alias.close()
        w2l = sb(ctx, "w2l", [P, E * EW], F32R)
        sb(ctx, "gap_v", [P, halo])
        w2h = sb(ctx, "w2h", [P, E * EW], F32R)
        xg = sb(ctx, "xg", [P, 4, RW])
        xoff = sb(ctx, "xoff", [P, 3])
        xid = sb(ctx, "xid", [P, 4], I32)
        xgh = sb(ctx, "xgh", [P, 2, KC, P], F32R)
        xgl = sb(ctx, "xgl", [P, 2, KC, P], F32R)
        ysb = sb(ctx, "ysb", [P, 4, D])
        hr = sb(ctx, "hr", [P, 2, F])
        hTh = sb(ctx, "hTh", [P, 2, FC, P], F32R)
        hTl = sb(ctx, "hTl", [P, 2, FC, P], F32R)
        ctx.close()
        M = 4
        yp = sb(top, "yp", [P, TOPK, NT * D])
        moe = sb(top, "moe", [P, 4, M * D])
        nrm = sb(top, "nrm", [P, 2, M * D])
        fin = sb(top, "fin", [P, 4, M * D])
        st4 = sb(top, "st4", [P, 2, M, 6])
        mv4 = sb(top, "mv4", [P, 2, M, 2])
        ve4, neg4, rs4, nm4 = (sb(top, n, [P, 2, M]) for n in ("ve4", "neg4", "rs4", "nm4"))

        xv = x.rearrange("b (q t) d -> (b q) (t d)", t=NT)
        ov = out.rearrange("b (q t) d -> (b q) (t d)", t=NT)

        w1v = w1.rearrange("e (c p) f -> p e c f", p=P)
        w2v = w2.rearrange("e (c p) d -> p e c d", p=P)
        parts = ((w1v, w1r, w1h, w1l), (w2v, w2r, w2h, w2l))

        def experts(eng, body):
            for part in range(2):
                body(0, part)
            with eng.Fori(1, E - 1) as e:
                for part in range(2):
                    body(e, part)
            for part in range(2):
                body(E - 1, part)

        def end_lists(eng, tail, lo, hi):
            for e in range(lo, hi):
                first = eng.value_load(tails[0:1, e:e + 1], min_val=0, max_val=E * ROOM - P)
                eng.dma_start(rows_in[ds(first, P), :], fill[:, :]).then_inc(tail, 16)

        def stage4_sp(sp):
            def load_w(e, part):
                if part == 0:
                    apart(sp, (s_prod, G * e + G), (s_wraw[0], 16 * e))
                else:
                    apart(sp, (s_wvp, G * e + G), (s_wvd, G * e + G))
                src, raw_w = parts[part][0:2]
                sp.dma_start(raw_w[:, ds(e * EW, EW)].rearrange("p (e c f) -> p e c f", e=1,
                                                                c=src.shape[2]),
                             src[:, ds(e, 1)]).then_inc(s_wlast if isinstance(e, int) and
                                                        e + part == E else s_wraw[part], 16)

            for n in range(2):
                sp.wait_ge(s_halo[n], 16 * 2 * B)
            experts(sp, load_w)
            for n in range(3):
                r = slice(n * E, (n + 1) * E)
                sp.dma_start(braw[r, 0:F], b1).then_inc(s_braw, 16)
                sp.dma_start(braw[r, F:F + D], b2).then_inc(s_braw, 16)
            sp.wait_ge(s_job, 1)
            end_lists(sp, s_tail[0], 0, E // 2)
            sp.wait_ge(s_jobs, 1)
            sp.wait_ge(s_scat, 16 * TOPK * NT)
            sp.wait_ge(s_spare, 16 * (E - 1))
            for n in range(2):
                sp.wait_ge(s_tail[n], 16 * (E // 2))

            def load_rows(j, k):
                need(sp, s_xgp, j - 3)
                need(sp, s_xid, j - 3)
                first = sp.value_load(jobs[0:1, 1, ds(j, 1)], min_val=0,
                                      max_val=E * ROOM + SPARE - P)
                sp.dma_start(xg[:, k, :], rows_in[ds(first, P), :]).then_inc(s_xg[k], 16)

            run_steps(sp, TILES, [(0, load_rows)], 4, 4)

            for k in range(4):
                sp.wait_ge(s_yst[k], 16 * ((TILES + 3 - k) // 4))
            back = rows_back[0:TOPK * N, :].rearrange("(k p t) d -> k p (t d)", k=TOPK, t=NT)

            for q in range(NT // M):
                for n in range(TOPK):
                    cols = slice(q * M * D, (q + 1) * M * D)
                    sp.dma_start(yp[:, n, cols], back[n, :, cols]).then_inc(s_yp[q], 16)

            def store_out(q, k):
                sp.wait_ge(s_fin, q + 1)
                sp.dma_start(ov[:, ds(q * M * D, M * D)], fin[:, k, :]).then_inc(s_out[k], 16)

            run_steps(sp, NT // M, [(0, store_out)], 4, 4)
            for k in range(4):
                sp.wait_ge(s_out[k], 16 * NT // M // 4)

        def stage4_act(act):
            def rows_high(j, k):
                act.wait_ge(s_xgp, j + 1)
                need(act, s_h, j - 1)
                k = k % 2
                nc.scalar.copy(xgh[:, k, :, :], psT[k][:, 0:D].rearrange("p (c m) -> p c m", c=KC)) \
                  .then_inc(s_xgh, 1)

            def hidden_high(j, k):
                act.wait_ge(s_hTp, j + 1)
                need(act, s_y, j - 1)
                k = k % 2
                nc.scalar.copy(hTh[:, k, :, :], psB[k][:, :].rearrange("p (c m) -> p c m", c=FC)) \
                  .then_inc(s_hTh, 1)

            def relu(j, k):
                act.wait_ge(s_h, j + 1)
                need(act, s_hTp, j - 1)
                k = k % 2
                nc.scalar.activation(hr[:, k, :], psA[k][:, 0:F], ACT.Relu).then_inc(s_hr, 1)

            run_steps(act, TILES, [(0, rows_high), (2, hidden_high), (1, relu)], 4)

            def norm4(q, k):
                act.wait_ge(s_nm4, q + 1)
                need(act, s_fin, q - 1)
                for m in range(M):
                    mv = nc.scalar.activation(nrm[:, k % 2, m * D:(m + 1) * D],
                                              moe[:, k % 4, m * D:(m + 1) * D], ACT.Identity,
                                              bias=nm4[:, k % 2, m:m + 1],
                                              scale=rs4[:, k % 2, m:m + 1])
                mv.then_inc(s_nrm, 1)

            def weigh(q, k):
                act.wait_ge(s_yp[k], 32)
                need(act, s_nrm, q - 3)
                for m in range(M):
                    t = q * M + m
                    nc.scalar.activation(moe[:, k % 4, m * D:(m + 1) * D], yp[:, 0, ds(t * D, D)],
                                         ACT.Identity, scale=gates[:, 0, ds(t, 1)]).then_inc(s_o1, 1)

            run_steps(act, NT // M, [(0, weigh), (2, norm4)], 8)

        def finish_unit(eng, eng_, q, k):
            need(eng, s_out[k], 4 * (q - k))
            eng_.tensor_tensor(fin[:, k, :], nrm[:, k % 2, :], xs[:, ds(q * M * D, M * D)],
                               ALU.add).then_inc(s_fin, 1)

        def stage4_dve(v, weights_of):
            def weights(j, k):
                if isinstance(j, int) and j == 3:
                    weights_of()

            def rows_low(j, k):
                v.wait_ge(s_xgh, j + 1)
                k2 = k % 2
                nc.vector.tensor_tensor(xgl[:, k2, :, :].rearrange("p c m -> p (c m)"), psT[k2][:, 0:D],
                                        xgh[:, k2, :, :].bitcast(F32).rearrange("p c m -> p (c m)"),
                                        ALU.subtract).then_inc(s_xgl, 1)

            def number(j, k):
                v.wait_ge(s_xg[k], 4 * (j - k) + 16)
                need(v, s_xid, j)
                w = xg[:, k, D + 1:D + 2]
                nc.vector.tensor_tensor(xoff[:, 0:1], w, mark[:, ds(j, 1)],
                                        ALU.not_equal).then_inc(s_xoff, 1)
                nc.vector.scalar_tensor_tensor(xoff[:, 1:2], w, 0.0, past[:, ds(j, 1)], ALU.is_equal,
                                               ALU.mult).then_inc(s_xoff, 1)
                apart(v, (s_xoff, 3 * j + 2))
                nc.vector.scalar_tensor_tensor(xoff[:, 2:3], xoff[:, 0:1], float(N), xoff[:, 1:2],
                                               ALU.mult, ALU.add).then_inc(s_xoff, 1)
                apart(v, (s_xoff, 3 * j + 3),
                      (s_yst[k], 4 * (j - k)))
                nc.vector.tensor_tensor(xid[:, k:k + 1], xoff[:, 2:3], xg[:, k, D:D + 1],
                                        ALU.add).then_inc(s_xid, 1)

            def hidden_low(j, k):
                v.wait_ge(s_hTh, j + 1)
                k = k % 2
                nc.vector.tensor_tensor(hTl[:, k, :, :].rearrange("p c m -> p (c m)"), psB[k][:, :],
                                        hTh[:, k, :, :].bitcast(F32).rearrange("p c m -> p (c m)"),
                                        ALU.subtract).then_inc(s_hTl, 1)

            def copy_out(j, k):
                v.wait_ge(s_y, j + 1)
                need(v, s_yst[k], 4 * (j - k))
                nc.vector.tensor_copy(ysb[:, k, :], psC[k % 2][:, 0:D]).then_inc(s_ys, 1)

            run_steps(v, TILES, [(0, rows_low), (2, hidden_low), (3, copy_out), (1, number), (1, weights)],
                      4, 4)

            def combine(q, k):
                a, b = k % 4, k % 2
                for m in range(M):
                    v.wait_ge(s_o1, q * M + m + 1)
                    nc.vector.scalar_tensor_tensor(
                        moe[:, a, m * D:(m + 1) * D], yp[:, 1, ds((q * M + m) * D, D)],
                        gates[:, 1, ds(q * M + m, 1)], moe[:, a, m * D:(m + 1) * D],
                        ALU.mult, ALU.add).then_inc(s_o2, 1)
                for m in range(M):
                    apart(v, (s_mv4, q * M - M),
                          (s_o2, q * M + m + 1))
                    nc.vector.bn_stats(st4[:, b, m, :], moe[:, a, m * D:(m + 1) * D]) \
                      .then_inc(s_st4, 1)
                apart(v, (s_nm4, q - 1),
                      (s_st4, q * M + M))
                for m in range(M):
                    nc.vector.bn_aggr(mv4[:, b, m, :], st4[:, b, m, :]).then_inc(s_mv4, 1)

            run_steps(v, NT // M, [(0, combine)], 8)
            for q in range(NT // M - 2, NT // M):
                v.wait_ge(s_nrm, q + 1)
                v.wait_ge(s_fin, q)
                finish_unit(v, nc.vector, q, q % 4)

        def stage5_pool(pool):
            def scatter_back(j, k):
                apart(pool, (s_xid, j + 1), (s_ys, j + 1))
                nc.gpsimd.indirect_dma_start(
                    rows_back, bass.IndirectOffsetOnAxis(ap=xid[:, k:k + 1], axis=0),
                    ysb[:, k, :], None).then_inc(s_yst[k], 16)

            run_steps(pool, TILES, [(0, scatter_back)], 4)

            def rstd4(q, k):
                pair = lambda a: a.to_broadcast([P, M])
                k = k % 2
                pool.wait_ge(s_mv4, M * q + M)
                need(pool, s_nm4, q - 1)
                nc.gpsimd.tensor_tensor(ve4[:, k], mv4[:, k, :, 1], pair(epss), ALU.add) \
                  .then_inc(s_ve4, 1)
                nc.gpsimd.tensor_tensor(neg4[:, k], mv4[:, k, :, 0], pair(minus), ALU.mult) \
                  .then_inc(s_neg4, 1)
                pool.wait_ge(s_ve4, q + 1)
                need(pool, s_nrm, q - 1)
                nc.gpsimd.tensor_tensor(rs4[:, k], ve4[:, k], pair(halves), ALU.pow) \
                  .then_inc(s_rs4, 1)
                pool.wait_ge(s_neg4, q + 1)
                pool.wait_ge(s_rs4, q + 1)
                nc.gpsimd.tensor_tensor(nm4[:, k], neg4[:, k], rs4[:, k], ALU.mult) \
                  .then_inc(s_nm4, 1)

            def finish(q, k):
                if q < NT // M - 2:
                    pool.wait_ge(s_nrm, q + 1)
                    finish_unit(pool, nc.gpsimd, q, k)

            run_steps(pool, NT // M, [(0, rstd4), (1, finish)], 4, 4)

        def stage4_pe(pe):
            pe.wait_ge(s_jobs, 2)
            pe.wait_ge(s_wlo[0], NU)
            pe.wait_ge(s_wlo[1], E)
            pe.wait_ge(s_bias, 7)

            def turn_rows(j, k):
                pe.wait_ge(s_xg[k], 4 * (j - k) + 16)
                need(pe, s_xgl, j - 1)
                transposes(pe, xg[:, k, :], psT[k % 2], KC).then_inc(s_xgp, 1)

            codes = {}

            def load_code(j, k):
                if k == 0 and (not isinstance(j, int) or 2 <= j <= TILES - CODED + 2):
                    codes["turn"] = pe.value_load(jobs[0:1, 2, ds(j, 1)], min_val=0,
                                                  max_val=E ** CODED - 1)
                    codes["from"] = j

            def expert(j, at):
                if isinstance(j, int):
                    if "from" not in codes or not 0 <= j - codes["from"] + 2 < CODED:
                        return pe.value_load(jobs[0:1, 0, j:j + 1], min_val=0, max_val=E - 1)
                    at = j - codes["from"] + 2
                return (codes["turn"] >> (at * (E.bit_length() - 1))) & (E - 1)

            def product(pe, bank, e, xh, xl, wh, wl, chunks, n, bias_at, low_ready):
                nc.tensor.matmul(bank, sel[:, ds(e * P, P)], bias[:, bias_at:bias_at + n],
                                 start=True, stop=False)
                for c in range(chunks):
                    w = ds(e * EW + c * n, n)
                    nc.tensor.matmul(bank, xh[:, c, :], wl[:, w], start=False, stop=False)
                    nc.tensor.matmul(bank, xh[:, c, :], wh[:, w], start=False, stop=False)
                low_ready()
                for c in range(chunks):
                    mm = nc.tensor.matmul(bank, xl[:, c, :], wh[:, ds(e * EW + c * n, n)],
                                          start=False, stop=(c == chunks - 1))
                return mm

            def hidden(j, k):
                apart(pe, (s_hr, j - 1),
                      (s_xgh, j + 1))
                at, k = (k + 1) % 4 + 1, k % 2
                product(pe, psA[k][:, 0:F], expert(j, at), xgh[:, k], xgl[:, k], w1h, w1l, KC, F, 0,
                        lambda: apart(pe, (s_xgl, j + 1))) \
                    .then_inc(s_h, 1)

            def turn_hidden(j, k):
                pe.wait_ge(s_hr, j + 1)
                need(pe, s_hTl, j - 1)
                k = k % 2
                transposes(pe, hr[:, k, :], psB[k], FC).then_inc(s_hTp, 1)

            def outp(j, k):
                apart(pe, (s_ys, j - 1),
                      (s_hTh, j + 1))
                at, k = (k + 2) % 4, k % 2
                product(pe, psC[k][:, 0:D], expert(j, at), hTh[:, k], hTl[:, k], w2h, w2l, FC, D, F,
                        lambda: apart(pe, (s_hTl, j + 1))) \
                    .then_inc(s_y, 1)

            run_steps(pe, TILES, [(0, load_code), (0, turn_rows), (2, turn_hidden), (1, hidden),
                                  (2, outp)], 4, 4)

        def proj_step(w, c):
            r = w * C + c
            return (r + LATE) % NT if isinstance(w, int) else r - PAD

        def weighted(eng, on, u, c, lo, hi):
            eng.wait_ge(s_fw, u + 1)
            need(eng, s_ws, C * u + c - 1)
            n = (hi - lo) * H
            return on.tensor_tensor(
                wval[:, c, lo * D:hi * D].rearrange("p (a d) -> p a d", d=DH),
                fw[:, c, lo * H:hi * H].rearrange("p (a o) -> p a o", o=1).to_broadcast([P, n, DH]),
                V[:, ds((u * C + c + lo) * D, (hi - lo) * D)].rearrange("p (a d) -> p a d", d=DH),
                ALU.mult)

        w_h = lambda a: a.rearrange("p c (w h) -> p c w h", h=H)
        SMALL = 6 + 3

        def transposes(pe, src, dst, chunks):
            for c in range(chunks):
                mm = nc.tensor.transpose(dst[:, c * P:(c + 1) * P], src[:, c * P:(c + 1) * P], ident)
            return mm

        block = top.enter_context(nc.Block())

        @block.sync
        def _(sp):
            sp.dma_start(con[:, :], consts).then_inc(s_const, 16)
            for n in (3, 0, 1, 2):
                m = GROUP * D
                sp.dma_start(xs[:, n * m:(n + 1) * m], xv[:, n * m:(n + 1) * m]).then_inc(s_x[n], 16)
                if n == 3:
                    sp.dma_start(wqkv[:, :, :], wqkvT.rearrange("(c p) n -> p c n", p=P)) \
                      .then_inc(s_wq, 16)
            sp.dma_start(wo[:, :, :], woT.rearrange("(c p) n -> p c n", p=P)).then_inc(s_w, 16)
            sp.dma_start(gatew[:, :, :], gate.rearrange("(c p) n -> p c n", p=P)).then_inc(s_w, 16)
            sp.wait_ge(s_halo0, 4)
            sp.wait_ge(s_qkvs, 2)
            for T in (K, V):
                for b in range(B):
                    lo, hi = b * SEQP, (b + 1) * SEQP
                    sp.dma_start(T[lo + 1:hi, 0:PAD * D],
                                 T[lo:hi - 1, NT * D:(NT + PAD) * D]).then_inc(s_halo[0], 16)
            sp.wait_ge(s_qkvs, 3)
            for T in (K, V):
                for b in range(B):
                    lo, hi = b * SEQP, (b + 1) * SEQP
                    sp.dma_start(T[lo:hi - 1, (NT + PAD) * D:(NT + 2 * PAD) * D],
                                 T[lo + 1:hi, PAD * D:2 * PAD * D]).then_inc(s_halo[1], 16)
            sp.wait_ge(s_iota, 3)
            sp.wait_ge(s_zero, 1)
            for n in range(E - 1):
                sp.dma_start(rows_in[E * ROOM + n * P:E * ROOM + (n + 1) * P, :],
                             fill[:, :]).then_inc(s_spare, 16)
            stage4_sp(sp)

        @block.gpsimd
        def _(pool):
            number = dict(allow_small_or_imprecise_dtypes=True)
            nc.gpsimd.iota(past[:, :], [[P, TILES]], base=0, channel_multiplier=0,
                           **number).then_inc(s_iota, 1)
            nc.gpsimd.iota(Q[:, :, D], [[1, NT]], base=0, channel_multiplier=NT,
                           **number).then_inc(s_iota, 1)
            nc.gpsimd.iota(fill[:, D:D + 1], [[1, 1]], base=N, channel_multiplier=1,
                           **number).then_inc(s_iota, 1)
            pool.wait_ge(s_const, 16)
            for i, n in enumerate((3, 0, 1, 2)):
                r = slice(n * GROUP, (n + 1) * GROUP)
                pool.wait_ge(s_mom0, 7 * i + 7)
                nc.gpsimd.tensor_tensor(ln0[:, 1, r], ln1s[:, 4, r], halves.to_broadcast([P, GROUP]),
                                        ALU.pow).then_inc(s_rstd0, 1)
                pool.wait_ge(s_rstd0, i + 1)
                nc.gpsimd.tensor_tensor(ln0[:, 0, r], ln1s[:, 0, r], ln0[:, 1, r],
                                        ALU.mult).then_inc(s_nm0, 1)

            def rstd(m, u, used):
                var = lmv[m][:, :, 1]
                mean = lmv[m][:, :, 0]
                pair = lambda a: a.to_broadcast([P, C])
                pool.wait_ge(s_lmv[m], C * u + C)
                nc.gpsimd.tensor_tensor(lve[m][:, :], var, pair(epss), ALU.add).then_inc(s_lve[m], 1)
                need(pool, s_lnm[m], u)
                nc.gpsimd.tensor_tensor(lneg[m][:, :], mean, pair(minus),
                                        ALU.mult).then_inc(s_lneg[m], 1)
                pool.wait_ge(s_lve[m], u + 1)
                for sem_, n in used:
                    need(pool, sem_, n)
                nc.gpsimd.tensor_tensor(lrs[m][:, :], lve[m][:, :], pair(halves),
                                        ALU.pow).then_inc(s_lrs[m], 1)
                pool.wait_ge(s_lneg[m], u + 1)
                pool.wait_ge(s_lrs[m], u + 1)
                nc.gpsimd.tensor_tensor(lnm[m][:, :], lneg[m][:, :], lrs[m][:, :],
                                        ALU.mult).then_inc(s_lnm[m], 1)

            def rstd2(u, k):
                rstd(0, u, ((s_x1, C * u),))

            def rstd3(u, k):
                rstd(1, u, ((s_xn2, u),))

            def weigh_exp(u, k):
                pool.wait_ge(s_exp, u + 1)
                need(pool, s_zs, u)
                need(pool, s_fw, u)
                nc.gpsimd.tensor_tensor(ew[:, 1], ew[:, 0],
                                        conn[:, :].rearrange("p (o a) -> p o a", o=1)
                                        .to_broadcast([P, C, WH]), ALU.mult).then_inc(s_wt, 1)

            def values(u, k):
                if not (isinstance(u, int) and u < NU // 4):
                    pool.wait_ge(s_halo[1], 16 * 2 * B)
                for c in range(C):
                    weighted(pool, nc.gpsimd, u, c, 0, PW).then_inc(s_wvp, 1)

            def send(g, n, rows=xr):
                for i in range(G):
                    nc.gpsimd.indirect_dma_start(
                        rows_in, bass.IndirectOffsetOnAxis(ap=slots[:, g, n, i:i + 1], axis=0),
                        rows[:, i, :], None).then_inc(s_scat, 16)

            def scatter(u, k):
                if k % 2 == 1:
                    apart(pool, (s_slots, u + 1), (s_rows, u + 1))
                    send(k // 2, 0, xr_last if isinstance(u, int) and u == NU - 1 else xr)
                elif not (isinstance(u, int) and u == 0):
                    send((k // 2 + 1) % 2, 1)

            def low1(u, k):
                if k % 2 == 1 and not (isinstance(u, int) and u >= NU - 3):
                    low1_of(u)

            def low1_of(u):
                pool.wait_ge(s_whi[0], u + 1)
                at = ds((u - 1) * (EW // 2), EW)
                nc.gpsimd.tensor_tensor(w1l[:, at], w1r[:, at], w1h[:, at].bitcast(F32),
                                        ALU.subtract).then_inc(s_wlo[0], 2)

            pool.wait_ge(s_cn, 15)
            pool.wait_ge(s_halo[0], 16 * 2 * B)
            run_steps(pool, NU, [(12, low1), (6, weigh_exp), (8, rstd3), (6, values), (7, rstd2),
                                 (11, scatter)], 4)
            send((NU // 2 + 1) % 2, 1, xr_last)
            for u in (NU - 3, NU - 1):
                low1_of(u)
            stage5_pool(pool)

        @block.vector
        def _(v):
            nc.vector.memset(fill[:, 0:D], 0.0)
            nc.vector.memset(fill[:, D + 1:RW], 0.0).then_inc(s_zero, 1)
            nc.vector.memset(ones1[:, :], 1.0).then_inc(s_zero, 1)
            nc.vector.memset(ones3[:, :], 1.0).then_inc(s_zero, 1)
            nc.vector.memset(onesb[:, :], 1.0).then_inc(s_zero, 1)
            nc.vector.memset(gm[:, G:G + 1, :], 0.0).then_inc(s_zero, 1)
            for T in (K, V):
                nc.vector.memset(T[:, 0:PAD * D], 0.0).then_inc(s_halo0, 1)
                nc.vector.memset(T[:, (NT + PAD) * D:(NT + 2 * PAD) * D], 0.0).then_inc(s_halo0, 1)
            v.wait_ge(s_const, 16)
            nc.vector.tensor_copy(tri[:, :], con[:, P:2 * P]).then_inc(s_zero, 1)
            nc.vector.tensor_copy(base[:, :], ebase).then_inc(s_zero, 1)
            def ln1(i, n):
                r = slice(n * GROUP, (n + 1) * GROUP)
                v.wait_ge(s_x[n], 16)
                for t in range(n * GROUP, (n + 1) * GROUP):
                    nc.vector.bn_stats(st0[:, t:t + 1, :], xs[:, t * D:(t + 1) * D]) \
                      .then_inc(s_stat0, 1)
                v.wait_ge(s_stat0, GROUP * (i + 1))
                mean, dif, dsq, m2, var = (ln1s[:, a, r] for a in range(5))
                col = [st0[:, r, a] for a in range(6)]
                nc.vector.tensor_tensor(mean, col[1], col[4], ALU.add).then_inc(s_mom0, 1)
                nc.vector.tensor_tensor(dif, col[1], col[4], ALU.subtract).then_inc(s_mom0, 1)
                nc.vector.tensor_tensor(m2, col[2], col[5], ALU.add).then_inc(s_mom0, 1)
                v.wait_ge(s_mom0, 7 * i + 3)
                nc.vector.tensor_tensor(dsq, dif, dif, ALU.mult).then_inc(s_mom0, 1)
                nc.vector.tensor_scalar(m2, m2, 1.0 / D, LN_EPS, ALU.mult, ALU.add) \
                  .then_inc(s_mom0, 1)
                v.wait_ge(s_mom0, 7 * i + 5)
                nc.vector.scalar_tensor_tensor(var, dsq, 0.25, m2, ALU.mult, ALU.add) \
                  .then_inc(s_mom0, 1)
                nc.vector.tensor_scalar(mean, mean, -0.5, None, ALU.mult).then_inc(s_mom0, 1)

            for i, n in enumerate((3, 0, 1, 2)):
                ln1(i, n)

            def put(a):
                return nc.vector.tensor_copy(bo3[:, :, :], a.rearrange("p (o d) -> p o d", o=1)
                                             .to_broadcast([3, C, D]))

            v.wait_ge(s_small, 16 * SMALL)
            put(bo_raw).then_inc(s_bo, 1)
            v.wait_ge(s_bo, 1)
            nc.vector.scalar_tensor_tensor(bo_mid, bo3[:, 0, :], later(0), bo_raw, ALU.mult,
                                           ALU.add).then_inc(s_bo, 1)
            v.wait_ge(s_bo, 2)
            put(bo_mid).then_inc(s_bo, 1)
            v.wait_ge(s_bo, 3)
            nc.vector.scalar_tensor_tensor(bo_low, bo3[:, 0, :], later(1), bo_mid, ALU.mult,
                                           ALU.add).then_inc(s_bo, 1)
            v.wait_ge(s_bo, 4)
            put(bo_low).then_inc(s_bo, 1)

            nc.vector.tensor_scalar(cn[:, 4, :], cn[:, 0, :], posn[0:WH, :], None,
                                    ALU.mult).then_inc(s_cn, 1)
            v.wait_ge(s_cn, 1)
            nc.vector.tensor_tensor(cn[:, 4, :], cn[:, 4, :], cn[:, 1, :], ALU.add).then_inc(s_cn, 1)
            v.wait_ge(s_cna, 1)
            nc.vector.tensor_tensor(cnw2[:, :, :], cnw2[:, :, :],
                                    cn[:, 5:6, :].to_broadcast([WH, J, J]), ALU.mult).then_inc(s_cn, 1)
            v.wait_ge(s_cn, 3)
            nc.vector.tensor_reduce(cn[:, 4, :], cnw2[:, :, :], AX.X, ALU.add).then_inc(s_cn, 1)
            v.wait_ge(s_cn, 4)
            nc.vector.tensor_tensor(cn[:, 4, :], cn[:, 4, :], cn[:, 2, :], ALU.add).then_inc(s_cn, 1)
            v.wait_ge(s_cna, 2)
            nc.vector.tensor_tensor(cn[:, 4, :], cn[:, 5, :], cn[:, 3, :], ALU.mult).then_inc(s_cn, 1)
            v.wait_ge(s_cn, 6)
            nc.vector.tensor_reduce(cnc[:, 1:2], cn[:, 4, :], AX.X, ALU.add).then_inc(s_cn, 1)
            v.wait_ge(s_cn, 7)
            nc.vector.tensor_tensor(cnc[:, 2:3], cnc[:, 1:2], cnc[:, 0:1], ALU.add).then_inc(s_cn, 1)
            v.wait_ge(s_cnp, 1)
            row = crow[:, 0, :]
            byh = lambda a: a.rearrange("p (w h) -> p h w", h=H)
            nc.vector.tensor_copy(row, psX2[0:1, 0:WH]).then_inc(s_cn, 1)
            v.wait_ge(s_cn, 9)
            nc.vector.tensor_reduce(csum[:, 0, :], byh(row), AX.X, ALU.max).then_inc(s_cn, 1)
            v.wait_ge(s_cn, 10)
            nc.vector.tensor_tensor(crow[:, 1, :].rearrange("p (w h) -> p w h", h=H),
                                    row.rearrange("p (w h) -> p w h", h=H),
                                    csum[:, 0:1, :].to_broadcast([1, WIN, H]),
                                    ALU.subtract).then_inc(s_cn, 1)
            v.wait_ge(s_cna, 3)
            nc.vector.tensor_reduce(csum[:, 1, :], byh(crow[:, 2, :]), AX.X, ALU.add).then_inc(s_cn, 1)
            v.wait_ge(s_cn, 12)
            nc.vector.reciprocal(csum[:, 2, :], csum[:, 1, :]).then_inc(s_cn, 1)
            v.wait_ge(s_cn, 13)
            nc.vector.tensor_tensor(crow[:, 1, :].rearrange("p (w h) -> p w h", h=H),
                                    crow[:, 2, :].rearrange("p (w h) -> p w h", h=H),
                                    csum[:, 2:3, :].to_broadcast([1, WIN, H]),
                                    ALU.mult).then_inc(s_cn, 1)
            v.wait_ge(s_cnp, 2)
            nc.vector.tensor_copy(conn[:, :], psL[:, 0:WH]).then_inc(s_cn, 1)
            v.wait_ge(s_cn, 15)

            v.wait_ge(s_halo[0], 16 * 2 * B)
            flat_c = lambda a: a.rearrange("p c d -> p (c d)")

            def multiply(c):
                def stage(u, k):
                    if c == 0:
                        v.wait_ge(s_qkvs, u + 4)
                        if not (isinstance(u, int) and u < NU // 4):
                            v.wait_ge(s_halo[1], 16 * 2 * B)
                    need(v, s_raw, C * u + c - 1)
                    nc.vector.tensor_tensor(
                        prod[:, c, :].rearrange("p (w d) -> p w d", w=WIN),
                        Q[:, ds(u * C + c, 1), 0:D]
                        .to_broadcast([P, WIN, D]),
                        K[:, ds((u * C + c) * D, WIN * D)].rearrange("p (w d) -> p w d", w=WIN),
                        ALU.mult).then_inc(s_prod, 1)
                return stage

            def reduce_heads(u, k):
                for c in range(C):
                    v.wait_ge(s_prod, C * u + c + 1)
                    need(v, s_low, u)
                    nc.vector.tensor_reduce(raw[:, c, :], prod[:, c, :].rearrange(
                        "p (a d) -> p a d", d=DH), AX.X, ALU.add).then_inc(s_raw, 1)

            def largest_score(u, k):
                v.wait_ge(s_raw, C * u + C)
                nc.vector.tensor_reduce(top_s[:, :, :], raw[:, :, :].rearrange(
                    "p c (w h) -> p c h w", h=H), AX.X, ALU.max).then_inc(s_max, 1)

            def lower(u, k):
                v.wait_ge(s_max, u + 1)
                need(v, s_exp, u)
                nc.vector.tensor_tensor(
                    w_h(low_s[:, :, :]), w_h(raw[:, :, :]),
                    top_s[:, :, :].rearrange("p c (o h) -> p c o h", o=1)
                    .to_broadcast([P, C, WIN, H]), ALU.subtract).then_inc(s_low, 1)

            def sums(u, k):
                v.wait_ge(s_wt, u + 1)
                need(v, s_den, u)
                nc.vector.tensor_reduce(
                    zs[:, :, :, :].rearrange("p n c h -> p (n c) h"),
                    ew[:, :, :, :].rearrange("p n c (w h) -> p (n c) h w", h=H),
                    AX.X, ALU.add).then_inc(s_zs, 1)

            def denominator(u, k):
                v.wait_ge(s_zs, u + 1)
                need(v, s_rden, u)
                nc.vector.scalar_tensor_tensor(flat_c(den[:, :, :]), flat_c(zs[:, 0]), 1e-9,
                                               flat_c(zs[:, 1]), ALU.mult,
                                               ALU.add).then_inc(s_den, 1)

            def invert(u, k):
                v.wait_ge(s_den, u + 1)
                need(v, s_fw, u)
                nc.vector.reciprocal(flat_c(rden[:, :, :]), flat_c(den[:, :, :])).then_inc(s_rden, 1)

            def attention_weights(u, k):
                v.wait_ge(s_rden, u + 1)
                need(v, s_wvd, C * u)
                need(v, s_wvp, C * u)
                nc.vector.tensor_tensor(
                    w_h(fw[:, :, :]), w_h(ew[:, 1]),
                    rden[:, :, :].rearrange("p c (o h) -> p c o h", o=1).to_broadcast([P, C, WIN, H]),
                    ALU.mult).then_inc(s_fw, 1)

            def values(u, k):
                for c in range(C):
                    weighted(v, nc.vector, u, c, PW, WIN).then_inc(s_wvd, 1)

            def row_stats(m, u, src, *waits):
                apart(v, (s_lmv[m], C * u), *waits)
                for c in range(C):
                    nc.vector.bn_stats(lst[m][:, c, :], src(c)).then_inc(s_lst[m], 1)

            def row_moments(m, u):
                apart(v, (s_lnm[m], u),
                      (s_lst[m], C * u + C))
                for c in range(C):
                    nc.vector.bn_aggr(lmv[m][:, c, :], lst[m][:, c, :]).then_inc(s_lmv[m], 1)

            def stats2(u, k):
                row_stats(0, u, lambda c: psY[:, c * D:(c + 1) * D], (s_wo, u + 1))

            def moments2(u, k):
                row_moments(0, u)

            def residual(u, k):
                v.wait_ge(s_xm, u + 1)
                v.wait_ge(s_lrs[0], u + 1)
                for c in range(C):
                    nc.vector.scalar_tensor_tensor(
                        xs[:, ds((u * C + c) * D, D)], psY[:, c * D:(c + 1) * D], lrs[0][:, c:c + 1],
                        xm[:, c, :], ALU.mult, ALU.add).then_inc(s_x1, 1)

            def stats3(u, k):
                row_stats(1, u, lambda c: xs[:, ds((u * C + c) * D, D)], (s_x1, C * u + C))

            def moments3(u, k):
                row_moments(1, u)

            V_ = nc.vector
            each = lambda a: a.rearrange("p (t o) -> p t o", o=1).to_broadcast([P, G, E])
            per_t = lambda a: a.rearrange("p (o e) -> p o e", o=1).to_broadcast([P, G, E])
            col = lambda n: gsc[:, n, :]
            q_, l_, u_ = (a[:, :, :] for a in (gq, gl, gu))
            PICKS, PLACES = 11, 5

            def group_step(u, n):
                return (u - 1) * ((PICKS + PLACES) // 2) + n

            def pick(n):
                def stage(u, k):
                    if k % 2 != 1:
                        return
                    steps = ds(u * C - C, G)
                    largest, second = gmax[:, 0, steps], gmax[:, 1, steps]
                    if n == 0:
                        v.wait_ge(s_lgs, u + 1)
                    else:
                        apart(v, (s_g, group_step(u, n)))
                    if n == 0:
                        ins = V_.tensor_reduce(largest, lgt[:, steps, :], AX.X, ALU.max)
                    elif n == 1:
                        ins = V_.tensor_tensor(l_, lgt[:, steps, :], each(largest), ALU.subtract)
                    elif n == 2:
                        ins = V_.scalar_tensor_tensor(q_, l_, 0.0, per_t(prior), ALU.is_ge, ALU.mult)
                    elif n == 3:
                        ins = V_.tensor_reduce(col(0), q_, AX.X, ALU.max)
                    elif n == 4:
                        V_.tensor_copy(Q[:, steps, D + 1], col(0)).then_inc(s_first, 2)
                        ins = V_.tensor_tensor(oh[:, 0], q_, each(col(0)), ALU.is_equal)
                    elif n == 5:
                        ins = V_.scalar_tensor_tensor(u_, oh[:, 0], -3e38, l_, ALU.mult, ALU.add)
                    elif n == 6:
                        ins = V_.tensor_reduce(second, u_, AX.X, ALU.max)
                    elif n == 7:
                        ins = V_.tensor_tensor(q_, u_, each(second), ALU.is_ge)
                    elif n == 8:
                        ins = V_.tensor_tensor(q_, q_, per_t(prior), ALU.mult)
                    elif n == 9:
                        v.wait_ge(s_first, u + 1)
                        ins = V_.tensor_reduce(col(1), q_, AX.X, ALU.max)
                    elif n == 10:
                        ins = V_.tensor_tensor(oh[:, 1], q_, each(col(1)), ALU.is_equal)
                    else:
                        need(v, s_gcnt, u - 1)
                        V_.tensor_tensor(gm[:, 0:G, :], oh[:, 0], oh[:, 1],
                                         ALU.add).then_inc(s_gmask, 2)
                        return
                    ins.then_inc(s_g, 1)
                return stage

            def place(n):
                def stage(u, k):
                    if k % 2 != 1:
                        return
                    if n == 0:
                        v.wait_ge(s_gcnt, u + 1)
                        V_.tensor_tensor(gpos[:, :, :], psG[:, 0:G, :], per_t(base[:, :]),
                                         ALU.add).then_inc(s_g, 1)
                    elif n == 1:
                        v.wait_ge(s_g, group_step(u, PICKS + 1))
                        V_.tensor_tensor(base[:, :], base[:, :], psG[:, G, :],
                                         ALU.add).then_inc(s_g, 1)
                        for m in range(TOPK):
                            V_.tensor_tensor(ohp[:, m], oh[:, m], gpos[:, :, :],
                                             ALU.mult).then_inc(s_g, 1)
                    elif n == 2:
                        v.wait_ge(s_g, group_step(u, PICKS + 4))
                        V_.tensor_reduce(slotf[:, :, :], ohp[:, :, :, :], AX.X,
                                         ALU.add).then_inc(s_g, 1)
                    else:
                        v.wait_ge(s_g, group_step(u, PICKS + 5))
                        need(v, s_scat, 16 * G * (u - 3))
                        V_.tensor_copy(slots[:, k // 2], slotf[:, :, :]).then_inc(s_slots, 2)
                return stage

            def low2_of(lo, hi):
                for e in range(lo, hi):
                    v.wait_ge(s_whi[1], e + 1)
                    at = slice(e * EW, (e + 1) * EW)
                    nc.vector.tensor_tensor(w2l[:, at], w2r[:, at], w2h[:, at].bitcast(F32),
                                            ALU.subtract).then_inc(s_wlo[1], 1)

            early_low2 = E // 2 - 1

            def low2(u, k):
                if isinstance(u, int) and u == NU - 1:
                    low2_of(0, early_low2)

            def split_bias(u, k):
                if not (isinstance(u, int) and u == NU - 1):
                    return
                GE = 3 * E
                raw_b = braw[:, :]
                less = lambda n: con[0:GE, 3 * P + 3 + n:3 * P + 4 + n]
                v.wait_ge(s_iota, 1)
                nc.vector.memset(ones_e, 1.0)
                nc.vector.memset(bias[:, :], 0.0).then_inc(s_bias, 1)
                nc.vector.tensor_copy(sel[:, :], con[:, 3 * P + 8:3 * P + 8 + E].rearrange(
                    "p (e o) -> p e o", o=1).to_broadcast([P, E, P])).then_inc(s_bias, 1)
                v.wait_ge(s_braw, 16 * 6)
                for n in range(3):
                    v.wait_ge(s_bias, 2 * n + 2)
                    nc.vector.tensor_copy(bias[0:GE, :], raw_b).then_inc(s_bias, 1)
                    if n < 2:
                        v.wait_ge(s_bias, 2 * n + 3)
                        nc.vector.scalar_tensor_tensor(raw_b, bias[0:GE, :], less(n), raw_b,
                                                       ALU.mult, ALU.add).then_inc(s_bias, 1)

            run_steps(v, NU, [
                (8, stats2), (6, multiply(0)), (8, moments2), (6, multiply(1)), (6, reduce_heads),
                (10, pick(0)), (11, place(0)), (6, largest_score),
                (10, pick(1)), (11, place(1)), (6, lower),
                (10, pick(2)), (11, place(2)), (8, residual),
                (10, pick(3)), (11, place(3)), (8, stats3), (10, pick(4)), (8, moments3),
                (10, pick(5)), (6, sums), (10, pick(6)), (6, denominator), (10, pick(7)),
                (6, invert), (10, pick(8)), (6, attention_weights), (10, pick(9)), (6, values),
                (10, pick(10)), (10, pick(11)), (9, split_bias), (9, low2)], 4)

            step = [0]
            gz, gr, gsum = (gw[:, n, :] for n in range(3))
            gtwo = gw[:, 3:5, :]

            def jop(ins, last=True):
                step[0] += 1
                ins.then_inc(s_job, 1)
                if last:
                    v.wait_ge(s_job, step[0])

            def weights_of():
                jop(V_.reciprocal(gr, gz))
                over_n = lambda a: a.rearrange("p (o t) -> p o t", o=1).to_broadcast([P, TOPK, NT])
                jop(V_.tensor_tensor(gtwo, gtwo, over_n(gr), ALU.mult))
                jop(V_.tensor_tensor(gsum, gw[:, 3, :], gw[:, 4, :], ALU.add))
                jop(V_.tensor_scalar(gsum, gsum, 1e-12, None, ALU.max))
                jop(V_.reciprocal(gr, gsum))
                jop(V_.tensor_tensor(gates[:, :, :], gtwo, over_n(gr), ALU.mult))

            n_, tl, tf, c_ = (cnt[:, n, :] for n in range(4))
            jop(V_.tensor_copy(tails[:, :], base[0:1, :]), last=False)
            jop(V_.scalar_tensor_tensor(n_, base[:, :], float(P - 1), ebase, ALU.add, ALU.subtract))
            jop(V_.tensor_copy(cnti[:, :], n_))
            jop(V_.tensor_single_scalar(cnti[:, :], cnti[:, :], P.bit_length() - 1,
                                        ALU.logical_shift_right))
            jop(V_.tensor_copy(tl, cnti[:, :]))
            jop(V_.tensor_tensor_scan(c_, ones_e, tl, 0.0, ALU.mult, ALU.add))
            jop(V_.tensor_scalar(c_, c_, float(P), None, ALU.mult))
            jop(V_.tensor_scalar(tf, tl, float(-P), float(ROOM), ALU.mult, ALU.add), last=False)
            over_j = lambda a: a.rearrange("p (o e) -> p o e", o=1).to_broadcast([P, TILES, E])
            jop(V_.tensor_tensor(jcmp[:, :, :], over_j(c_),
                                 past[:, :].rearrange("p (j o) -> p j o", o=1)
                                 .to_broadcast([P, TILES, E]), ALU.is_le))
            jop(V_.tensor_reduce(jf[:, 0, :], jcmp[:, :, :], AX.X, ALU.add))
            jop(V_.tensor_tensor(jcmp[:, :, :], jcmp[:, :, :], over_j(tf), ALU.mult))
            jop(V_.tensor_reduce(jf[:, 1, :], jcmp[:, :, :], AX.X, ALU.add))
            jop(V_.tensor_tensor(jf[:, 2, :], past[:, :], jf[:, 1, :], ALU.add))
            V_.tensor_copy(jobs[:, 1, :], jf[0:1, 2, :]).then_inc(s_jobs, 1)
            jop(V_.tensor_scalar(jf[:, 0, :], jf[:, 0, :], float(E - 1), None, ALU.min))
            ej = lambda i: jf[0:1, 0, i:i + TILES - CODED + 1]
            code = jf[0:1, 1, 2:TILES - CODED + 3]
            jop(V_.scalar_tensor_tensor(code, ej(CODED - 1), float(E), ej(CODED - 2), ALU.mult,
                                        ALU.add))
            for i in reversed(range(CODED - 2)):
                jop(V_.scalar_tensor_tensor(code, code, float(E), ej(i), ALU.mult, ALU.add))
            jop(V_.tensor_copy(jobs[:, 2, 2:TILES - CODED + 3], code), last=False)
            V_.tensor_copy(jobs[:, 0, :], jf[0:1, 0, :]).then_inc(s_jobs, 1)
            jop(V_.tensor_scalar(mark[:, :], jf[:, 0, :], -1.0, float(E), ALU.mult, ALU.add))
            le = lgt[:, :, :]
            V_.tensor_tensor(le, le, gmax[:, 0, :].rearrange("p (t o) -> p t o", o=1)
                             .to_broadcast([P, NT, E]), ALU.subtract).then_inc(s_glow, 1)
            v.wait_ge(s_gexp, 2)
            jop(V_.tensor_reduce(gz, le, AX.X, ALU.add))
            low2_of(early_low2, E)
            stage4_dve(v, weights_of)

        @block.scalar
        def _(act):
            for dst, src in ((cn[:, 0, :], cw1.rearrange("h j a -> h (j a)")), (cn[:, 1, :], cb1),
                             (cnw2, cw2.rearrange("h j i -> h (j i)")), (cn[:, 2, :], cb2),
                             (cn[:, 3, :], cw3.rearrange("h a j -> h (a j)")), (cnc[:, 0:1], cb3)):
                if dst is cnw2:
                    dst = dst.rearrange("p j i -> p (j i)")
                n = src.shape[1]
                nc.scalar.dma_start(dst, src.rearrange("(o h) n -> o h n", o=1)
                                    .to_broadcast([WIN, H, n])).then_inc(s_small, 16)
            for n in range(3):
                nc.scalar.dma_start(bo_raw[n:n + 1, :], bo.rearrange("(a d) -> a d", a=1)) \
                  .then_inc(s_small, 16)
            def norm1(w, k):
                if isinstance(w, int):
                    t = w * C + C - 1 - PAD
                    act.wait_ge(s_nm0, 1 if t < 0 else min(t // GROUP + 2, 4))
                apart(act, (s_xTp, w))
                for c in range(C):
                    t = proj_step(w, c)
                    nc.scalar.activation(xn[:, c, :], xs[:, ds(t * D, D)], ACT.Identity,
                                         bias=ln0[:, 0, ds(t, 1)],
                                         scale=ln0[:, 1, ds(t, 1)]).then_inc(s_xn, 1)

            def evac_xT(w, k):
                act.wait_ge(s_xTp, w + 1)
                need(act, s_qkv, w)
                nc.scalar.copy(xnT[:, :, :, :].rearrange("p c k m -> p (c k m)"),
                               psX[:, :]).then_inc(s_xT, 1)

            def evac_qkv(w, k):
                act.wait_ge(s_qkv, w + 1)
                t = proj_step(w, 0)
                jumps = isinstance(w, int) and proj_step(w, C - 1) < t
                spans = [(0, 1), (1, C)] if jumps else [(0, C)]
                for a, b in spans:
                    t = proj_step(w, a)
                    nc.scalar.copy(Q[:, ds(t, b - a), 0:D],
                                   psQ[:, a * D:b * D].rearrange("p (c d) -> p c d", d=D))
                    for T, bank in ((K, psK), (V, psV)):
                        mv = nc.scalar.copy(T[:, ds((t + PAD) * D, (b - a) * D)], bank[:, a * D:b * D])
                mv.then_inc(s_qkvs, 4 if isinstance(w, int) and w == NU - 1 else 1)

            def expo(u, k):
                act.wait_ge(s_low, u + 1)
                need(act, s_zs, u)
                need(act, s_wt, u)
                nc.scalar.activation(ew[:, 0], low_s[:, :, :], ACT.Exp, scale=scale) \
                  .then_inc(s_exp, 1)

            def evac_attT(u, k):
                act.wait_ge(s_ws, C * u + C)
                need(act, s_wo, u)
                nc.scalar.copy(attT[:, :, :, :].rearrange("p k c m -> p (k c m)"),
                               psW[:, :]).then_inc(s_aT, 1)

            def shift_x(u, k):
                act.wait_ge(s_lnm[0], u + 1)
                need(act, s_x1, C * u)
                for c in range(C):
                    mv = nc.scalar.activation(xm[:, c, :], xs[:, ds((u * C + c) * D, D)],
                                              ACT.Identity, bias=lnm[0][:, c:c + 1])
                mv.then_inc(s_xm, 1)

            def norm3(u, k):
                apart(act, (s_x2p, u),
                      (s_keep, u), (s_lnm[1], u + 1))
                for c in range(C):
                    mv = nc.scalar.activation(xn2[:, c, :], xs[:, ds((u * C + c) * D, D)],
                                              ACT.Identity, bias=lnm[1][:, c:c + 1],
                                              scale=lrs[1][:, c:c + 1])
                mv.then_inc(s_xn2, 1)

            def keep(u, k):
                act.wait_ge(s_xn2, u + 1)
                nc.scalar.copy(Q[:, ds(u * C, C), 0:D], xn2[:, :, :]).then_inc(s_keep, 1)

            def stage_rows(u, k):
                if k == 1:
                    act.wait_ge(s_first, u + 1)
                    act.wait_ge(s_keep, u + 1)
                    if isinstance(u, int) and u == NU - 1:
                        staged = xr_last
                        act.wait_ge(s_wt, NU)
                    else:
                        staged = xr
                        need(act, s_scat, 16 * G * (u - 1))
                    nc.scalar.copy(staged[:, :, :], Q[:, ds(u * C - C, G), :]).then_inc(s_rows, 2)
                    act.wait_ge(s_rows, u + 1)
                    act.wait_ge(s_wraw[0], (u + 1) * 8)
                    at = ds((u - 1) * (EW // 2), EW)
                    nc.scalar.copy(w1h[:, at], w1r[:, at]).then_inc(s_whi[0], 2)

            def evac_x2T(u, k):
                act.wait_ge(s_x2p, u + 1)
                need(act, s_lg, u)
                nc.scalar.copy(x2T[:, :, :, :].rearrange("p c k m -> p (c k m)"),
                               psX[:, :]).then_inc(s_x2T, 1)

            def evac_logits(u, k):
                act.wait_ge(s_lg, u + 1)
                nc.scalar.copy(lgt[:, ds(u * C, C), :].rearrange("p c e -> p (c e)"),
                               psL[:, 0:C * E]).then_inc(s_lgs, 1)

            def connect(w, k):
                if isinstance(w, int) and w == 2:
                    for n in range(2):
                        act.wait_ge(s_cn, 3 * n + 2)
                        nc.scalar.activation(cn[:, 5, :], cn[:, 4, :], ACT.Gelu).then_inc(s_cna, 1)
                elif isinstance(w, int) and w == 3:
                    act.wait_ge(s_cn, 11)
                    nc.scalar.activation(crow[:, 2, :], crow[:, 1, :], ACT.Exp).then_inc(s_cna, 1)

            def high2(lo, hi):
                def stage(u, k):
                    if isinstance(u, int) and u == NU - 1:
                        if lo:
                            act.wait_ge(s_wlast, 16)
                            act.wait_ge(s_ws, NT)
                        else:
                            act.wait_ge(s_wraw[1], 16 * (E - 1))
                            act.wait_ge(s_low, NU)
                        for e in range(lo, hi):
                            at = slice(e * EW, (e + 1) * EW)
                            nc.scalar.copy(w2h[:, at], w2r[:, at]).then_inc(s_whi[1], 1)
                return stage

            IN_PROD = C * WIN * D // EW
            run_steps(act, NU, [
                (2, evac_qkv), (9, norm3), (1, evac_xT), (8, shift_x), (6, expo), (7, evac_attT),
                (9, evac_x2T), (9, evac_logits), (9, keep), (11, stage_rows), (0, norm1),
                (8, high2(0, IN_PROD)), (9, high2(IN_PROD, E)), (0, connect)])
            act.wait_ge(s_job, 1)
            end_lists(act, s_tail[1], E // 2, E)
            act.wait_ge(s_glow, 1)
            nc.scalar.activation(lgt[:, :, :], lgt[:, :, :], ACT.Exp).then_inc(s_gexp, 1)
            nc.scalar.activation(gw[:, 3, :], gmax[:, 0, :], ACT.Exp, scale=0.0)
            nc.scalar.activation(gw[:, 4, :], gmax[:, 1, :], ACT.Exp).then_inc(s_gexp, 1)
            stage4_act(act)

        @block.tensor
        def _(pe):
            pe.wait_ge(s_const, 16)
            pe.wait_ge(s_zero, 7)

            def turn_x(w, k):
                pe.wait_ge(s_xn, C * w + C)
                need(pe, s_xT, w)
                need(pe, s_x2T, w - APART)
                for c in range(C):
                    mm = transposes(pe, xn[:, c, :], psX[:, c * D:(c + 1) * D], KC)
                mm.then_inc(s_xTp, 1)

            def qkv(w, k):
                pe.wait_ge(s_xT, w + 1)
                need(pe, s_qkvs, w)
                for n, bank in enumerate((psQ, psK, psV)):
                    for c in range(C):
                        for i in range(KC):
                            mm = nc.tensor.matmul(bank[:, c * D:(c + 1) * D], xnT[:, c, i, :],
                                                  wqkv[:, i, n * D:(n + 1) * D],
                                                  start=(i == 0), stop=(i == KC - 1))
                mm.then_inc(s_qkv, 1)

            def window_sum(u, k):
                need(pe, s_aT, u)
                for c in range(C):
                    pe.wait_ge(s_wvp, C * u + c + 1)
                    pe.wait_ge(s_wvd, C * u + c + 1)
                    for i in range(KC):
                        for w in range(WIN):
                            mm = nc.tensor.matmul(
                                psW[:, (i * C + c) * P:(i * C + c + 1) * P],
                                wval[:, c, w * D + i * P:w * D + (i + 1) * P], ident,
                                start=(w == 0), stop=(w == WIN - 1))
                    mm.then_inc(s_ws, 1)

            def out_product(u, k):
                pe.wait_ge(s_aT, u + 1)
                need(pe, s_x1, C * u)
                nc.tensor.matmul(psY[:, :], ones3[:, :], bo3[:, :, :].rearrange("p c d -> p (c d)"),
                                 start=True, stop=False)
                for c in range(C):
                    for i in range(KC):
                        mm = nc.tensor.matmul(psY[:, c * D:(c + 1) * D], attT[:, i, c, :], wo[:, i, :],
                                              start=False, stop=(c == C - 1 and i == KC - 1))
                mm.then_inc(s_wo, 1)

            def turn_x2(u, k):
                pe.wait_ge(s_xn2, u + 1)
                need(pe, s_x2T, u)
                pe.wait_ge(s_xT, min(u + APART + 1, NU) if isinstance(u, int) else u + APART + 1)
                for c in range(C):
                    mm = transposes(pe, xn2[:, c, :], psX[:, c * D:(c + 1) * D], KC)
                mm.then_inc(s_x2p, 1)

            def logits(u, k):
                pe.wait_ge(s_x2T, u + 1)
                need(pe, s_lgs, u)
                for c in range(C):
                    for i in range(KC):
                        mm = nc.tensor.matmul(psL[:, c * E:(c + 1) * E], x2T[:, c, i, :],
                                              gatew[:, i, :], start=(i == 0), stop=(i == KC - 1))
                mm.then_inc(s_lg, 1)

            def count_pairs(u, k):
                if k == 1:
                    pe.wait_ge(s_gmask, u + 1)
                    need(pe, s_slots, u - 1)
                    nc.tensor.matmul(psG[:, :, :], tri[:, :], gm[:, :, :], start=True, stop=False)
                    for t in range(G):
                        mm = nc.tensor.matmul(psG[:, t + 1:G + 1, :], onesb[:, :],
                                              gm[:, t:t + 1, :].to_broadcast([P, G - t, E]),
                                              start=False, stop=(t == G - 1))
                    mm.then_inc(s_gcnt, 2)

            def connect(w, k):
                if isinstance(w, int) and w == 2:
                    pe.wait_ge(s_cn, 8)
                    nc.tensor.matmul(psX2[0:1, 0:WH], cnc[:, 2:3], ident[0:WH, 0:WH], start=True,
                                     stop=True).then_inc(s_cnp, 1)
                elif isinstance(w, int) and w == 3:
                    pe.wait_ge(s_cn, 14)
                    nc.tensor.matmul(psL[:, 0:WH], ones1[:, :], crow[:, 1, :], start=True,
                                     stop=True).then_inc(s_cnp, 1)
                    pe.wait_ge(s_w, 32)
                    pe.wait_ge(s_bo, 5)

            pe.wait_ge(s_wq, 16)
            APART = 8
            run_steps(pe, NU, [(1, turn_x), (7, window_sum), (9, turn_x2), (7, out_product),
                               (9, logits), (1, qkv), (1, connect), (10, count_pairs)])

            stage4_pe(pe)


def kernel(L0_attn_x, L0_attn_wq, L0_attn_wk, L0_attn_wv, L0_attn_wo, L0_attn_bo, L0_attn_cw1, L0_attn_cb1,
           L0_attn_cw2, L0_attn_cb2, L0_attn_cw3, L0_attn_cb3, L0_ffn_gate, L0_ffn_W1, L0_ffn_b1,
           L0_ffn_W2, L0_ffn_b2):
    import numpy as np
    import concourse.bacc as bacc
    from concourse.bass_utils import run_bass_kernel_spmd

    wqkvT = np.concatenate([np.asarray(w).T for w in (L0_attn_wq, L0_attn_wk, L0_attn_wv)], axis=1)
    H, E, N = L0_attn_cw1.shape[0], L0_ffn_W1.shape[0], L0_attn_x.shape[0] * L0_attn_x.shape[1]
    p = np.arange(P)
    consts = np.zeros((P, 3 * P + 8 + E), np.float32)
    consts[:, 0:P] = np.eye(P)
    consts[:, P:2 * P] = p[:, None] < p[None, :]
    consts[:, 2 * P:2 * P + E] = E - np.arange(E)
    consts[:, 2 * P + E:2 * P + 2 * E] = np.arange(E) * (N + P)
    consts[:, 3 * P] = -0.5
    consts[:, 3 * P + 1] = -1.0
    consts[:, 3 * P + 5] = -1.0 * (p >= 1)
    consts[:, 3 * P + 6] = -1.0 * (p >= 2)
    consts[:, 3 * P + 7] = 1e-5
    consts[:, 3 * P + 2] = np.linspace(0.0, 1.0, 7, dtype=np.float32)[np.minimum(p // H, 6)]
    consts[:, 3 * P + 3] = -1.0 * (p >= E)
    consts[:, 3 * P + 4] = -1.0 * (p >= 2 * E)
    consts[:, 3 * P + 8:] = (p[:, None] % E == np.arange(E)) & (p[:, None] < 3 * E)
    arrays = {
        "x": L0_attn_x, "wqkvT": wqkvT, "woT": np.asarray(L0_attn_wo).T, "bo": L0_attn_bo,
        "cw1": L0_attn_cw1, "cb1": L0_attn_cb1, "cw2": L0_attn_cw2, "cb2": L0_attn_cb2,
        "cw3": L0_attn_cw3, "cb3": L0_attn_cb3, "gate": L0_ffn_gate, "w1": L0_ffn_W1,
        "b1": L0_ffn_b1, "w2": L0_ffn_W2, "b2": L0_ffn_b2, "consts": consts,
    }
    arrays = {f"in_{n}": np.ascontiguousarray(a) for n, a in arrays.items()}
    nc = bacc.Bacc("TRN2", target_bir_lowering=False, num_devices=1)
    args = [nc.dram_tensor(n, a.shape, mybir.dt.from_np(a.dtype), kind="ExternalInput").ap()
            for n, a in arrays.items()]
    out = nc.dram_tensor("out_x", L0_attn_x.shape, F32, kind="ExternalOutput").ap()
    build(nc, *args, out)
    r = run_bass_kernel_spmd(nc, [arrays], core_ids=[0])
    return r.results[0]["out_x"]
```
